# Optimizing a Trainium2 kernel written in Bass

```python
import numpy as np
import jax
import jax.numpy as jnp

def _softmax(x, axis=-1):
    return jax.nn.softmax(x, axis=axis)

def _gelu(x):
    return jax.nn.gelu(x, approximate=True)

def _silu(x):
    return jax.nn.silu(x)

def _sigmoid(x):
    return jax.nn.sigmoid(x)

def _layernorm(x, axis=-1, eps=1e-05):
    m = jnp.mean(x, axis=axis, keepdims=True)
    v = jnp.var(x, axis=axis, keepdims=True)
    return (x - m) / jnp.sqrt(v + eps)

def _scatter_add(tgt, idx, src, axis=0):
    return tgt.at[idx].add(src)

def _segment_sum(src, seg, n):
    return jax.ops.segment_sum(src, seg, n)
kernel_name = 'mk_metaformer_d1_conv_nchw512_r2_cfd832'

def setup_inputs(seed: int=0):
    np.random.seed(seed)
    _w = jnp.asarray

    def _rec_inputs():
        import jax
        import jax.numpy as jnp
        _gk = jax.random.key(seed)
        x = -0.0001905 + 1 * jax.random.normal(jax.random.fold_in(_gk, 1), (128, 256, 9, 9), jnp.float32)
        return x
    x = _rec_inputs()

    def _L0_conv_setup():
        import jax, jax.numpy as jnp
        import numpy as np
        BS, C, H, W = (128, 256, 9, 9)
        D = 9
        SPA_HEAD = 32
        HW = H * W
        EPS = 1e-05

        def _bn(x, p, axis=1):
            g, b, m, v = p
            sh = [1] * x.ndim
            sh[axis] = -1
            return (x - m.reshape(sh)) * (g.reshape(sh) * jax.lax.rsqrt(v.reshape(sh) + EPS)) + b.reshape(sh)

        def _conv2d(x, w, groups=1):
            return jax.lax.conv_general_dilated(x, w, (1, 1), 'SAME', dimension_numbers=('NCHW', 'OIHW', 'NCHW'), feature_group_count=groups)
        key = jax.random.key(seed)
        ks = list(jax.random.split(key, 16))

        def rn(k, shape, s=0.05):
            return (jax.random.normal(k, shape) * s).astype(jnp.float32)

        def bnp(k, c):
            k1, k2, k3, k4 = jax.random.split(k, 4)
            g = jax.random.uniform(k1, (c,), minval=0.5, maxval=1.5)
            v = jax.random.uniform(k4, (c,), minval=0.5, maxval=1.5)
            return jnp.stack([g, rn(k2, (c,)), rn(k3, (c,)), v]).astype(jnp.float32)
        return {'x': jax.random.normal(ks[0], (BS, C, H, W), jnp.float32), 'alpha': jnp.full((1,), 0.5, jnp.float32), 'sa_key_w': rn(ks[1], (C, 1, 3, 3)), 'sa_key_bn': bnp(ks[2], C), 'sa_att_w1': rn(ks[3], (C, 2 * C // SPA_HEAD, 1, 1)), 'sa_att_bn': bnp(ks[4], C), 'sa_att_w2': rn(ks[5], (SPA_HEAD, C // SPA_HEAD, 1, 1)), 'sa_att_b2': rn(ks[6], (SPA_HEAD,)), 'se_key_w': rn(ks[7], (HW, 1, D)), 'se_key_b': rn(ks[8], (HW,)), 'se_att_w1': rn(ks[9], (HW, 2 * HW)), 'se_att_bn': bnp(ks[10], HW), 'se_att_w2': rn(ks[11], (D, HW)), 'se_att_b2': rn(ks[12], (D,)), 'se_val_w': rn(ks[13], (C, 1, 3, 3)), 'se_val_b': rn(ks[14], (C,))}
    _L0_conv_all = _L0_conv_setup()
    _L0_conv_in = {k: v for k, v in _L0_conv_all.items() if k in ('alpha', 'sa_key_w', 'sa_key_bn', 'sa_att_w1', 'sa_att_bn', 'sa_att_w2', 'sa_att_b2', 'se_key_w', 'se_key_b', 'se_att_w1', 'se_att_bn', 'se_att_w2', 'se_att_b2', 'se_val_w', 'se_val_b')}
    del _L0_conv_all

    def _L0_ffn_setup():
        import jax, jax.numpy as jnp
        import numpy as np
        B, S, D, H, E = (4, 1024, 256, 512, 8)
        key = jax.random.key(seed)
        ks = jax.random.split(key, 4)
        x = jax.random.normal(ks[0], (B, S, D), jnp.float32)
        Wr = jax.random.normal(ks[1], (E, D), jnp.float32) * 0.02
        br = jnp.zeros((E,), jnp.float32)
        W1 = jax.random.normal(ks[2], (E, D, H), jnp.float32) * 0.02
        b1 = jnp.zeros((E, H), jnp.float32)
        W2 = jax.random.normal(ks[3], (E, H, D), jnp.float32) * 0.02
        b2 = jnp.zeros((E, D), jnp.float32)
        return {'x': x, 'Wr': Wr, 'br': br, 'W1': W1, 'b1': b1, 'W2': W2, 'b2': b2}
    _L0_ffn_all = _L0_ffn_setup()
    _L0_ffn_in = {k: v for k, v in _L0_ffn_all.items() if k in ('Wr', 'br', 'W1', 'b1', 'W2', 'b2')}
    del _L0_ffn_all
    return {'x': x, 'L0_conv_alpha': _L0_conv_in['alpha'], 'L0_conv_sa_key_w': _L0_conv_in['sa_key_w'], 'L0_conv_sa_key_bn': _L0_conv_in['sa_key_bn'], 'L0_conv_sa_att_w1': _L0_conv_in['sa_att_w1'], 'L0_conv_sa_att_bn': _L0_conv_in['sa_att_bn'], 'L0_conv_sa_att_w2': _L0_conv_in['sa_att_w2'], 'L0_conv_sa_att_b2': _L0_conv_in['sa_att_b2'], 'L0_conv_se_key_w': _L0_conv_in['se_key_w'], 'L0_conv_se_key_b': _L0_conv_in['se_key_b'], 'L0_conv_se_att_w1': _L0_conv_in['se_att_w1'], 'L0_conv_se_att_bn': _L0_conv_in['se_att_bn'], 'L0_conv_se_att_w2': _L0_conv_in['se_att_w2'], 'L0_conv_se_att_b2': _L0_conv_in['se_att_b2'], 'L0_conv_se_val_w': _L0_conv_in['se_val_w'], 'L0_conv_se_val_b': _L0_conv_in['se_val_b'], 'L0_ffn_Wr': _L0_ffn_in['Wr'], 'L0_ffn_br': _L0_ffn_in['br'], 'L0_ffn_W1': _L0_ffn_in['W1'], 'L0_ffn_b1': _L0_ffn_in['b1'], 'L0_ffn_W2': _L0_ffn_in['W2'], 'L0_ffn_b2': _L0_ffn_in['b2']}

def reference(x, L0_conv_alpha, L0_conv_sa_key_w, L0_conv_sa_key_bn, L0_conv_sa_att_w1, L0_conv_sa_att_bn, L0_conv_sa_att_w2, L0_conv_sa_att_b2, L0_conv_se_key_w, L0_conv_se_key_b, L0_conv_se_att_w1, L0_conv_se_att_bn, L0_conv_se_att_w2, L0_conv_se_att_b2, L0_conv_se_val_w, L0_conv_se_val_b, L0_ffn_Wr, L0_ffn_br, L0_ffn_W1, L0_ffn_b1, L0_ffn_W2, L0_ffn_b2):
    import jax
    import jax.numpy as jnp

    def _L0_conv_ref(x, alpha, sa_key_w, sa_key_bn, sa_att_w1, sa_att_bn, sa_att_w2, sa_att_b2, se_key_w, se_key_b, se_att_w1, se_att_bn, se_att_w2, se_att_b2, se_val_w, se_val_b):
        import jax, jax.numpy as jnp
        import numpy as np
        BS, C, H, W = (128, 256, 9, 9)
        D = 9
        SPA_HEAD = 32
        HW = H * W
        EPS = 1e-05

        def _bn(x, p, axis=1):
            g, b, m, v = p
            sh = [1] * x.ndim
            sh[axis] = -1
            return (x - m.reshape(sh)) * (g.reshape(sh) * jax.lax.rsqrt(v.reshape(sh) + EPS)) + b.reshape(sh)

        def _conv2d(x, w, groups=1):
            return jax.lax.conv_general_dilated(x, w, (1, 1), 'SAME', dimension_numbers=('NCHW', 'OIHW', 'NCHW'), feature_group_count=groups)
        bs, c, h, w = x.shape
        hw = h * w
        k = x.reshape(bs, c, hw).transpose(0, 2, 1)
        k1 = jax.lax.conv_general_dilated(k, se_key_w, (1,), [(D // 2, D // 2)], dimension_numbers=('NCH', 'OIH', 'NCH'), feature_group_count=hw) + se_key_b[None, :, None]
        k1 = k1.transpose(0, 2, 1).reshape(bs, c, h, w)
        q_flat = x.reshape(bs, 1, c * hw)
        k_flat = k1.reshape(bs, 1, c * hw)
        kq = jnp.stack([q_flat, k_flat], axis=2).reshape(bs, 2 * hw, c)
        a = jax.nn.relu(_bn(jnp.einsum('oi,bic->boc', se_att_w1, kq), se_att_bn))
        a = jnp.einsum('oi,bic->boc', se_att_w2, a) + se_att_b2[None, :, None]
        a = jax.nn.softmax(a, axis=1)
        v = _conv2d(x, se_val_w, groups=c) + se_val_b[None, :, None, None]
        pad_v = jnp.pad(v, ((0, 0), (D // 2, D // 2), (0, 0), (0, 0)))
        v_win = jnp.stack([pad_v[:, k0:k0 + c] for k0 in range(D)], axis=2)
        out1 = jnp.einsum('bcdhw,bdc->bchw', v_win, a) + k1
        k1s = jax.nn.relu(_bn(_conv2d(x, sa_key_w, groups=c), sa_key_bn))
        kq2 = jnp.stack([k1s, x], axis=2).reshape(bs, 2 * c, h, w)
        a2 = jax.nn.relu(_bn(_conv2d(kq2, sa_att_w1, groups=SPA_HEAD), sa_att_bn))
        a2 = _conv2d(a2, sa_att_w2, groups=SPA_HEAD) + sa_att_b2[None, :, None, None]
        a2 = jax.nn.softmax(a2.reshape(bs, SPA_HEAD, hw), axis=-1)
        k2 = jnp.broadcast_to(a2[:, :, None, :], (bs, SPA_HEAD, c // SPA_HEAD, hw)).reshape(bs, c, hw)
        out2 = k1s + (k2 * x.reshape(bs, c, hw)).reshape(bs, c, h, w)
        return alpha * out1 + (1.0 - alpha) * out2

    def _L0_ffn_ref(x, Wr, br, W1, b1, W2, b2):
        import jax, jax.numpy as jnp
        import numpy as np
        B, S, D, H, E = (4, 1024, 256, 512, 8)
        b, s, d = x.shape
        n = b * s
        e = Wr.shape[0]
        xf = x.reshape(n, d)
        logits = xf @ Wr.T + br
        probs = jax.nn.softmax(logits, axis=-1)
        top2_prob, top2_idx = jax.lax.top_k(probs, 2)
        comb = jnp.zeros((n, e), x.dtype).at[jnp.arange(n)[:, None], top2_idx].add(top2_prob)
        h = jax.nn.gelu(jnp.einsum('nd,edh->enh', xf, W1) + b1[:, None, :], approximate=False)
        o = jnp.einsum('enh,ehd->end', h, W2) + b2[:, None, :]
        y = jnp.einsum('ne,end->nd', comb, o)
        return y.reshape(b, s, d)

    def _gn(v, G=32, eps=1e-05):
        B_, C_, H_, W_ = v.shape
        g = v.reshape(B_, G, C_ // G, H_, W_)
        m = jnp.mean(g, axis=(2, 3, 4), keepdims=True)
        s = jnp.var(g, axis=(2, 3, 4), keepdims=True)
        return ((g - m) / jnp.sqrt(s + eps)).reshape(v.shape)

    def _ln_c(v, eps=1e-06):
        m = jnp.mean(v, axis=1, keepdims=True)
        s = jnp.var(v, axis=1, keepdims=True)
        return (v - m) / jnp.sqrt(s + eps)

    def _ln_t(v, eps=1e-05):
        m = jnp.mean(v, axis=-1, keepdims=True)
        s = jnp.var(v, axis=-1, keepdims=True)
        return (v - m) / jnp.sqrt(s + eps)

    def _to_tokens(v):
        B_, C_, H_, W_ = v.shape
        return v.reshape(B_, C_, H_ * W_).transpose(0, 2, 1)

    def _from_tokens(t, like):
        B_, C_, H_, W_ = like.shape
        return t.transpose(0, 2, 1).reshape(B_, C_, H_, W_)
    x = x + _L0_conv_ref(_ln_c(x), L0_conv_alpha, L0_conv_sa_key_w, L0_conv_sa_key_bn, L0_conv_sa_att_w1, L0_conv_sa_att_bn, L0_conv_sa_att_w2, L0_conv_sa_att_b2, L0_conv_se_key_w, L0_conv_se_key_b, L0_conv_se_att_w1, L0_conv_se_att_bn, L0_conv_se_att_w2, L0_conv_se_att_b2, L0_conv_se_val_w, L0_conv_se_val_b)
    t = _to_tokens(x)
    t = t + _L0_ffn_ref(_ln_t(t), L0_ffn_Wr, L0_ffn_br, L0_ffn_W1, L0_ffn_b1, L0_ffn_W2, L0_ffn_b2)
    x = _from_tokens(t, x)
    return x

_drawn_inputs = setup_inputs


def setup_inputs(seed=0):
    import zlib

    import numpy as np

    out = dict(_drawn_inputs(seed))
    spreads = {'L0_ffn_br': (0.0, 0.346), 'L0_ffn_b1': (0.0, 0.8), 'L0_ffn_b2': (0.0, 0.314)}
    factors = {'L0_conv_sa_att_w1': 40.628,
     'L0_conv_sa_att_w2': 37.856,
     'L0_conv_sa_att_b2': 64.0,
     'L0_conv_se_att_w1': 8.0,
     'L0_conv_se_att_w2': 8.0,
     'L0_conv_se_att_b2': 45.282,
     'L0_conv_se_val_b': 6.583,
     'L0_ffn_W1': 2.829}
    for name, (base, spread) in spreads.items():
        noise = np.random.default_rng([zlib.crc32(name.encode()), seed]).standard_normal(out[name].shape)
        drawn = base * np.exp(spread * noise) if base else spread * noise
        out[name] = jnp.asarray(drawn.astype(out[name].dtype))
    for name, factor in factors.items():
        out[name] = (out[name] * factor).astype(out[name].dtype)
    return out
```

```python
import concourse.bass as bass
from concourse import mybir
from contextlib import ExitStack

BS, C, H, W = 128, 256, 9, 9
HW = H * W
HALVES = C // 128
D = 9
EXPERTS, HID = 8, 512
BN_EPS, LN_C_EPS, LN_T_EPS = 1e-5, 1e-6, 1e-5
G = 4
GROUPS = BS // G
TOK = G * HW
SUB = TOK // 3
KB = HID // 128
QUAD = 4
CHUNK = 32
WSCALE = 64.0
BAND0, BAND1 = 132, 160
ZLEN = 264
BAND1_START = 96

CREDIT = 1
CREDITED = """k1_c phase_b k1_ev v_c ks_c pt_c e_c x1_c fin_c gel_c cv_p mb_p tr_c st_v0 st_v1 lg_p raw_p
              w2_p""".split()


def metaformer_kernel(nc, x, taps, tap_bn, tap_rows, toeplitz_mask, ident, band_masks, rot_masks, zstrings,
                      key_bias, se_w1, se_bn, se_w2, sa_w1, sa_bn, sa_w2, sa_b2, alpha, router, router_bias,
                      lower, ffn_w1, ffn_b1, ffn_w2, ffn_b2, out):
    fp32, fp16 = mybir.dt.float32, mybir.dt.float16
    ALU, ACT, AX = mybir.AluOpType, mybir.ActivationFunctionType, mybir.AxisListType

    ctx = ExitStack()
    with ctx:
        def sb(name, shape, dt=fp32):
            return ctx.enter_context(nc.sbuf_tensor(name, shape, dt))

        def sem(name):
            return ctx.enter_context(nc.semaphore(name))

        def dram(name, shape):
            return nc.dram_tensor(name, shape, fp32, kind="Internal").ap()

        xn_d, k1_d, v_d, ks_d, r_d = (dram(n, [BS, C * HW]) for n in ("xn_d", "k1_d", "v_d", "ks_d", "r_d"))

        u_d = dram("u_d", [HW, 128, 136])

        ident_s = sb("ident_s", [128, 128])
        band_s = sb("band_s", [128, BAND0 + BAND1])
        rot_s = sb("rot_s", [128, 8])
        alpha_s = sb("alpha_s", [128, 2])
        se_w1_s = sb("se_w1_s", [HW, 2, HW])
        se_w2_s = sb("se_w2_s", [HW + 1, D])
        se_bn_s = sb("se_bn_s", [HW, 4])
        se_ab = sb("se_ab", [HW, 3])
        sa_w1_s = sb("sa_w1_s", [128, HALVES, 2, 128])
        sa_w2_s = sb("sa_w2_s", [128, HALVES, 128])
        sa_bn_s = sb("sa_bn_s", [128, HALVES, 4])
        sa_ab = sb("sa_ab", [128, HALVES, 3])
        sa_b2_s = sb("sa_b2_s", [128, HALVES])
        router_s = sb("router_s", [128, HALVES, EXPERTS])
        router_bias_s = sb("router_bias_s", [128, EXPERTS])
        lower_s = sb("lower_s", [128, EXPERTS * EXPERTS])
        b1_s = sb("b1_s", [128, EXPERTS, KB])
        b2_s = sb("b2_s", [EXPERTS, C])
        sel_s = sb("sel_s", [EXPERTS, EXPERTS, 128])
        big = sb("big", [128, C * HW])
        pool_ = sb("pool_", [128, C * HW])

        cursor = [0]

        def take(parts, *dims):
            n = 1
            for d in dims:
                n *= d
            a = pool_[0:parts, cursor[0]:cursor[0] + n]
            cursor[0] += n
            assert cursor[0] <= C * HW
            names = "abcde"[:len(dims)]
            if len(dims) > 1:
                a = a.rearrange(f"p ({' '.join(names)}) -> p {' '.join(names)}",
                                **{m: d for m, d in zip(names, dims)})
            return a

        stats = sb("stats", [128, 4, HW])
        u_s = sb("u_s", [128, 3, 136])
        xp_s = sb("xp_s", [128, 3, C])
        xt_s = sb("xt_s", [128, 3, C])
        kb_s = sb("kb_s", [128, HW])
        sq_s = sb("sq_s", [128, 8 * HW])

        psum = [ctx.enter_context(nc.psum_tensor(f"bank{i}", [128, 512], fp32)) for i in range(0)]
        ps = ctx.enter_context(nc.psum_tensor("ps", [128, 8, 512], fp32))

        cursor[0] = 0
        mask_s = take(11, HW, HW + 1)
        m_s = take(HW + 1, CHUNK, 2, HW)
        taps_s = take(11, 2, C)
        tapc_s = take(11, 2, CHUNK)
        tapbn_s = take(11, 2, C)
        taprow_s = take(11, 2)
        xq_s = take(128, 2, QUAD, HW)
        xr_s = take(128, 2, QUAD, HW)
        kr_s = take(128, 2, QUAD, HW)
        pt_s = take(HW + 1, 2, QUAD, BS)
        v_s = take(128, 2, QUAD, HW)
        ks_s = take(128, 2, QUAD, HW)
        r_s = take(128, 2, QUAD, HW)
        cursor[0] = 0
        kq_s = take(HW, 2, 2, G, C)
        xc_s, vc_s, kc_s, rc_s = (take(128, 2, HALVES, G, HW) for _ in range(4))
        a_s = take(HW + 1, G, C)
        lg_s = take(128, G * 2, D)
        st_s = take(128, 4, G * 2)
        ap_s = take(128, G * 2, 15)
        t1_s = take(128, G * 2, 32)
        ar_s = take(128, G * 2, 16)
        arx_s = take(128, G * 2, 128)
        a0_s = take(128, G, BAND0)
        a1_s = take(128, G, BAND1)
        a2_s = take(128, HALVES, TOK)
        e_s = take(128, HALVES, G, HW)
        sm_s = take(128, 4, HALVES * G)
        cursor[0] = 0
        w1_s = take(128, EXPERTS * 2 * HID).bitcast(fp16).rearrange("p (s e k n) -> p s e k n", s=2, e=EXPERTS, k=2)
        w2_s = take(128, EXPERTS * KB * C).bitcast(fp16).rearrange("p (s e k n) -> p s e k n", s=2, e=EXPERTS, k=KB)
        xs_s = sb("xs_s", [128, HALVES, TOK])
        bs_s = sb("bs_s", [SUB, 3, 10])
        pr_s = sb("pr_s", [SUB, 3, 4, EXPERTS])
        cmp_s = sb("cmp_s", [SUB, 2, 3, EXPERTS * EXPERTS])
        comb_t = sb("comb_t", [EXPERTS, TOK])
        wl_s = xs_s
        xf_t = take(SUB, 3, C)
        xf_c = xs_s
        xh_s = sb("xh_s", [128, 2, HALVES, TOK], fp16)
        cb_s = sb("cb_s", [128, TOK])
        hf_s = sb("hf_s", [128, 2, TOK])
        hc_s = sb("hc_s", [128, 2, TOK])
        hh_s = sb("hh_s", [128, 2, 2, TOK], fp16)

        names = """settle_g settle_v tapc_c var_c root_c win_out w_in x_in sum_c cent sq_c norm xn_out k1_out kb_in u_in xp_c tr_c xt_c k1_c k1_ev
                   tab_in tab_c xq_in0 xq_in1 rk_in0 rk_in1 mb_p mb_e0 mb_e1 tq_p pt_c cv_p v_c ks_c r1_c r_c st_v0 st_v1 ch_d
                   ch_a ch_g kq_in0 kq_in1 c_in0 c_in1 se1_p a_c lg_p lgs_c ex_c ap_c ar_c arx_c raw_p msk_c sa1_p a2_c
                   l2_p l2m_c e_c band_p x1_c ones_c one_g wst_in wst_c whi_c wlo_c xs_c t1_p xft_c t2_p xfc_c
                   xhi_c xlo_c rl_p comb_c ct_p ctc_c cb_p cb_c h_p gel_c hc_c hhi_c hlo_c w2_p y_p fin_c out_s
                   sq_p phase_a phase_b probs_c""".split()
        S = {n: sem(n) for n in names}

        def by_pixel(buf):
            return buf[:, :].rearrange("b (c p) -> b p c", p=HW)

        def by_channel(buf):
            return buf[:, :].rearrange("b (c p) -> b c p", p=HW)

        chan = 8
        W_IN = 16 * 17
        block = ctx.enter_context(nc.Block())

        @block.sync
        def _(sp):
            sp.dma_start(big[:, :], x).then_inc(S["x_in"], 16)
            n = 0
            for dst, src in ((ident_s[:, :], ident), (band_s[:, :], band_masks), (rot_s[:, :], rot_masks),
                             (alpha_s[:, 0:1], alpha), (se_w1_s[:, :, :], se_w1), (se_w2_s[:, :], se_w2),
                             (se_bn_s[:, :], se_bn), (sa_w1_s[:, :, :, :], sa_w1), (sa_w2_s[:, :, :], sa_w2),
                             (sa_bn_s[:, :, :], sa_bn), (sa_b2_s[:, :], sa_b2), (router_s[:, :, :], router),
                             (router_bias_s[:, :], router_bias), (lower_s[:, :], lower), (b1_s[:, :, :], ffn_b1),
                             (b2_s[:, :], ffn_b2), (kb_s[:, :], key_bias)):
                sp.dma_start(dst, src).then_inc(S["w_in"], 16)
                n += 1
            assert 16 * n == W_IN
            sp.wait_ge(S["norm"], 1)
            sp.dma_start(xn_d, big[:, :]).then_inc(S["xn_out"], 16)
            window = bass.AP(zstrings.tensor, 127, [[ZLEN, HW], [-1, 128], [1, 136]])
            sp.dma_start(u_d, window).then_inc(S["win_out"], 16)
            sp.wait_ge(S["win_out"], 16)
            with sp.Fori(0, HW // 3) as i:
                sp.wait_ge(S["k1_c"], i + CREDIT)
                src = u_d[bass.ds(i * 3, 3), :, :].rearrange("t c j -> c t j")
                sp.dma_start(u_s[:, :, :], src).then_inc(S["u_in"], 16)
            sp.wait_ge(S["k1_ev"], HW // 3 + CREDIT)
            sp.dma_start(k1_d, pool_[:, :]).then_inc(S["k1_out"], 16)
            sp.wait_ge(S["k1_out"], 16)
            sp.wait_ge(S["xn_out"], 16)
            for dst, src in ((mask_s, toeplitz_mask), (taps_s, taps), (tapbn_s, tap_bn), (taprow_s, tap_rows)):
                sp.dma_start(dst, src).then_inc(S["tab_in"], 16)
            def load_quad(q, par):
                cols = bass.ds(q * (QUAD * HW), QUAD * HW)
                sp.wait_ge(S["sq_p"], q)
                sp.dma_start(xq_s[:, par], xn_d[:, cols].rearrange("b (c p) -> b c p", p=HW)).then_inc(S[f"xq_in{par}"], 16)
                sp.dma_start(xr_s[:, par], x[:, cols].rearrange("b (c p) -> b c p", p=HW)).then_inc(S[f"rk_in{par}"], 16)
                sp.dma_start(kr_s[:, par], k1_d[:, cols].rearrange("b (c p) -> b c p", p=HW)).then_inc(S[f"rk_in{par}"], 16)

            def store_quad(q, par):
                cols = bass.ds(q * (QUAD * HW), QUAD * HW)
                for dst, src, made in ((v_d, v_s, "v_c"), (ks_d, ks_s, "ks_c"), (r_d, r_s, "r_c")):
                    sp.wait_ge(S[made], q + 1 + (0 if made == "r_c" else CREDIT))
                    sp.dma_start(dst[:, cols].rearrange("b (c p) -> b c p", p=HW),
                                 src[:, par]).then_inc(S[f"st_v{par}"], 16)

            load_quad(0, 0)
            with sp.Fori(0, C // QUAD // 2 - 1) as i:
                for par in range(2):
                    load_quad(i * 2 + par + 1, 1 - par)
                    store_quad(i * 2 + par, par)
            last_quad = C // QUAD - 1
            load_quad(last_quad, 1)
            store_quad(last_quad - 1, 0)
            store_quad(last_quad, 1)
            for par in range(2):
                sp.wait_ge(S[f"st_v{par}"], 48 * (C // QUAD // 2) + CREDIT)
            with sp.Fori(0, GROUPS // 2) as i:
                for par in range(2):
                    g = i * 2 + par
                    sp.wait_ge(S["phase_b"], g + CREDIT)
                    rows = bass.ds(g * G, G)
                    for k, src in enumerate((xn_d, k1_d)):
                        sp.dma_start(kq_s[:, par, k],
                                     src[rows, :].rearrange("b (i j) -> i b j", j=C)).then_inc(S[f"kq_in{par}"], 16)
                    for dst, src in ((xc_s, xn_d), (vc_s, v_d), (kc_s, ks_d), (rc_s, r_d)):
                        for h in range(HALVES):
                            sp.dma_start(dst[:, par, h],
                                         src[rows, h * 128 * HW:(h + 1) * 128 * HW]
                                         .rearrange("b (c p) -> c b p", p=HW)).then_inc(S[f"c_in{par}"], 16)
            sp.wait_ge(S["x1_c"], GROUPS + CREDIT)
            n = 0
            for e in range(EXPERTS):
                for src in (ffn_w1, ffn_w2):
                    for k in range(2):
                        if n:
                            sp.wait_ge(S["wlo_c"], n)
                        sp.dma_start(xs_s[:, :, :].rearrange("p h t -> p (h t)")[:, 0:512],
                                     src[e, k]).then_inc(S["wst_in"], 16)
                        n += 1
            with sp.Fori(0, GROUPS) as g:
                sp.wait_ge(S["fin_c"], g + 1 + CREDIT)
                for h in range(HALVES):
                    sp.dma_start(out[bass.ds(g * G, G), h * 128 * HW:(h + 1) * 128 * HW]
                                 .rearrange("b (c p) -> c b p", p=HW),
                                 big[:, bass.ds(g * (HALVES * TOK) + h * TOK, TOK)]
                                 .rearrange("c (b p) -> c b p", p=HW)).then_inc(S["out_s"], 16)
            sp.wait_ge(S["out_s"], 16 * HALVES * GROUPS)

        @block.tensor
        def _(pe):
            pe.wait_ge(S["w_in"], W_IN)
            pb = 2
            with pe.Fori(0, HW // 3) as i:
                pe.wait_ge(S["xp_c"], i + 1)
                for k in range(3):
                    for h in range(HALVES):
                        last = nc.tensor.transpose(ps[:, k, h * 128:(h + 1) * 128],
                                                   xp_s[:, k, h * 128:(h + 1) * 128], ident_s[:, :])
                last.then_inc(S["tr_c"], 1)
                pe.wait_ge(S["u_in"], 16 * (i + 1))
                pe.wait_ge(S["xt_c"], i + 1)
                pe.wait_ge(S["k1_ev"], i + CREDIT)
                for k in range(3):
                    nc.tensor.matmul(ps[:, 3 + k, 0:132], xt_s[:, k, 0:128], u_s[:, k, 4:136],
                                     start=True, stop=False, skip_group_check=True)
                    last = nc.tensor.matmul(ps[:, 3 + k, 124:256], xt_s[:, k, 128:256], u_s[:, k, 0:132],
                                            start=False, stop=True, skip_group_check=True)
                last.then_inc(S["k1_c"], 1)
            pe.wait_ge(S["tab_c"], 1)
            with pe.Fori(0, C // CHUNK) as i:
                pe.wait_ge(S["v_c"], i * 8 + CREDIT)
                pe.wait_ge(S["ks_c"], i * 8 + CREDIT)
                pe.wait_ge(S["tapc_c"], i + 1)
                for n in range(9):
                    if n >= 2:
                        pe.wait_ge(S[f"mb_e{n % 2}"], i * (5 - n % 2) + n // 2)
                    b0 = 2 * (n % 2)
                    flat = ps[0:HW + 1, b0:b0 + 2, :].rearrange("p b n -> p (b n)")
                    for m in range(9):
                        last = nc.tensor.matmul(flat[:, m * 2 * CHUNK:(m + 1) * 2 * CHUNK].rearrange("p (v c) -> p v c", v=2),
                                                mask_s[:, n * 9 + m, :],
                                                tapc_s[:, :, :],
                                                start=True, stop=True)
                    last.then_inc(S["mb_p"], 1)
                for q in range(8):
                    par = q % 2
                    pe.wait_ge(S[f"xq_in{par}"], 16 * (i * 4 + q // 2 + 1))
                    pe.wait_ge(S["pt_c"], i * 8 + max(q - 1, 0) + CREDIT)
                    for c in range(QUAD):
                        last = nc.tensor.transpose(ps[0:HW, 4 + par, c * BS:(c + 1) * BS], xq_s[:, par, c, :],
                                                   ident_s[:, :])
                    last.then_inc(S["tq_p"], 1)
                    if q == 0:
                        pe.wait_ge(S["mb_e0"], i * 5 + 5)
                        pe.wait_ge(S["mb_e1"], i * 4 + 4)
                    pe.wait_ge(S["pt_c"], i * 8 + q + 1 + CREDIT)
                    if q >= 2:
                        pe.wait_ge(S["v_c"], i * 8 + q - 1 + CREDIT)
                        pe.wait_ge(S["ks_c"], i * 8 + q - 1 + CREDIT)
                    b0 = 6 if par == 0 else 2
                    for c in range(QUAD):
                        o = ps[:, b0 + c // 2, (c % 2) * 2 * HW:(c % 2 + 1) * 2 * HW]
                        last = nc.tensor.matmul(o, pt_s[:, par, c, :], m_s[:, q * QUAD + c, :, :]
                                                .rearrange("p v n -> p (v n)"), start=True, stop=True)
                    last.then_inc(S["cv_p"], 1)
            pe.wait_ge(S["phase_a"], 1)
            with pe.Fori(0, GROUPS // 2) as i:
                for par in range(2):
                    g = i * 2 + par
                    pe.wait_ge(S[f"kq_in{par}"], 32 * (i + 1))
                    for n in range(2):
                        for k in range(2):
                            last = nc.tensor.matmul(ps[0:HW, n, :], se_w1_s[:, k, :],
                                                    kq_s[:, par, k, 2 * n:2 * n + 2, :].rearrange("p b j -> p (b j)"),
                                                    start=k == 0, stop=k == 1)
                        last.then_inc(S["se1_p"], 1)
                    pe.wait_ge(S[f"c_in{par}"], 128 * (i + 1))
                    pe.wait_ge(S["e_c"], g + CREDIT)
                    for h in range(HALVES):
                        nc.tensor.matmul(ps[:, 2 + h, 0:TOK], sa_w1_s[:, h, 0, :],
                                         kc_s[:, par, h, :, :].rearrange("p b n -> p (b n)"), start=True, stop=False)
                        nc.tensor.matmul(ps[:, 2 + h, 0:TOK], sa_w1_s[:, h, 1, :],
                                         xc_s[:, par, h, :, :].rearrange("p b n -> p (b n)"),
                                         start=False, stop=True).then_inc(S["sa1_p"], 1)
                    for n in range(2):
                        pe.wait_ge(S["a_c"], g * 2 + n + 1)
                        for b in range(2 * n, 2 * n + 2):
                            for h in range(HALVES):
                                j = b * 2 + h
                                last = nc.tensor.matmul(ps[:, 4, j * D:(j + 1) * D],
                                                        a_s[:, b, h * 128:(h + 1) * 128], se_w2_s[:, :],
                                                        start=True, stop=True)
                    last.then_inc(S["lg_p"], 1)
                    for h in range(HALVES):
                        pe.wait_ge(S["a2_c"], g * 2 + h + 1)
                        nc.tensor.matmul(ps[:, 2 + h, 0:TOK], sa_w2_s[:, h, :], a2_s[:, h, :],
                                         start=True, stop=True).then_inc(S["l2_p"], 1)
                    pe.wait_ge(S["arx_c"], g + 1)
                    for n in range(2):
                        for b in range(2):
                            for h in range(HALVES):
                                last = nc.tensor.matmul(ps[:, 5 - n, b * C + h * 128:b * C + (h + 1) * 128],
                                                        arx_s[:, (2 * n + b) * 2 + h, :], ident_s[:, :],
                                                        start=True, stop=True)
                        last.then_inc(S["raw_p"], 1)
                    pe.wait_ge(S["msk_c"], 2 * (g + 1))
                    pe.wait_ge(S["x1_c"], g + CREDIT)
                    for b in range(G):
                        v0, v1 = vc_s[:, par, 0, b, :], vc_s[:, par, 1, b, :]
                        o = slice(b * HW, (b + 1) * HW)
                        nc.tensor.matmul(ps[:, 6, o], a0_s[:, b, 0:128], v0, start=True, stop=False,
                                         skip_group_check=True)
                        nc.tensor.matmul(ps[96:128, 6, o], a1_s[:, b, 0:32], v1, start=False, stop=True,
                                         skip_group_check=True)
                        nc.tensor.matmul(ps[:, 7, o], a1_s[:, b, 32:160], v1, start=True, stop=False,
                                         skip_group_check=True)
                        last = nc.tensor.matmul(ps[0:4, 7, o], a0_s[:, b, 128:132], v0, start=False, stop=True,
                                                skip_group_check=True)
                    last.then_inc(S["band_p"], 1)
            pe.wait_ge(S["wlo_c"], EXPERTS * 4)
            with pe.Fori(0, GROUPS) as g:
                pe.wait_ge(S["xs_c"], g + 1)
                for s in range(3):
                    for h in range(HALVES):
                        last = nc.tensor.transpose(ps[0:SUB, s // 2, (s % 2) * C + h * 128:(s % 2) * C + (h + 1) * 128],
                                                   xs_s[:, h, s * SUB:(s + 1) * SUB], ident_s[:, :])
                last.then_inc(S["t1_p"], 1)
                pe.wait_ge(S["xft_c"], g + 1)
                for h in range(HALVES):
                    for s in range(3):
                        last = nc.tensor.transpose(ps[:, 2 + h, s * SUB:(s + 1) * SUB],
                                                   xf_t[:, s, h * 128:(h + 1) * 128], ident_s[0:SUB, 0:SUB])
                last.then_inc(S["t2_p"], 1)
                pe.wait_ge(S["xfc_c"], g + 1)
                for s in range(3):
                    for h in range(HALVES):
                        last = nc.tensor.matmul(ps[0:SUB, 0, s * EXPERTS:(s + 1) * EXPERTS],
                                                xf_c[:, h, s * SUB:(s + 1) * SUB], router_s[:, h, :],
                                                start=h == 0, stop=h == 1)
                last.then_inc(S["rl_p"], 1)
                pe.wait_ge(S["comb_c"], g + 1)
                for s in range(3):
                    last = nc.tensor.transpose(ps[0:EXPERTS, 0, s * SUB:(s + 1) * SUB], pr_s[:, s, 3, :],
                                               ident_s[0:SUB, 0:SUB])
                last.then_inc(S["ct_p"], 1)
                pe.wait_ge(S["ctc_c"], g + 1)
                pe.wait_ge(S["xlo_c"], g + 1)
                pe.wait_ge(S["fin_c"], g + CREDIT)

                def up(n):
                    e, j = divmod(n, KB)
                    if j == 0:
                        if e:
                            pe.wait_ge(S["cb_c"], g * EXPERTS + e)
                        nc.tensor.matmul(ps[:, 1, 0:TOK], sel_s[:, e, :], comb_t[:, :],
                                         start=True, stop=True).then_inc(S["cb_p"], 1)
                    if n >= 4:
                        pe.wait_ge(S["gel_c"], g * 32 + n - 3 + CREDIT)
                    else:
                        pe.wait_ge(S["gel_c"], g * 32 + CREDIT)
                    bank = 2 + n % 4
                    order = [(k, a, b) for k in range(2) for a, b in ((0, 0), (0, 1), (1, 0))]
                    for t, (k, a, b) in enumerate(order):
                        last = nc.tensor.matmul(ps[:, bank, 0:TOK], w1_s[:, a, e, k, j * 128:(j + 1) * 128],
                                                xh_s[:, b, k, :], start=t == 0, stop=t == 5)
                    last.then_inc(S["h_p"], 1)

                def down(n):
                    e, j = divmod(n, KB)
                    pe.wait_ge(S["hlo_c"], g * 32 + n + 1)
                    pe.wait_ge(S["hhi_c"], g * 32 + n + 1)
                    for h in range(HALVES):
                        for a, b in ((0, 0), (0, 1), (1, 0)):
                            last = nc.tensor.matmul(ps[:, 6 + h, 0:TOK], w2_s[:, a, e, j, h * 128:(h + 1) * 128],
                                                    hh_s[:, n % 2, b, :], start=False, stop=False,
                                                    skip_group_check=True)
                    last.then_inc(S["w2_p"], 1)

                for h in range(HALVES):
                    nc.tensor.matmul(ps[:, 6 + h, 0:TOK], b2_s[:, h * 128:(h + 1) * 128], comb_t[:, :],
                                     start=True, stop=False, skip_group_check=True)
                for n in range(EXPERTS * KB):
                    up(n)
                    if n >= 2:
                        down(n - 2)
                down(EXPERTS * KB - 2)
                down(EXPERTS * KB - 1)

        @block.vector
        def _(dve):
            done = {"before": 0, "links": 0, "roots": 0}

            def link(ins):
                done["links"] += 1
                ins.then_inc(S["ch_d"], 1)
                dve.wait_ge(S["ch_d"], done["before"] + done["links"])


            def inverse_root(var, eps, scale, dst):
                nc.vector.tensor_scalar(dst, var, scale, eps, ALU.mult, ALU.add).then_inc(S["var_c"], 1)
                done["roots"] += 1
                dve.wait_ge(S["root_c"], done["roots"])
                link(nc.vector.reciprocal(dst, dst))

            dve.wait_ge(S["w_in"], W_IN)
            for p, ab in ((se_bn_s[:, :].unsqueeze(1), se_ab[:, :].unsqueeze(1)), (sa_bn_s, sa_ab)):
                gg, bb, mm, vv = (p[:, :, k:k + 1] for k in range(4))
                inverse_root(vv, BN_EPS, 1.0, ab[:, :, 0:1])
                link(nc.vector.tensor_tensor(ab[:, :, 0:1], ab[:, :, 0:1], gg, ALU.mult))
                link(nc.vector.tensor_tensor(ab[:, :, 2:3], ab[:, :, 0:1], mm, ALU.mult))
                link(nc.vector.tensor_tensor(ab[:, :, 1:2], bb, ab[:, :, 2:3], ALU.subtract))
            link(nc.vector.tensor_scalar(alpha_s[:, 1:2], alpha_s[:, 0:1], -1.0, 1.0, ALU.mult, ALU.add))
            link(nc.vector.tensor_scalar(b2_s[:, :], b2_s[:, :], WSCALE, None, ALU.mult))
            dve.wait_ge(S["x_in"], 16)
            link(nc.vector.reduce_sum(stats[:, 0, :], by_pixel(big), axis=AX.X))
            link(nc.vector.tensor_scalar(stats[:, 0, :], stats[:, 0, :], 1.0 / C, None, ALU.mult))
            link(nc.vector.tensor_tensor(by_channel(big), by_channel(big),
                                         stats[:, 0, :].unsqueeze(1).to_broadcast([128, C, HW]), ALU.subtract))
            link(nc.vector.tensor_tensor(by_channel(pool_), by_channel(big), by_channel(big), ALU.mult))
            link(nc.vector.reduce_sum(stats[:, 1, :], by_pixel(pool_), axis=AX.X))
            inverse_root(stats[:, 1, :], LN_C_EPS, 1.0 / C, stats[:, 1, :])
            nc.vector.tensor_tensor(by_channel(big), by_channel(big),
                                    stats[:, 1, :].unsqueeze(1).to_broadcast([128, C, HW]),
                                    ALU.mult).then_inc(S["norm"], 1)
            with dve.Fori(0, HW // 3) as i:
                dve.wait_ge(S["k1_c"], i + 1 + CREDIT)
                nc.vector.tensor_tensor(by_pixel(pool_)[:, bass.ds(i * 3, 3), :], ps[:, 3:6, 0:C],
                                        kb_s[:, bass.ds(i * 3, 3)].unsqueeze(2).to_broadcast([128, 3, C]),
                                        ALU.add).then_inc(S["k1_ev"], 1)
            dve.wait_ge(S["tab_in"], 64)
            inverse_root(tapbn_s[:, 1, :], BN_EPS, 1.0, tapbn_s[:, 1, :])
            link(nc.vector.tensor_tensor(tapbn_s[:, 0, :], tapbn_s[:, 0, :], tapbn_s[:, 1, :], ALU.mult))
            link(nc.vector.tensor_scalar(tapbn_s[:, 0, :], tapbn_s[:, 0, :], taprow_s[:, 0:1], taprow_s[:, 1:2],
                                         ALU.mult, ALU.add))
            link(nc.vector.tensor_tensor(taps_s[:, 1, :], taps_s[:, 1, :], tapbn_s[:, 0, :], ALU.mult))
            nc.vector.memset(pt_s[:, :, :, :], 1.0).then_inc(S["tab_c"], 1)
            with dve.Fori(0, C // CHUNK) as i:
                dve.wait_ge(S["mb_p"], i * 9 + CREDIT)
                nc.vector.tensor_copy(tapc_s[:, :, :], taps_s[:, :, bass.ds(i * CHUNK, CHUNK)]).then_inc(S["tapc_c"], 1)
                for n in range(1, 9, 2):
                    dve.wait_ge(S["mb_p"], i * 9 + n + 1 + CREDIT)
                    if n == 1:
                        dve.wait_ge(S["cv_p"], i * 8 + CREDIT)
                    flat = ps[0:HW + 1, 2:4, :].rearrange("p b n -> p (b n)")[:, 0:9 * 2 * CHUNK]
                    nc.vector.tensor_copy(m_s[:, :, :, n * 9:(n + 1) * 9].rearrange("p c v m -> p m v c"),
                                          flat.rearrange("p (m v c) -> p m v c", m=9, v=2)).then_inc(S["mb_e1"], 1)
                for q in range(8):
                    par = q % 2
                    dve.wait_ge(S["tq_p"], i * 8 + q + 1)
                    if q >= 2:
                        dve.wait_ge(S["cv_p"], i * 8 + q - 1 + CREDIT)
                    nc.vector.tensor_copy(pt_s[0:HW, par, :, :].rearrange("p c b -> p (c b)"),
                                          ps[0:HW, 4 + par, :]).then_inc(S["pt_c"], 1)
                    dve.wait_ge(S["r1_c"], i * 8 + q + 1)
                    dve.wait_ge(S["ks_c"], i * 8 + q + 1 + CREDIT)
                    nc.vector.scalar_tensor_tensor(r_s[:, par], ks_s[:, par], alpha_s[:, 1:2], kr_s[:, par],
                                                   ALU.mult, ALU.add).then_inc(S["r_c"], 1)
            for par in range(2):
                dve.wait_ge(S[f"st_v{par}"], 48 * (C // QUAD // 2) + CREDIT)
            link(nc.vector.memset(a_s[:, :, :], 1.0))
            link(nc.vector.memset(ap_s[:, :, :], 0.0))
            nc.vector.memset(t1_s[:, :, :], 0.0).then_inc(S["phase_a"], 1)
            dve.wait_ge(S["phase_a"], 1)
            base = done["links"]
            per = 19
            with dve.Fori(0, GROUPS // 2) as i:
                done["before"], done["links"] = i * (2 * per) + base, 0
                for par in range(2):
                    g = i * 2 + par
                    dve.wait_ge(S["lg_p"], g + 1 + CREDIT)
                    lg = ps[:, 4, 0:G * 2 * D].rearrange("p (j d) -> p j d", d=D)
                    link(nc.vector.reduce_max(st_s[:, 0, :], lg, axis=AX.X))
                    nc.vector.tensor_tensor(lg_s[:, :, :], lg, st_s[:, 0, :].unsqueeze(2).to_broadcast([128, G * 2, D]),
                                            ALU.subtract).then_inc(S["lgs_c"], 1)
                    dve.wait_ge(S["ex_c"], g + 1)
                    link(nc.vector.reduce_sum(st_s[:, 1, :], lg_s[:, :, :], axis=AX.X))
                    link(nc.vector.reciprocal(st_s[:, 2, :], st_s[:, 1, :]))
                    link(nc.vector.tensor_scalar(st_s[:, 3, :], st_s[:, 2, :], alpha_s[:, 0:1], None, ALU.mult))
                    link(nc.vector.tensor_tensor(ap_s[:, :, 3:12], lg_s[:, :, :],
                                                 st_s[:, 3, :].unsqueeze(2).to_broadcast([128, G * 2, D]), ALU.mult))
                    for r in range(4):
                        o = t1_s[:, :, :].rearrange("p j (t n) -> p j t n", t=2)[:, :, :, 0:12]
                        a = ap_s[:, :, 3 - r:15 - r].unsqueeze(2).to_broadcast([128, G * 2, 2, 12])
                        if r == 0:
                            for t in range(2):
                                ins = nc.vector.tensor_scalar(t1_s[:, :, 16 * t:16 * t + 12], ap_s[:, :, 3:15],
                                                              rot_s[:, 0:1], None, ALU.mult)
                            link(ins)
                        else:
                            for t in range(2):
                                ins = nc.vector.scalar_tensor_tensor(
                                    t1_s[:, :, 16 * t:16 * t + 12], ap_s[:, :, 3 - r:15 - r], rot_s[:, r:r + 1],
                                    t1_s[:, :, 16 * t:16 * t + 12], ALU.mult, ALU.add)
                            link(ins)
                    for r in range(4):
                        src = t1_s[:, :, 16 - 4 * r:32 - 4 * r] if r else t1_s[:, :, 0:16]
                        if r == 0:
                            link(nc.vector.tensor_scalar(ar_s[:, :, :], src, rot_s[:, 4:5], None, ALU.mult))
                        else:
                            ins = nc.vector.scalar_tensor_tensor(ar_s[:, :, :], src, rot_s[:, 4 + r:5 + r],
                                                                 ar_s[:, :, :], ALU.mult, ALU.add)
                            if r < 3:
                                link(ins)
                            else:
                                ins.then_inc(S["ar_c"], 1)
                    for h in range(HALVES):
                        dve.wait_ge(S["l2_p"], g * 2 + h + 1)
                        ins = nc.vector.reduce_max(sm_s[:, 0, h * G:(h + 1) * G],
                                                   ps[:, 2 + h, 0:TOK].rearrange("p (b n) -> p b n", b=G), axis=AX.X)
                    link(ins)
                    bb = sa_b2_s[:, :].unsqueeze(2).to_broadcast([128, HALVES, G])
                    m3 = sm_s[:, :, :].rearrange("p k (h b) -> p k h b", h=HALVES)
                    link(nc.vector.tensor_tensor(m3[:, 1], m3[:, 0], bb, ALU.add))
                    nc.vector.tensor_tensor(m3[:, 2], bb, m3[:, 1], ALU.subtract).then_inc(S["l2m_c"], 1)
                    for n in range(2):
                        dve.wait_ge(S["raw_p"], g * 2 + n + 1 + CREDIT)
                        raw = ps[:, 5 - n, :].rearrange("p (b c) -> p b c", b=2)
                        nc.vector.tensor_tensor(a0_s[:, 2 * n:2 * n + 2, :], raw[:, :, 0:BAND0],
                                                band_s[:, 0:BAND0].unsqueeze(1).to_broadcast([128, 2, BAND0]), ALU.mult)
                        nc.vector.tensor_tensor(a1_s[:, 2 * n:2 * n + 2, :], raw[:, :, BAND1_START:C],
                                                band_s[:, BAND0:].unsqueeze(1).to_broadcast([128, 2, BAND1]),
                                                ALU.mult).then_inc(S["msk_c"], 1)
                    dve.wait_ge(S["e_c"], g + 1 + CREDIT)
                    link(nc.vector.reciprocal(sm_s[:, 0, :], sm_s[:, 3, :]))
                    link(nc.vector.tensor_scalar(sm_s[:, 1, :], sm_s[:, 0, :], alpha_s[:, 1:2], None, ALU.mult))
                    e3 = e_s[:, :, :, :].rearrange("p h b n -> p (h b) n")
                    ins = nc.vector.tensor_tensor(e3, e3, xc_s[:, par].rearrange("p h b n -> p (h b) n"), ALU.mult)
                    link(ins)
                    link(nc.vector.tensor_tensor(e3, e3, sm_s[:, 1, :].unsqueeze(2).to_broadcast([128, HALVES * G, HW]),
                                                 ALU.mult))
                    link(nc.vector.tensor_tensor(e3, e3, rc_s[:, par].rearrange("p h b n -> p (h b) n"), ALU.add))
                    dve.wait_ge(S["band_p"], g + 1)
                    nc.vector.tensor_tensor(big[:, bass.ds(g * (HALVES * TOK), HALVES * TOK)]
                                            .rearrange("p (h t) -> p h t", h=HALVES),
                                            e_s[:, :, :, :].rearrange("p h b n -> p h (b n)"), ps[:, 6:8, 0:TOK],
                                            ALU.add).then_inc(S["x1_c"], 1)
            assert done["links"] == 2 * per
            base = base + per * GROUPS
            for n in range(EXPERTS * 4):
                e, second, k = n // 4, (n // 2) % 2, n % 2
                st = xs_s[:, :, :].rearrange("p h t -> p (h t)")[:, 0:512]
                if second:
                    hi = w2_s[:, 0, e, 2 * k:2 * k + 2, :].rearrange("p k n -> p (k n)")
                    lo = w2_s[:, 1, e, 2 * k:2 * k + 2, :].rearrange("p k n -> p (k n)")
                else:
                    hi, lo = w1_s[:, 0, e, k, :], w1_s[:, 1, e, k, :]
                dve.wait_ge(S["wst_in"], 16 * (n + 1))
                nc.vector.tensor_scalar(hi, st, WSCALE, None, ALU.mult).then_inc(S["whi_c"], 1)
                dve.wait_ge(S["whi_c"], n + 1)
                nc.vector.scalar_tensor_tensor(lo, st, WSCALE, hi, ALU.mult, ALU.subtract).then_inc(S["wlo_c"], 1)
            dve.wait_ge(S["wlo_c"], EXPERTS * 4)
            perc = 13
            with dve.Fori(0, GROUPS) as g:
                done["before"], done["links"] = g * perc + base, 0
                x1 = big[:, bass.ds(g * (HALVES * TOK), HALVES * TOK)]
                nc.vector.tensor_copy(xs_s[:, :, :].rearrange("p h t -> p (h t)"), x1).then_inc(S["xs_c"], 1)
                dve.wait_ge(S["t1_p"], g + 1)
                row = [ps[0:SUB, s // 2, (s % 2) * C:(s % 2 + 1) * C] for s in range(3)]
                for s in range(3):
                    ins = nc.vector.bn_stats(bs_s[:, s, 0:6], row[s])
                link(ins)
                dve.sem_inc(S["settle_v"], 1)
                for s in range(3):
                    ins = nc.vector.bn_aggr(bs_s[:, s, 6:8], bs_s[:, s, 0:6])
                link(ins)
                nc.vector.tensor_scalar(bs_s[:, :, 8:9], bs_s[:, :, 7:8], LN_T_EPS, None, ALU.add).then_inc(S["var_c"], 1)
                dve.wait_ge(S["root_c"], g + (done["roots"] + 1))
                link(nc.vector.reciprocal(bs_s[:, :, 8:9], bs_s[:, :, 8:9]))
                for s in range(3):
                    ins = nc.vector.tensor_scalar(xf_t[:, s, :], row[s], bs_s[:, s, 6:7], bs_s[:, s, 8:9],
                                                  ALU.subtract, ALU.mult)
                ins.then_inc(S["xft_c"], 1)
                dve.wait_ge(S["t2_p"], g + 1)
                nc.vector.tensor_copy(xf_c[:, :, :], ps[:, 2:4, 0:TOK]).then_inc(S["xfc_c"], 1)
                dve.wait_ge(S["xhi_c"], g + 1)
                nc.vector.tensor_tensor(xh_s[:, 1], xf_c[:, :, :], xh_s[:, 0], ALU.subtract).then_inc(S["xlo_c"], 1)
                dve.wait_ge(S["rl_p"], g + 1)
                lgt = ps[0:SUB, 0, 0:3 * EXPERTS].rearrange("p (s e) -> p s e", s=3)
                link(nc.vector.tensor_tensor(pr_s[:, :, 0, :], lgt,
                                             router_bias_s[0:SUB, :].unsqueeze(1).to_broadcast([SUB, 3, EXPERTS]), ALU.add))
                link(nc.vector.reduce_max(bs_s[:, :, 9:10].rearrange("p s o -> p (s o)"), pr_s[:, :, 0, :], axis=AX.X))
                nc.vector.tensor_tensor(pr_s[:, :, 1, :], pr_s[:, :, 0, :],
                                        bs_s[:, :, 9:10].to_broadcast([SUB, 3, EXPERTS]),
                                        ALU.subtract).then_inc(S["probs_c"], 1)
                dve.wait_ge(S["ex_c"], GROUPS + g + 1)
                link(nc.vector.reduce_sum(bs_s[:, :, 9:10].rearrange("p s o -> p (s o)"), pr_s[:, :, 2, :], axis=AX.X))
                link(nc.vector.reciprocal(bs_s[:, :, 8:9], bs_s[:, :, 9:10]))
                link(nc.vector.tensor_tensor(pr_s[:, :, 1, :], pr_s[:, :, 2, :],
                                             bs_s[:, :, 8:9].to_broadcast([SUB, 3, EXPERTS]), ALU.mult))
                E2 = EXPERTS * EXPERTS
                gt, eq = (cmp_s[:, k].rearrange("p s (e j) -> p s e j", j=EXPERTS) for k in range(2))
                for s in range(3):
                    mine = pr_s[:, s, 1, :].unsqueeze(2).to_broadcast([SUB, EXPERTS, EXPERTS])
                    other = pr_s[:, s, 1, :].unsqueeze(1).to_broadcast([SUB, EXPERTS, EXPERTS])
                    nc.vector.tensor_tensor(gt[:, s], other, mine, ALU.is_gt)
                    ins = nc.vector.tensor_tensor(eq[:, s], other, mine, ALU.is_equal)
                link(ins)
                link(nc.vector.tensor_tensor(cmp_s[:, 1], cmp_s[:, 1],
                                             lower_s[0:SUB, :].unsqueeze(1).to_broadcast([SUB, 3, E2]), ALU.mult))
                link(nc.vector.tensor_tensor(cmp_s[:, 0], cmp_s[:, 0], cmp_s[:, 1], ALU.add))
                link(nc.vector.tensor_reduce(pr_s[:, :, 0, :], gt, axis=AX.X, op=ALU.add))
                link(nc.vector.tensor_scalar(pr_s[:, :, 2, :], pr_s[:, :, 0, :], 1.5, None, ALU.is_lt))
                nc.vector.tensor_tensor(pr_s[:, :, 3, :], pr_s[:, :, 1, :], pr_s[:, :, 2, :],
                                        ALU.mult).then_inc(S["comb_c"], 1)
                dve.wait_ge(S["ct_p"], g + 1)
                nc.vector.tensor_copy(comb_t[:, :], ps[0:EXPERTS, 0, 0:TOK]).then_inc(S["ctc_c"], 1)
                for n in range(EXPERTS * KB):
                    e, j = divmod(n, KB)
                    if j == 0:
                        dve.wait_ge(S["cb_p"], g * EXPERTS + e + 1)
                        nc.vector.tensor_copy(cb_s[:, :], ps[:, 1, 0:TOK]).then_inc(S["cb_c"], 1)
                        dve.wait_ge(S["cb_c"], g * EXPERTS + e + 1)
                    dve.wait_ge(S["gel_c"], g * 32 + n + 1 + CREDIT)
                    if n >= 2:
                        dve.wait_ge(S["hhi_c"], g * 32 + n - 1)
                    nc.vector.tensor_tensor(hc_s[:, n % 2], hf_s[:, n % 2], cb_s[:, :],
                                            ALU.mult).then_inc(S["hc_c"], 1)
                    dve.wait_ge(S["hhi_c"], g * 32 + n + 1)
                    nc.vector.tensor_tensor(hh_s[:, n % 2, 1], hc_s[:, n % 2], hh_s[:, n % 2, 0],
                                            ALU.subtract).then_inc(S["hlo_c"], 1)
                dve.wait_ge(S["w2_p"], (g + 1) * EXPERTS * KB + CREDIT)
                nc.vector.scalar_tensor_tensor(x1.rearrange("p (h t) -> p h t", h=HALVES), ps[:, 6:8, 0:TOK],
                                               1.0 / WSCALE, x1.rearrange("p (h t) -> p h t", h=HALVES),
                                               ALU.mult, ALU.add).then_inc(S["fin_c"], 1)
            assert done["links"] == perc

        @block.scalar
        def _(act):
            for n, v in enumerate((se_ab[:, 0:1], sa_ab[:, :, 0:1], stats[:, 1, :])):
                act.wait_ge(S["var_c"], n + 1)
                nc.scalar.activation(v, v, ACT.Sqrt).then_inc(S["root_c"], 1)
            act.wait_ge(S["norm"], 1)
            with act.Fori(0, HW // 3) as i:
                act.wait_ge(S["tr_c"], i + CREDIT)
                nc.scalar.activation(xp_s[:, :, :], by_pixel(big)[:, bass.ds(i * 3, 3), :], ACT.Copy).then_inc(S["xp_c"], 1)
                act.wait_ge(S["tr_c"], i + 1 + CREDIT)
                act.wait_ge(S["k1_c"], i + CREDIT)
                nc.scalar.activation(xt_s[:, :, :], ps[:, 0:3, 0:C], ACT.Copy).then_inc(S["xt_c"], 1)
            act.wait_ge(S["var_c"], 4)
            nc.scalar.activation(tapbn_s[:, 1, :], tapbn_s[:, 1, :], ACT.Sqrt).then_inc(S["root_c"], 1)
            act.wait_ge(S["tab_c"], 1)
            with act.Fori(0, C // CHUNK) as i:
                for n in range(0, 9, 2):
                    act.wait_ge(S["mb_p"], i * 9 + n + 1 + CREDIT)
                    if n == 0:
                        act.wait_ge(S["cv_p"], i * 8 + CREDIT)
                    flat = ps[0:HW + 1, 0:2, :].rearrange("p b n -> p (b n)")[:, 0:9 * 2 * CHUNK]
                    nc.scalar.activation(m_s[:, :, :, n * 9:(n + 1) * 9].rearrange("p c v m -> p m v c"),
                                         flat.rearrange("p (m v c) -> p m v c", m=9, v=2), ACT.Copy).then_inc(S["mb_e0"], 1)
                for q in range(8):
                    par = q % 2
                    b0 = 6 if par == 0 else 2
                    act.wait_ge(S["cv_p"], i * 8 + q + 1 + CREDIT)
                    act.wait_ge(S[f"st_v{par}"], 48 * (i * 4 + q // 2) + CREDIT)
                    cv = ps[:, b0:b0 + 2, 0:4 * HW].rearrange("p k (c v n) -> p k c v n", c=2, v=2)
                    nc.scalar.activation(v_s[:, par].rearrange("p (k c) n -> p k c n", k=2), cv[:, :, :, 0, :],
                                         ACT.Copy).then_inc(S["v_c"], 1)
                    nc.scalar.activation(ks_s[:, par].rearrange("p (k c) n -> p k c n", k=2), cv[:, :, :, 1, :],
                                         ACT.Relu).then_inc(S["ks_c"], 1)
            act.wait_ge(S["phase_a"], 1)
            with act.Fori(0, GROUPS // 2) as i:
                for par in range(2):
                    g = i * 2 + par
                    for n in range(2):
                        act.wait_ge(S["se1_p"], g * 2 + n + 1)
                        act.wait_ge(S["lg_p"], g + CREDIT)
                        nc.scalar.activation(a_s[0:HW, 2 * n:2 * n + 2, :].rearrange("p b j -> p (b j)"), ps[0:HW, n, :],
                                             ACT.Relu, bias=se_ab[:, 1:2], scale=se_ab[:, 0:1]).then_inc(S["a_c"], 1)
                    for h in range(HALVES):
                        act.wait_ge(S["sa1_p"], g * 2 + h + 1)
                        nc.scalar.activation(a2_s[:, h, :], ps[:, 2 + h, 0:TOK], ACT.Relu, bias=sa_ab[:, h, 1:2],
                                             scale=sa_ab[:, h, 0:1]).then_inc(S["a2_c"], 1)
                    act.wait_ge(S["lgs_c"], g + 1)
                    nc.scalar.activation(lg_s[:, :, :], lg_s[:, :, :], ACT.Exp).then_inc(S["ex_c"], 1)
                    act.wait_ge(S["l2m_c"], g + 1)
                    act.wait_ge(S["x1_c"], g + CREDIT)
                    for h in range(HALVES):
                        for b in range(G):
                            j = h * G + b
                            ins = nc.scalar.activation(e_s[:, h, b, :], ps[:, 2 + h, b * HW:(b + 1) * HW], ACT.Exp,
                                                       bias=sm_s[:, 2, j:j + 1], accum_out=sm_s[:, 3, j:j + 1])
                    ins.then_inc(S["e_c"], 1)
            with act.Fori(0, GROUPS) as g:
                act.wait_ge(S["var_c"], g + 5)
                nc.scalar.activation(bs_s[:, :, 8:9], bs_s[:, :, 8:9], ACT.Sqrt).then_inc(S["root_c"], 1)
                act.wait_ge(S["probs_c"], g + 1)
                nc.scalar.activation(pr_s[:, :, 2, :], pr_s[:, :, 1, :], ACT.Exp).then_inc(S["ex_c"], 1)
                for n in range(EXPERTS * KB):
                    e, j = divmod(n, KB)
                    act.wait_ge(S["h_p"], g * 32 + n + 1)
                    if n >= 2:
                        act.wait_ge(S["hc_c"], g * 32 + n - 1)
                    nc.scalar.activation(hf_s[:, n % 2], ps[:, 2 + n % 4, 0:TOK], ACT.Gelu, bias=b1_s[:, e, j:j + 1],
                                         scale=1.0 / WSCALE).then_inc(S["gel_c"], 1)

        @block.gpsimd
        def _(pool):
            for n in CREDITED:
                pool.sem_inc(S[n], CREDIT)
            nc.gpsimd.memset(sel_s[:, :, :], 0.0).then_inc(S["one_g"], 1)
            pool.wait_ge(S["one_g"], 1)
            nc.gpsimd.affine_select(out=sel_s[:, :, :], in_=sel_s[:, :, :], compare_op=ALU.not_equal, fill=1.0,
                                    base=0, pattern=[[-1, EXPERTS], [0, 128]], channel_multiplier=1).then_inc(S["ones_c"], 1)
            pool.wait_ge(S["w_in"], W_IN)

            def settle():
                pool.sem_inc(S["settle_g"], 1)

            pool.sem_inc(S["sq_p"], 1)
            pool.sem_inc(S["phase_b"], 1)
            with pool.Fori(0, C // QUAD // 2) as i:
                for par in range(2):
                    q = i * 2 + par
                    pool.wait_ge(S[f"rk_in{par}"], 32 * (i + 1))
                    settle()
                    nc.gpsimd.tensor_scalar(kr_s[:, par], kr_s[:, par], alpha_s[:, 0:1], None, ALU.mult).then_inc(S["ch_g"], 1)
                    pool.wait_ge(S["ch_g"], q + 1)
                    settle()
                    nc.gpsimd.tensor_tensor(kr_s[:, par], kr_s[:, par], xr_s[:, par], ALU.add).then_inc(S["r1_c"], 1)
                    pool.wait_ge(S["r_c"], q + 1)
                    pool.wait_ge(S["cv_p"], q + 1 + CREDIT)
                    pool.sem_inc(S["sq_p"], 1)
            with pool.Fori(0, GROUPS) as g:
                pool.wait_ge(S["ar_c"], g + 1)
                pool.wait_ge(S["raw_p"], 2 * g + CREDIT)
                settle()
                nc.gpsimd.tensor_copy(arx_s[:, :, :].rearrange("p j (t n) -> p j t n", n=16),
                                      ar_s[:, :, :].unsqueeze(2).to_broadcast([128, G * 2, 8, 16])).then_inc(S["arx_c"], 1)
                pool.wait_ge(S["x1_c"], g + 1 + CREDIT)
                pool.sem_inc(S["phase_b"], 1)
            with pool.Fori(0, GROUPS) as g:
                pool.wait_ge(S["xfc_c"], g + 1)
                pool.wait_ge(S["w2_p"], g * 32 + CREDIT)
                settle()
                nc.gpsimd.tensor_copy(xh_s[:, 0], xf_c[:, :, :]).then_inc(S["xhi_c"], 1)
                for n in range(EXPERTS * KB):
                    pool.wait_ge(S["hc_c"], g * 32 + n + 1)
                    if n >= 2:
                        pool.wait_ge(S["w2_p"], g * 32 + n - 1 + CREDIT)
                    settle()
                    nc.gpsimd.tensor_copy(hh_s[:, n % 2, 0], hc_s[:, n % 2]).then_inc(S["hhi_c"], 1)


def _shape_constants(np):
    toep = np.zeros((11, HW, HW + 1), np.float32)
    for ky in range(3):
        for kx in range(3):
            for y in range(H):
                for xx in range(W):
                    yy, xi = y + ky - 1, xx + kx - 1
                    if 0 <= yy < H and 0 <= xi < W:
                        toep[ky * 3 + kx, y * W + xx, yy * W + xi] = 1.0
    toep[9, :, HW] = -1.0
    toep[10, :, HW] = 1.0
    r = np.arange(128)
    band0 = (abs(np.arange(BAND0)[None] - r[:, None]) <= D // 2)
    band1 = (abs(np.arange(BAND1)[None] + BAND1_START - 128 - r[:, None]) <= D // 2)
    turn = (r - D // 2) % 16
    rot = np.concatenate([(turn % 4)[:, None] == np.arange(4), (turn // 4)[:, None] == np.arange(4)], 1)
    rows = np.ones((11, 2), np.float32)
    rows[:, 1] = 0.0
    rows[10] = (0.0, 1.0)
    lower = np.tile(np.tril(np.ones((EXPERTS, EXPERTS)), -1).reshape(1, -1), (128, 1))
    f = np.float32
    return toep, np.concatenate([band0, band1], 1).astype(f), rot.astype(f), rows, lower.astype(f)


def kernel(**inputs):
    import numpy as np
    import concourse.bacc as bacc
    from concourse import mybir as mb
    from concourse.bass_utils import run_bass_kernel_spmd

    i = {k.replace("L0_", ""): np.ascontiguousarray(v) for k, v in inputs.items()}
    toep, bands, rot, rows, lower = _shape_constants(np)
    f = np.float32
    taps = np.zeros((11, 2, C), f)
    taps[0:9, 0] = i["conv_se_val_w"].reshape(C, 9).T
    taps[10, 0] = i["conv_se_val_b"]
    taps[0:9, 1] = i["conv_sa_key_w"].reshape(C, 9).T
    taps[9, 1] = i["conv_sa_key_bn"][2]
    taps[10, 1] = i["conv_sa_key_bn"][1]
    tap_bn = np.ascontiguousarray(np.broadcast_to(i["conv_sa_key_bn"][[0, 3]], (11, 2, C)))
    z = np.zeros((HW, ZLEN), f)
    z[:, 127:136] = i["conv_se_key_w"][:, 0, ::-1]
    w1 = i["conv_sa_att_w1"].reshape(C, 8, 2)
    w2 = i["conv_sa_att_w2"].reshape(C // 8, 8)
    sa_w1 = np.zeros((128, HALVES, 2, 128), f)
    sa_w2 = np.zeros((128, HALVES, 128), f)
    for h in range(HALVES):
        for g in range(16):
            s = slice(g * 8, g * 8 + 8)
            for k in range(2):
                sa_w1[s, h, k, s] = w1[h * 128 + g * 8:h * 128 + g * 8 + 8, :, k].T
            sa_w2[s, h, s] = np.broadcast_to(w2[h * 16 + g][:, None], (8, 8))

    def halves(a):
        return np.ascontiguousarray(a.reshape(HALVES, 128, -1).transpose(1, 0, 2))

    se_w2 = np.concatenate([i["conv_se_att_w2"].T, i["conv_se_att_b2"][None]], 0)
    arrays = {
        "x": i["x"].reshape(BS, C * HW), "taps": taps, "tap_bn": tap_bn, "tap_rows": rows, "toeplitz_mask": toep,
        "ident": np.eye(128, dtype=f), "band_masks": bands, "rot_masks": rot, "zstrings": z,
        "key_bias": np.broadcast_to(i["conv_se_key_b"], (128, HW)),
        "se_w1": i["conv_se_att_w1"].T.reshape(2, HW, HW).transpose(1, 0, 2), "se_bn": i["conv_se_att_bn"].T,
        "se_w2": se_w2, "sa_w1": sa_w1, "sa_bn": halves(i["conv_sa_att_bn"].T), "sa_w2": sa_w2,
        "sa_b2": np.repeat(i["conv_sa_att_b2"], 8).reshape(HALVES, 128).T,
        "alpha": np.broadcast_to(i["conv_alpha"], (128, 1)),
        "router": halves(i["ffn_Wr"].T), "router_bias": np.broadcast_to(i["ffn_br"], (128, EXPERTS)),
        "lower": lower,
        "ffn_w1": i["ffn_W1"].reshape(EXPERTS, 2, 128, HID),
        "ffn_b1": i["ffn_b1"].reshape(EXPERTS, KB, 128).transpose(2, 0, 1),
        "ffn_w2": i["ffn_W2"].reshape(EXPERTS, 2, 2, 128, C).transpose(0, 1, 3, 2, 4).reshape(EXPERTS, 2, 128, 2 * C),
        "ffn_b2": i["ffn_b2"],
    }
    nc = bacc.Bacc("TRN2", target_bir_lowering=False, num_devices=1)
    feeds, args = {}, []
    for name, a in arrays.items():
        a = np.ascontiguousarray(a)
        feeds[f"in_{name}"] = a
        args.append(nc.dram_tensor(f"in_{name}", a.shape, mb.dt.from_np(a.dtype), kind="ExternalInput").ap())
    args.append(nc.dram_tensor("out_0", (BS, C * HW), mb.dt.float32, kind="ExternalOutput").ap())
    metaformer_kernel(nc, *args)
    r = run_bass_kernel_spmd(nc, [feeds], core_ids=[0])
    return r.results[0]["out_0"].reshape(BS, C, H, W)
```

```python
import concourse.bass as bass
from concourse import mybir
from contextlib import ExitStack

BS, C, H, W = 128, 256, 9, 9
HW = H * W
HALVES = C // 128
D = 9
EXPERTS, HID = 8, 512
BN_EPS, LN_C_EPS, LN_T_EPS = 1e-5, 1e-6, 1e-5
G = 4
GROUPS = BS // G
TOK = G * HW
SUB = TOK // 3
KB = HID // 128
QUAD = 4
CHUNK = 32
WSCALE = 64.0
SLOTS = 256
REGION = BS * HW + SLOTS
TILES = -(-(2 * BS * HW + EXPERTS * (SLOTS - 1)) // (2 * SLOTS)) * 2
BAND0, BAND1 = 132, 160
ZLEN = 264
BAND1_START = 96

CREDIT = 2
CREDITED = """k1_c phase_b k1_ev v_c ks_c pt_c e_c x1_c fin_c gel_c cv_p mb_p tr_c st_v0 st_v1 lg_p raw_p
              w2_p xft_c lgr_c rl_p sent0 sent1 yst0 yst1 yo_c back_p""".split()


def metaformer_kernel(nc, x, taps, tap_bn, tap_rows, toeplitz_mask, ident, band_masks, rot_masks, zstrings,
                      key_bias, se_w1, se_bn, se_w2, sa_w1, sa_bn, sa_w2, sa_b2, alpha, router, router_bias,
                      lower, before, region_start, turn, ffn_w1, ffn_b1, ffn_w2, ffn_b2, out):
    fp32, fp16 = mybir.dt.float32, mybir.dt.float16
    ALU, ACT, AX = mybir.AluOpType, mybir.ActivationFunctionType, mybir.AxisListType

    ctx = ExitStack()
    with ctx:
        def sb(name, shape, dt=fp32):
            return ctx.enter_context(nc.sbuf_tensor(name, shape, dt))

        def sem(name):
            return ctx.enter_context(nc.semaphore(name))

        def dram(name, shape):
            return nc.dram_tensor(name, shape, fp32, kind="Internal").ap()

        xn_d, k1_d, v_d, ks_d, r_d = (dram(n, [BS, C * HW]) for n in ("xn_d", "k1_d", "v_d", "ks_d", "r_d"))

        rows_d = dram("rows_d", [EXPERTS * REGION + SLOTS, C])
        y_d = dram("y_d", [TILES * SLOTS, C])
        u_d = dram("u_d", [HW, 128, 136])

        ident_s = sb("ident_s", [128, 128])
        band_s = sb("band_s", [128, BAND0 + BAND1])
        rot_s = sb("rot_s", [128, 8])
        alpha_s = sb("alpha_s", [128, 2])
        se_w1_s = sb("se_w1_s", [HW, 2, HW])
        se_w2_s = sb("se_w2_s", [HW + 1, D])
        se_bn_s = sb("se_bn_s", [HW, 4])
        se_ab = sb("se_ab", [HW, 3])
        sa_w1_s = sb("sa_w1_s", [128, HALVES, 2, 128])
        sa_w2_s = sb("sa_w2_s", [128, HALVES, 128])
        sa_bn_s = sb("sa_bn_s", [128, HALVES, 4])
        sa_ab = sb("sa_ab", [128, HALVES, 3])
        sa_b2_s = sb("sa_b2_s", [128, HALVES])
        router_s = sb("router_s", [128, HALVES, EXPERTS])
        router_bias_s = sb("router_bias_s", [128, EXPERTS])
        lower_s = sb("lower_s", [128, EXPERTS * EXPERTS])
        b1_s = sb("b1_s", [128, EXPERTS * KB])
        before_s = sb("before_s", [128, 128])
        ones_s = sb("ones_s", [128, 128])
        region_s = sb("region_s", [128, EXPERTS])
        turn_s = sb("turn_s", [1, TILES])
        big = sb("big", [128, C * HW])
        pool_ = sb("pool_", [128, C * HW])

        cursor = [0]

        def take(parts, *dims):
            n = 1
            for d in dims:
                n *= d
            a = pool_[0:parts, cursor[0]:cursor[0] + n]
            cursor[0] += n
            assert cursor[0] <= C * HW
            names = "abcde"[:len(dims)]
            if len(dims) > 1:
                a = a.rearrange(f"p ({' '.join(names)}) -> p {' '.join(names)}",
                                **{m: d for m, d in zip(names, dims)})
            return a

        aux = sb("aux", [128, 4608])
        aux_at = [0]

        def take_aux(parts, *dims, dt=fp32):
            n = 1
            for d in dims:
                n *= d
            words = n if dt != fp16 else n // 2
            a = aux[0:parts, aux_at[0]:aux_at[0] + words]
            aux_at[0] += words
            assert aux_at[0] <= 4608
            a = a if dt == fp32 else a.bitcast(dt)
            names = "abcde"[:len(dims)]
            if len(dims) > 1:
                a = a.rearrange(f"p ({' '.join(names)}) -> p {' '.join(names)}",
                                **{m: d for m, d in zip(names, dims)})
            return a

        stats = take_aux(128, 4, HW)
        u_s = take_aux(128, 3, 136)
        xp_s = take_aux(128, 3, C)
        xt_s = take_aux(128, 3, C)
        kb_s = take_aux(128, HW)

        ps = ctx.enter_context(nc.psum_tensor("ps", [128, 8, 512], fp32))

        cursor[0] = 0
        mask_s = take(11, HW, HW + 1)
        m_s = take(HW + 1, CHUNK, 2, HW)
        taps_s = take(11, 2, C)
        tapc_s = take(11, 2, CHUNK)
        tapbn_s = take(11, 2, C)
        taprow_s = take(11, 2)
        xq_s = take(128, 2, QUAD, HW)
        xr_s = take(128, 2, QUAD, HW)
        kr_s = take(128, 2, QUAD, HW)
        pt_s = take(HW + 1, 2, QUAD, BS)
        v_s = take(128, 2, QUAD, HW)
        ks_s = take(128, 2, QUAD, HW)
        r_s = take(128, 2, QUAD, HW)
        cursor[0] = 0
        kq_s = take(HW, 2, 2, G, C)
        xc_s, vc_s, kc_s, rc_s = (take(128, 2, HALVES, G, HW) for _ in range(4))
        a_s = take(HW + 1, G, C)
        lg_s = take(128, G * 2, D)
        st_s = take(128, 4, G * 2)
        ap_s = take(128, G * 2, 15)
        t1_s = take(128, G * 2, 32)
        ar_s = take(128, G * 2, 16)
        arx_s = take(128, G * 2, 128)
        a0_s = take(128, G, BAND0)
        a1_s = take(128, G, BAND1)
        a2_s = take(128, HALVES, TOK)
        e_s = take(128, HALVES, G, HW)
        sm_s = take(128, 4, HALVES * G)
        cursor[0] = 0
        w1_s = take(128, EXPERTS * 2 * HID).bitcast(fp16).rearrange("p (s n) -> p s n", s=2)
        w2_s = take(128, EXPERTS * KB * C).bitcast(fp16).rearrange("p (s n) -> p s n", s=2)
        b2_s = take(128, EXPERTS * C)
        rin_s = take(128, 2, 2, C)
        yo_s = take(128, 2, 2, C)
        stage_s = rin_s.rearrange("p a b c -> p a (b c)")
        i32, u32 = mybir.dt.int32, mybir.dt.uint32
        pos_s = sb("pos_s", [SUB, GROUPS * 6])
        wt_s = sb("wt_s", [SUB, GROUPS * 6])
        idx_s = sb("idx_s", [SUB, 2, 6], u32)
        base_s = sb("base_s", [SUB, EXPERTS])
        til_s = sb("til_s", [SUB, 4, EXPERTS])
        tili_s = sb("tili_s", [SUB, 2, EXPERTS], i32)
        tabi_s = sb("tabi_s", [1, 2, TILES], i32)
        aux_at[0] = 0
        xf_s = take_aux(SUB, 2, 3, C)
        xs_s = take_aux(128, HALVES, TOK)
        bs_s = take_aux(SUB, 3, 10)
        pr_s = take_aux(SUB, 3, 4, EXPERTS)
        cmp_s = take_aux(SUB, 2, 3, EXPERTS * EXPERTS)
        hot_s = take_aux(SUB, 3, 3, EXPERTS)
        tot_s = take_aux(SUB, EXPERTS)
        at_s = take_aux(SUB, 3, EXPERTS)
        pick_s = take_aux(SUB, 4, 3, EXPERTS)
        aux_at[0] = 0
        tab_s = take_aux(1, 4, TILES)
        tcmp_s = take_aux(1, 2, TILES, EXPERTS)
        zero_s = take_aux(128, 2, C)
        step_s = take_aux(SUB, 2, GROUPS * 6)
        aux_at[0] = 0
        xh_s = take_aux(128, 2, 2, HALVES * SLOTS, dt=fp16)
        hf_s = take_aux(128, KB * SLOTS)
        hh_s = take_aux(128, 2, 2, KB, SLOTS, dt=fp16)
        aux_at[0] = 0
        got_s = take_aux(SUB, 2, 6, C)
        mix_s = take_aux(SUB, 3, C)

        names = """tapc_c settle_g settle_v settle_p var_c root_c win_out w_in x_in norm xn_out k1_out u_in xp_c
                   tr_c xt_c k1_c k1_ev tab_in tab_c xq_in0 xq_in1 rk_in0 rk_in1 mb_p mb_e0 mb_e1 tq_p pt_c cv_p
                   v_c ks_c r1_c r_c st_v0 st_v1 ch_d ch_g kq_in0 kq_in1 c_in0 c_in1 se1_p a_c lg_p lgs_c ex_c ar_c
                   arx_c raw_p msk_c sa1_p a2_c l2_p l2m_c e_c band_p x1_c sq_p phase_a phase_b wst_in0 wst_in1
                   whi_c wlo_c b2_in ones_v rm_p rw_c xs_c t1_p rl_p lgr_c var2_c ln_c rstd_c nmr_c probs_c ex2_c
                   tot_c tri_p xft_c idx_c sent0 sent1 scat0 scat1 base_c pad_out tab_r rin0 rin1 tt_p xhi_c xlo_c h_p gel_c
                   hhi_c hlo_c w2_p yo_c yst0 yst1 idx2_c gat0 gat1 mx0_c mix_c back_p fin_c out_s""".split()
        S = {n: sem(n) for n in names}

        def by_pixel(buf):
            return buf[:, :].rearrange("b (c p) -> b p c", p=HW)

        def by_channel(buf):
            return buf[:, :].rearrange("b (c p) -> b c p", p=HW)

        chan = 8
        W_IN = 16 * 19
        block = ctx.enter_context(nc.Block())

        @block.sync
        def _(sp):
            sp.dma_start(big[:, :], x).then_inc(S["x_in"], 16)
            n = 0
            for dst, src in ((ident_s[:, :], ident), (band_s[:, :], band_masks), (rot_s[:, :], rot_masks),
                             (alpha_s[:, 0:1], alpha), (se_w1_s[:, :, :], se_w1), (se_w2_s[:, :], se_w2),
                             (se_bn_s[:, :], se_bn), (sa_w1_s[:, :, :, :], sa_w1), (sa_w2_s[:, :, :], sa_w2),
                             (sa_bn_s[:, :, :], sa_bn), (sa_b2_s[:, :], sa_b2), (router_s[:, :, :], router),
                             (router_bias_s[:, :], router_bias), (lower_s[:, :], lower), (b1_s[:, :], ffn_b1),
                             (before_s[:, :], before),
                             (region_s[:, :], region_start), (turn_s[:, :], turn), (kb_s[:, :], key_bias)):
                sp.dma_start(dst, src).then_inc(S["w_in"], 16)
                n += 1
            assert 16 * n == W_IN
            sp.wait_ge(S["norm"], 1)
            sp.dma_start(xn_d, big[:, :]).then_inc(S["xn_out"], 16)
            window = bass.AP(zstrings.tensor, 127, [[ZLEN, HW], [-1, 128], [1, 136]])
            sp.dma_start(u_d, window).then_inc(S["win_out"], 16)
            sp.wait_ge(S["win_out"], 16)
            with sp.Fori(0, HW // 3) as i:
                sp.wait_ge(S["k1_c"], i + CREDIT)
                src = u_d[bass.ds(i * 3, 3), :, :].rearrange("t c j -> c t j")
                sp.dma_start(u_s[:, :, :], src).then_inc(S["u_in"], 16)
            sp.wait_ge(S["k1_ev"], HW // 3 + CREDIT)
            sp.dma_start(k1_d, pool_[:, :]).then_inc(S["k1_out"], 16)
            sp.wait_ge(S["k1_out"], 16)
            sp.wait_ge(S["xn_out"], 16)
            for dst, src in ((mask_s, toeplitz_mask), (taps_s, taps), (tapbn_s, tap_bn), (taprow_s, tap_rows)):
                sp.dma_start(dst, src).then_inc(S["tab_in"], 16)
            def load_quad(q, par):
                cols = bass.ds(q * (QUAD * HW), QUAD * HW)
                sp.wait_ge(S["sq_p"], q)
                sp.dma_start(xq_s[:, par], xn_d[:, cols].rearrange("b (c p) -> b c p", p=HW)).then_inc(S[f"xq_in{par}"], 16)
                sp.dma_start(xr_s[:, par], x[:, cols].rearrange("b (c p) -> b c p", p=HW)).then_inc(S[f"rk_in{par}"], 16)
                sp.dma_start(kr_s[:, par], k1_d[:, cols].rearrange("b (c p) -> b c p", p=HW)).then_inc(S[f"rk_in{par}"], 16)

            def store_quad(q, par):
                cols = bass.ds(q * (QUAD * HW), QUAD * HW)
                for dst, src, made in ((v_d, v_s, "v_c"), (ks_d, ks_s, "ks_c"), (r_d, r_s, "r_c")):
                    sp.wait_ge(S[made], q + 1 + (0 if made == "r_c" else CREDIT))
                    sp.dma_start(dst[:, cols].rearrange("b (c p) -> b c p", p=HW),
                                 src[:, par]).then_inc(S[f"st_v{par}"], 16)

            load_quad(0, 0)
            with sp.Fori(0, C // QUAD // 2 - 1) as i:
                for par in range(2):
                    load_quad(i * 2 + par + 1, 1 - par)
                    store_quad(i * 2 + par, par)
            last_quad = C // QUAD - 1
            load_quad(last_quad, 1)
            store_quad(last_quad - 1, 0)
            store_quad(last_quad, 1)
            for par in range(2):
                sp.wait_ge(S[f"st_v{par}"], 48 * (C // QUAD // 2) + CREDIT)
            with sp.Fori(0, GROUPS // 2) as i:
                for par in range(2):
                    g = i * 2 + par
                    sp.wait_ge(S["phase_b"], g + CREDIT)
                    rows = bass.ds(g * G, G)
                    for k, src in enumerate((xn_d, k1_d)):
                        sp.dma_start(kq_s[:, par, k],
                                     src[rows, :].rearrange("b (i j) -> i b j", j=C)).then_inc(S[f"kq_in{par}"], 16)
                    for dst, src in ((xc_s, xn_d), (vc_s, v_d), (kc_s, ks_d), (rc_s, r_d)):
                        for h in range(HALVES):
                            sp.dma_start(dst[:, par, h],
                                         src[rows, h * 128 * HW:(h + 1) * 128 * HW]
                                         .rearrange("b (c p) -> c b p", p=HW)).then_inc(S[f"c_in{par}"], 16)
            sp.wait_ge(S["x1_c"], GROUPS + CREDIT)
            sp.dma_start(b2_s, bass.AP(ffn_b2.tensor, 0, [[0, 128], [1, EXPERTS * C]])).then_inc(S["b2_in"], 16)
            for n in range(EXPERTS * 4):
                e, second, k = n // 4, (n // 2) % 2, n % 2
                if n >= 2:
                    sp.wait_ge(S["wlo_c"], n - 1)
                sp.dma_start(stage_s[:, n % 2], (ffn_w2 if second else ffn_w1)[e, k]).then_inc(S[f"wst_in{n % 2}"], 16)
            sp.wait_ge(S["base_c"], 1)
            for e in range(EXPERTS):
                first_free = sp.value_load(tili_s[0:1, 1, e:e + 1], min_val=e * REGION,
                                           max_val=(e + 1) * REGION - SLOTS)
                sp.dma_start(rows_d[bass.ds(first_free, SLOTS), :].rearrange("(s q) c -> q s c", q=128),
                             zero_s[:, :, :]).then_inc(S["pad_out"], 16)
            sp.dma_start(rows_d[EXPERTS * REGION:, :].rearrange("(s q) c -> q s c", q=128),
                         zero_s[:, :, :]).then_inc(S["pad_out"], 16)
            sp.wait_ge(S["pad_out"], 16 * (EXPERTS + 1))
            sp.wait_ge(S["scat0"], 96 * (GROUPS // 2))
            sp.wait_ge(S["scat1"], 96 * (GROUPS // 2))
            sp.wait_ge(S["wlo_c"], EXPERTS * 4)

            def load_rows(t, par):
                row = sp.value_load(tabi_s[0:1, 0, bass.ds(t, 1)], min_val=0, max_val=EXPERTS * REGION)
                sp.dma_start(rin_s[:, par], rows_d[bass.ds(row, SLOTS), :]
                             .rearrange("(s q) c -> q s c", q=128)).then_inc(S[f"rin{par}"], 16)

            def store_rows(t, par):
                sp.dma_start(y_d[bass.ds(t * SLOTS, SLOTS), :].rearrange("(s q) c -> q s c", q=128),
                             yo_s[:, par]).then_inc(S[f"yst{par}"], 16)

            load_rows(0, 0)
            load_rows(1, 1)
            for t in range(2):
                sp.wait_ge(S["tt_p"], t + 1)
                load_rows(t + 2, t)
            with sp.Fori(1, TILES // 2 - 1) as i:
                for par in range(2):
                    t = i * 2 + par
                    sp.wait_ge(S["tt_p"], t + 1)
                    load_rows(t + 2, par)
                    sp.wait_ge(S["yo_c"], t - 1 + CREDIT)
                    store_rows(t - 2, par)
            for t in range(TILES - 4, TILES):
                sp.wait_ge(S["yo_c"], t + 1 + CREDIT)
                store_rows(t, t % 2)
            with sp.Fori(0, GROUPS) as g:
                sp.wait_ge(S["fin_c"], g + 1 + CREDIT)
                for h in range(HALVES):
                    sp.dma_start(out[bass.ds(g * G, G), h * 128 * HW:(h + 1) * 128 * HW]
                                 .rearrange("b (c p) -> c b p", p=HW),
                                 big[:, bass.ds(g * (HALVES * TOK) + h * TOK, TOK)]
                                 .rearrange("c (b p) -> c b p", p=HW)).then_inc(S["out_s"], 16)
            sp.wait_ge(S["out_s"], 16 * HALVES * GROUPS)

        @block.tensor
        def _(pe):
            pe.wait_ge(S["w_in"], W_IN)
            pb = 2
            with pe.Fori(0, HW // 3) as i:
                pe.wait_ge(S["xp_c"], i + 1)
                for k in range(3):
                    for h in range(HALVES):
                        last = nc.tensor.transpose(ps[:, k, h * 128:(h + 1) * 128],
                                                   xp_s[:, k, h * 128:(h + 1) * 128], ident_s[:, :])
                last.then_inc(S["tr_c"], 1)
                pe.wait_ge(S["u_in"], 16 * (i + 1))
                pe.wait_ge(S["xt_c"], i + 1)
                pe.wait_ge(S["k1_ev"], i + CREDIT)
                for k in range(3):
                    nc.tensor.matmul(ps[:, 3 + k, 0:132], xt_s[:, k, 0:128], u_s[:, k, 4:136],
                                     start=True, stop=False, skip_group_check=True)
                    last = nc.tensor.matmul(ps[:, 3 + k, 124:256], xt_s[:, k, 128:256], u_s[:, k, 0:132],
                                            start=False, stop=True, skip_group_check=True)
                last.then_inc(S["k1_c"], 1)
            pe.wait_ge(S["tab_c"], 1)
            with pe.Fori(0, C // CHUNK) as i:
                pe.wait_ge(S["v_c"], i * 8 + CREDIT)
                pe.wait_ge(S["ks_c"], i * 8 + CREDIT)
                pe.wait_ge(S["tapc_c"], i + 1)
                for n in range(9):
                    if n >= 2:
                        pe.wait_ge(S[f"mb_e{n % 2}"], i * (5 - n % 2) + n // 2)
                    b0 = 2 * (n % 2)
                    flat = ps[0:HW + 1, b0:b0 + 2, :].rearrange("p b n -> p (b n)")
                    for m in range(9):
                        last = nc.tensor.matmul(flat[:, m * 2 * CHUNK:(m + 1) * 2 * CHUNK].rearrange("p (v c) -> p v c", v=2),
                                                mask_s[:, n * 9 + m, :],
                                                tapc_s[:, :, :],
                                                start=True, stop=True)
                    last.then_inc(S["mb_p"], 1)
                for q in range(8):
                    par = q % 2
                    pe.wait_ge(S[f"xq_in{par}"], 16 * (i * 4 + q // 2 + 1))
                    pe.wait_ge(S["pt_c"], i * 8 + max(q - 1, 0) + CREDIT)
                    for c in range(QUAD):
                        last = nc.tensor.transpose(ps[0:HW, 4 + par, c * BS:(c + 1) * BS], xq_s[:, par, c, :],
                                                   ident_s[:, :])
                    last.then_inc(S["tq_p"], 1)
                    if q == 0:
                        pe.wait_ge(S["mb_e0"], i * 5 + 5)
                        pe.wait_ge(S["mb_e1"], i * 4 + 4)
                    pe.wait_ge(S["pt_c"], i * 8 + q + 1 + CREDIT)
                    if q >= 2:
                        pe.wait_ge(S["v_c"], i * 8 + q - 1 + CREDIT)
                        pe.wait_ge(S["ks_c"], i * 8 + q - 1 + CREDIT)
                    b0 = 6 if par == 0 else 2
                    for c in range(QUAD):
                        o = ps[:, b0 + c // 2, (c % 2) * 2 * HW:(c % 2 + 1) * 2 * HW]
                        last = nc.tensor.matmul(o, pt_s[:, par, c, :], m_s[:, q * QUAD + c, :, :]
                                                .rearrange("p v n -> p (v n)"), start=True, stop=True)
                    last.then_inc(S["cv_p"], 1)
            pe.wait_ge(S["phase_a"], 1)
            with pe.Fori(0, GROUPS // 2) as i:
                for par in range(2):
                    g = i * 2 + par
                    pe.wait_ge(S[f"kq_in{par}"], 32 * (i + 1))
                    for n in range(2):
                        for k in range(2):
                            last = nc.tensor.matmul(ps[0:HW, n, :], se_w1_s[:, k, :],
                                                    kq_s[:, par, k, 2 * n:2 * n + 2, :].rearrange("p b j -> p (b j)"),
                                                    start=k == 0, stop=k == 1)
                        last.then_inc(S["se1_p"], 1)
                    pe.wait_ge(S[f"c_in{par}"], 128 * (i + 1))
                    pe.wait_ge(S["e_c"], g + CREDIT)
                    for h in range(HALVES):
                        nc.tensor.matmul(ps[:, 2 + h, 0:TOK], sa_w1_s[:, h, 0, :],
                                         kc_s[:, par, h, :, :].rearrange("p b n -> p (b n)"), start=True, stop=False)
                        nc.tensor.matmul(ps[:, 2 + h, 0:TOK], sa_w1_s[:, h, 1, :],
                                         xc_s[:, par, h, :, :].rearrange("p b n -> p (b n)"),
                                         start=False, stop=True).then_inc(S["sa1_p"], 1)
                    for n in range(2):
                        pe.wait_ge(S["a_c"], g * 2 + n + 1)
                        for b in range(2 * n, 2 * n + 2):
                            for h in range(HALVES):
                                j = b * 2 + h
                                last = nc.tensor.matmul(ps[:, 4, j * D:(j + 1) * D],
                                                        a_s[:, b, h * 128:(h + 1) * 128], se_w2_s[:, :],
                                                        start=True, stop=True)
                    last.then_inc(S["lg_p"], 1)
                    for h in range(HALVES):
                        pe.wait_ge(S["a2_c"], g * 2 + h + 1)
                        nc.tensor.matmul(ps[:, 2 + h, 0:TOK], sa_w2_s[:, h, :], a2_s[:, h, :],
                                         start=True, stop=True).then_inc(S["l2_p"], 1)
                    pe.wait_ge(S["arx_c"], g + 1)
                    for n in range(2):
                        for b in range(2):
                            for h in range(HALVES):
                                last = nc.tensor.matmul(ps[:, 5 - n, b * C + h * 128:b * C + (h + 1) * 128],
                                                        arx_s[:, (2 * n + b) * 2 + h, :], ident_s[:, :],
                                                        start=True, stop=True)
                        last.then_inc(S["raw_p"], 1)
                    pe.wait_ge(S["msk_c"], 2 * (g + 1))
                    pe.wait_ge(S["x1_c"], g + CREDIT)
                    for b in range(G):
                        v0, v1 = vc_s[:, par, 0, b, :], vc_s[:, par, 1, b, :]
                        o = slice(b * HW, (b + 1) * HW)
                        nc.tensor.matmul(ps[:, 6, o], a0_s[:, b, 0:128], v0, start=True, stop=False,
                                         skip_group_check=True)
                        nc.tensor.matmul(ps[96:128, 6, o], a1_s[:, b, 0:32], v1, start=False, stop=True,
                                         skip_group_check=True)
                        nc.tensor.matmul(ps[:, 7, o], a1_s[:, b, 32:160], v1, start=True, stop=False,
                                         skip_group_check=True)
                        last = nc.tensor.matmul(ps[0:4, 7, o], a0_s[:, b, 128:132], v0, start=False, stop=True,
                                                skip_group_check=True)
                    last.then_inc(S["band_p"], 1)
            pe.wait_ge(S["ones_v"], 1)
            for h in range(HALVES):
                last = nc.tensor.matmul(ps[:, 2, 0:EXPERTS], ones_s[:, :], router_s[:, h, :], start=h == 0, stop=h == 1)
            last.then_inc(S["rm_p"], 1)
            pe.wait_ge(S["rw_c"], 1)
            with pe.Fori(0, GROUPS // 2) as i:
                for par in range(2):
                    g = i * 2 + par
                    b0 = 4 * par
                    pe.wait_ge(S["xs_c"], g + 1)
                    pe.wait_ge(S["xft_c"], g - 1 + CREDIT)
                    for s in range(3):
                        for h in range(HALVES):
                            last = nc.tensor.transpose(
                                ps[0:SUB, b0 + s // 2, (s % 2) * C + h * 128:(s % 2) * C + (h + 1) * 128],
                                xs_s[:, h, s * SUB:(s + 1) * SUB], ident_s[:, :])
                    last.then_inc(S["t1_p"], 1)
                    pe.wait_ge(S["lgr_c"], g + CREDIT)
                    for s in range(3):
                        for h in range(HALVES):
                            last = nc.tensor.matmul(ps[0:SUB, 2, s * EXPERTS:(s + 1) * EXPERTS],
                                                    xs_s[:, h, s * SUB:(s + 1) * SUB], router_s[:, h, :],
                                                    start=h == 0, stop=h == 1)
                    last.then_inc(S["rl_p"], 1)
                    pe.wait_ge(S["tot_c"], g + 1)
                    nc.tensor.matmul(ps[0:SUB, 3, 0:EXPERTS], before_s[0:SUB, 0:SUB], tot_s[:, :], start=True, stop=True)
                    nc.tensor.matmul(ps[0:SUB, 3, EXPERTS:2 * EXPERTS], ones_s[0:SUB, 0:SUB], tot_s[:, :],
                                     start=True, stop=True).then_inc(S["tri_p"], 1)

            def turn_rows(t, par, come, first=False):
                pe.wait_ge(S[f"rin{par}"], 16 * come)
                if not first:
                    pe.wait_ge(S["xlo_c"], t - 1)
                for h in range(HALVES):
                    for s in range(2):
                        last = nc.tensor.transpose(ps[:, par, h * SLOTS + s * 128:h * SLOTS + (s + 1) * 128],
                                                   rin_s[:, par, s, h * 128:(h + 1) * 128], ident_s[:, :])
                last.then_inc(S["tt_p"], 1)

            def up(t, par, first=False):
                e = pe.value_load(tabi_s[0:1, 1, bass.ds(t, 1)], min_val=0, max_val=EXPERTS - 1)
                pe.wait_ge(S["xlo_c"], t + 1)
                if not first:
                    pe.wait_ge(S["gel_c"], 4 * (t - 1) + CREDIT)
                pe.sem_inc(S["settle_p"], 1)
                for j in range(KB):
                    o = ps[:, 2 + 2 * par + j // 2, (j % 2) * SLOTS:(j % 2 + 1) * SLOTS]
                    n = 0
                    for k in range(HALVES):
                        for a, b in ((0, 0), (0, 1), (1, 0)):
                            last = nc.tensor.matmul(o, w1_s[:, a, bass.ds(e * (2 * HID) + (k * HID + j * 128), 128)],
                                                    xh_s[:, par, b, k * SLOTS:(k + 1) * SLOTS],
                                                    start=n == 0, stop=n == 5)
                            n += 1
                    last.then_inc(S["h_p"], 1)

            def down(t, par):
                e = pe.value_load(tabi_s[0:1, 1, bass.ds(t, 1)], min_val=0, max_val=EXPERTS - 1)
                pe.wait_ge(S["hlo_c"], t + 1)
                pe.wait_ge(S["yo_c"], t - 1 + CREDIT)
                for s in range(2):
                    n = 0
                    for j in range(KB):
                        for a, b in ((0, 0), (0, 1), (1, 0)):
                            last = nc.tensor.matmul(ps[:, 6 + par, s * C:(s + 1) * C],
                                                    hh_s[:, par, a, j, s * 128:(s + 1) * 128],
                                                    w2_s[:, b, bass.ds(e * (KB * C) + j * C, C)],
                                                    start=n == 0, stop=n == 11)
                            n += 1
                last.then_inc(S["w2_p"], 1)

            pe.wait_ge(S["tab_r"], 1)
            pe.wait_ge(S["wlo_c"], EXPERTS * 4)
            turn_rows(0, 0, 1, first=True)
            turn_rows(1, 1, 1, first=True)
            up(0, 0, first=True)
            with pe.Fori(0, TILES // 2 - 1) as i:
                for k in range(2):
                    t = i * 2 + 1 + k
                    turn_rows(t + 1, k, i + 2)
                    up(t, 1 - k)
                    down(t - 1, k)
            up(TILES - 1, 1)
            down(TILES - 2, 0)
            down(TILES - 1, 1)
            with pe.Fori(0, GROUPS) as g:
                pe.wait_ge(S["mix_c"], g + 1)
                pe.wait_ge(S["fin_c"], g + CREDIT)
                for h in range(HALVES):
                    for s in range(3):
                        last = nc.tensor.transpose(ps[:, h, s * SUB:(s + 1) * SUB], mix_s[:, s, h * 128:(h + 1) * 128],
                                                   ident_s[0:SUB, 0:SUB])
                last.then_inc(S["back_p"], 1)

        @block.vector
        def _(dve):
            done = {"before": 0, "links": 0, "roots": 0}

            def link(ins):
                done["links"] += 1
                ins.then_inc(S["ch_d"], 1)
                dve.wait_ge(S["ch_d"], done["before"] + done["links"])


            def inverse_root(var, eps, scale, dst):
                nc.vector.tensor_scalar(dst, var, scale, eps, ALU.mult, ALU.add).then_inc(S["var_c"], 1)
                done["roots"] += 1
                dve.wait_ge(S["root_c"], done["roots"])
                link(nc.vector.reciprocal(dst, dst))

            dve.wait_ge(S["w_in"], W_IN)
            for p, ab in ((se_bn_s[:, :].unsqueeze(1), se_ab[:, :].unsqueeze(1)), (sa_bn_s, sa_ab)):
                gg, bb, mm, vv = (p[:, :, k:k + 1] for k in range(4))
                inverse_root(vv, BN_EPS, 1.0, ab[:, :, 0:1])
                link(nc.vector.tensor_tensor(ab[:, :, 0:1], ab[:, :, 0:1], gg, ALU.mult))
                link(nc.vector.tensor_tensor(ab[:, :, 2:3], ab[:, :, 0:1], mm, ALU.mult))
                link(nc.vector.tensor_tensor(ab[:, :, 1:2], bb, ab[:, :, 2:3], ALU.subtract))
            link(nc.vector.tensor_scalar(alpha_s[:, 1:2], alpha_s[:, 0:1], -1.0, 1.0, ALU.mult, ALU.add))
            dve.wait_ge(S["x_in"], 16)
            link(nc.vector.reduce_sum(stats[:, 0, :], by_pixel(big), axis=AX.X))
            link(nc.vector.tensor_scalar(stats[:, 0, :], stats[:, 0, :], 1.0 / C, None, ALU.mult))
            link(nc.vector.tensor_tensor(by_channel(big), by_channel(big),
                                         stats[:, 0, :].unsqueeze(1).to_broadcast([128, C, HW]), ALU.subtract))
            link(nc.vector.tensor_tensor(by_channel(pool_), by_channel(big), by_channel(big), ALU.mult))
            link(nc.vector.reduce_sum(stats[:, 1, :], by_pixel(pool_), axis=AX.X))
            inverse_root(stats[:, 1, :], LN_C_EPS, 1.0 / C, stats[:, 1, :])
            nc.vector.tensor_tensor(by_channel(big), by_channel(big),
                                    stats[:, 1, :].unsqueeze(1).to_broadcast([128, C, HW]),
                                    ALU.mult).then_inc(S["norm"], 1)
            with dve.Fori(0, HW // 3) as i:
                dve.wait_ge(S["k1_c"], i + 1 + CREDIT)
                nc.vector.tensor_tensor(by_pixel(pool_)[:, bass.ds(i * 3, 3), :], ps[:, 3:6, 0:C],
                                        kb_s[:, bass.ds(i * 3, 3)].unsqueeze(2).to_broadcast([128, 3, C]),
                                        ALU.add).then_inc(S["k1_ev"], 1)
            dve.wait_ge(S["tab_in"], 64)
            inverse_root(tapbn_s[:, 1, :], BN_EPS, 1.0, tapbn_s[:, 1, :])
            link(nc.vector.tensor_tensor(tapbn_s[:, 0, :], tapbn_s[:, 0, :], tapbn_s[:, 1, :], ALU.mult))
            link(nc.vector.tensor_scalar(tapbn_s[:, 0, :], tapbn_s[:, 0, :], taprow_s[:, 0:1], taprow_s[:, 1:2],
                                         ALU.mult, ALU.add))
            link(nc.vector.tensor_tensor(taps_s[:, 1, :], taps_s[:, 1, :], tapbn_s[:, 0, :], ALU.mult))
            nc.vector.memset(pt_s[:, :, :, :], 1.0).then_inc(S["tab_c"], 1)
            with dve.Fori(0, C // CHUNK) as i:
                dve.wait_ge(S["mb_p"], i * 9 + CREDIT)
                nc.vector.tensor_copy(tapc_s[:, :, :], taps_s[:, :, bass.ds(i * CHUNK, CHUNK)]).then_inc(S["tapc_c"], 1)
                for n in range(1, 9, 2):
                    dve.wait_ge(S["mb_p"], i * 9 + n + 1 + CREDIT)
                    if n == 1:
                        dve.wait_ge(S["cv_p"], i * 8 + CREDIT)
                    flat = ps[0:HW + 1, 2:4, :].rearrange("p b n -> p (b n)")[:, 0:9 * 2 * CHUNK]
                    nc.vector.tensor_copy(m_s[:, :, :, n * 9:(n + 1) * 9].rearrange("p c v m -> p m v c"),
                                          flat.rearrange("p (m v c) -> p m v c", m=9, v=2)).then_inc(S["mb_e1"], 1)
                for q in range(8):
                    par = q % 2
                    dve.wait_ge(S["tq_p"], i * 8 + q + 1)
                    if q >= 2:
                        dve.wait_ge(S["cv_p"], i * 8 + q - 1 + CREDIT)
                    nc.vector.tensor_copy(pt_s[0:HW, par, :, :].rearrange("p c b -> p (c b)"),
                                          ps[0:HW, 4 + par, :]).then_inc(S["pt_c"], 1)
                    dve.wait_ge(S["r1_c"], i * 8 + q + 1)
                    dve.wait_ge(S["ks_c"], i * 8 + q + 1 + CREDIT)
                    nc.vector.scalar_tensor_tensor(r_s[:, par], ks_s[:, par], alpha_s[:, 1:2], kr_s[:, par],
                                                   ALU.mult, ALU.add).then_inc(S["r_c"], 1)
            for par in range(2):
                dve.wait_ge(S[f"st_v{par}"], 48 * (C // QUAD // 2) + CREDIT)
            link(nc.vector.memset(a_s[:, :, :], 1.0))
            link(nc.vector.memset(ap_s[:, :, :], 0.0))
            nc.vector.memset(t1_s[:, :, :], 0.0).then_inc(S["phase_a"], 1)
            dve.wait_ge(S["phase_a"], 1)
            base = done["links"]
            per = 19
            with dve.Fori(0, GROUPS // 2) as i:
                done["before"], done["links"] = i * (2 * per) + base, 0
                for par in range(2):
                    g = i * 2 + par
                    dve.wait_ge(S["lg_p"], g + 1 + CREDIT)
                    lg = ps[:, 4, 0:G * 2 * D].rearrange("p (j d) -> p j d", d=D)
                    link(nc.vector.reduce_max(st_s[:, 0, :], lg, axis=AX.X))
                    nc.vector.tensor_tensor(lg_s[:, :, :], lg, st_s[:, 0, :].unsqueeze(2).to_broadcast([128, G * 2, D]),
                                            ALU.subtract).then_inc(S["lgs_c"], 1)
                    dve.wait_ge(S["ex_c"], g + 1)
                    link(nc.vector.reduce_sum(st_s[:, 1, :], lg_s[:, :, :], axis=AX.X))
                    link(nc.vector.reciprocal(st_s[:, 2, :], st_s[:, 1, :]))
                    link(nc.vector.tensor_scalar(st_s[:, 3, :], st_s[:, 2, :], alpha_s[:, 0:1], None, ALU.mult))
                    link(nc.vector.tensor_tensor(ap_s[:, :, 3:12], lg_s[:, :, :],
                                                 st_s[:, 3, :].unsqueeze(2).to_broadcast([128, G * 2, D]), ALU.mult))
                    for r in range(4):
                        o = t1_s[:, :, :].rearrange("p j (t n) -> p j t n", t=2)[:, :, :, 0:12]
                        a = ap_s[:, :, 3 - r:15 - r].unsqueeze(2).to_broadcast([128, G * 2, 2, 12])
                        if r == 0:
                            for t in range(2):
                                ins = nc.vector.tensor_scalar(t1_s[:, :, 16 * t:16 * t + 12], ap_s[:, :, 3:15],
                                                              rot_s[:, 0:1], None, ALU.mult)
                            link(ins)
                        else:
                            for t in range(2):
                                ins = nc.vector.scalar_tensor_tensor(
                                    t1_s[:, :, 16 * t:16 * t + 12], ap_s[:, :, 3 - r:15 - r], rot_s[:, r:r + 1],
                                    t1_s[:, :, 16 * t:16 * t + 12], ALU.mult, ALU.add)
                            link(ins)
                    for r in range(4):
                        src = t1_s[:, :, 16 - 4 * r:32 - 4 * r] if r else t1_s[:, :, 0:16]
                        if r == 0:
                            link(nc.vector.tensor_scalar(ar_s[:, :, :], src, rot_s[:, 4:5], None, ALU.mult))
                        else:
                            ins = nc.vector.scalar_tensor_tensor(ar_s[:, :, :], src, rot_s[:, 4 + r:5 + r],
                                                                 ar_s[:, :, :], ALU.mult, ALU.add)
                            if r < 3:
                                link(ins)
                            else:
                                ins.then_inc(S["ar_c"], 1)
                    for h in range(HALVES):
                        dve.wait_ge(S["l2_p"], g * 2 + h + 1)
                        ins = nc.vector.reduce_max(sm_s[:, 0, h * G:(h + 1) * G],
                                                   ps[:, 2 + h, 0:TOK].rearrange("p (b n) -> p b n", b=G), axis=AX.X)
                    link(ins)
                    bb = sa_b2_s[:, :].unsqueeze(2).to_broadcast([128, HALVES, G])
                    m3 = sm_s[:, :, :].rearrange("p k (h b) -> p k h b", h=HALVES)
                    link(nc.vector.tensor_tensor(m3[:, 1], m3[:, 0], bb, ALU.add))
                    nc.vector.tensor_tensor(m3[:, 2], bb, m3[:, 1], ALU.subtract).then_inc(S["l2m_c"], 1)
                    for n in range(2):
                        dve.wait_ge(S["raw_p"], g * 2 + n + 1 + CREDIT)
                        raw = ps[:, 5 - n, :].rearrange("p (b c) -> p b c", b=2)
                        nc.vector.tensor_tensor(a0_s[:, 2 * n:2 * n + 2, :], raw[:, :, 0:BAND0],
                                                band_s[:, 0:BAND0].unsqueeze(1).to_broadcast([128, 2, BAND0]), ALU.mult)
                        nc.vector.tensor_tensor(a1_s[:, 2 * n:2 * n + 2, :], raw[:, :, BAND1_START:C],
                                                band_s[:, BAND0:].unsqueeze(1).to_broadcast([128, 2, BAND1]),
                                                ALU.mult).then_inc(S["msk_c"], 1)
                    dve.wait_ge(S["e_c"], g + 1 + CREDIT)
                    link(nc.vector.reciprocal(sm_s[:, 0, :], sm_s[:, 3, :]))
                    link(nc.vector.tensor_scalar(sm_s[:, 1, :], sm_s[:, 0, :], alpha_s[:, 1:2], None, ALU.mult))
                    e3 = e_s[:, :, :, :].rearrange("p h b n -> p (h b) n")
                    ins = nc.vector.tensor_tensor(e3, e3, xc_s[:, par].rearrange("p h b n -> p (h b) n"), ALU.mult)
                    link(ins)
                    link(nc.vector.tensor_tensor(e3, e3, sm_s[:, 1, :].unsqueeze(2).to_broadcast([128, HALVES * G, HW]),
                                                 ALU.mult))
                    link(nc.vector.tensor_tensor(e3, e3, rc_s[:, par].rearrange("p h b n -> p (h b) n"), ALU.add))
                    dve.wait_ge(S["band_p"], g + 1)
                    nc.vector.tensor_tensor(big[:, bass.ds(g * (HALVES * TOK), HALVES * TOK)]
                                            .rearrange("p (h t) -> p h t", h=HALVES),
                                            e_s[:, :, :, :].rearrange("p h b n -> p h (b n)"), ps[:, 6:8, 0:TOK],
                                            ALU.add).then_inc(S["x1_c"], 1)
            assert done["links"] == 2 * per
            done["before"], done["links"] = base + per * GROUPS, 0
            for n in range(EXPERTS * 4):
                e, second, k = n // 4, (n // 2) % 2, n % 2
                w = w2_s if second else w1_s
                cols = slice((2 * e + k) * 512, (2 * e + k + 1) * 512)
                st = stage_s[:, n % 2]
                dve.wait_ge(S[f"wst_in{n % 2}"], 16 * (n // 2 + 1))
                nc.vector.tensor_scalar(w[:, 0, cols], st, WSCALE, None, ALU.mult).then_inc(S["whi_c"], 1)
                dve.wait_ge(S["whi_c"], n + 1)
                nc.vector.scalar_tensor_tensor(w[:, 1, cols], st, WSCALE, w[:, 0, cols],
                                               ALU.mult, ALU.subtract).then_inc(S["wlo_c"], 1)
            nc.vector.memset(ones_s[:, :], 1.0).then_inc(S["ones_v"], 1)
            dve.wait_ge(S["rm_p"], 1)
            for h in range(HALVES):
                ins = nc.vector.scalar_tensor_tensor(router_s[:, h, :], ps[:, 2, 0:EXPERTS], -1.0 / C, router_s[:, h, :],
                                                     ALU.mult, ALU.add)
            ins.then_inc(S["rw_c"], 1)
            link(nc.vector.tensor_copy(base_s[:, :], region_s[0:SUB, :]))
            E2 = EXPERTS * EXPERTS
            base = done["before"] + done["links"]
            per_r = 18
            with dve.Fori(0, GROUPS // 2) as i:
                done["before"], done["links"] = i * (2 * per_r) + base, 0
                for par in range(2):
                    g = i * 2 + par
                    b0 = 4 * par
                    dve.wait_ge(S["t1_p"], g + 1)
                    row = [ps[0:SUB, b0 + s // 2, (s % 2) * C:(s % 2 + 1) * C] for s in range(3)]
                    for s in range(3):
                        ins = nc.vector.bn_stats(bs_s[:, s, 0:6], row[s])
                    link(ins)
                    dve.sem_inc(S["settle_v"], 1)
                    for s in range(3):
                        ins = nc.vector.bn_aggr(bs_s[:, s, 6:8], bs_s[:, s, 0:6])
                    link(ins)
                    dve.wait_ge(S["xft_c"], g + CREDIT)
                    nc.vector.tensor_scalar(bs_s[:, :, 8:9], bs_s[:, :, 7:8], LN_T_EPS, None, ALU.add).then_inc(S["var2_c"], 1)
                    dve.wait_ge(S["rstd_c"], g + 1)
                    nc.vector.scalar_tensor_tensor(bs_s[:, :, 9:10], bs_s[:, :, 6:7], -1.0, bs_s[:, :, 8:9],
                                                   ALU.mult, ALU.mult).then_inc(S["nmr_c"], 1)
                    dve.wait_ge(S["rl_p"], g + 1 + CREDIT)
                    lgt = ps[0:SUB, 2, 0:3 * EXPERTS].rearrange("p (s e) -> p s e", s=3)
                    ins = nc.vector.tensor_tensor(pr_s[:, :, 0, :], lgt, bs_s[:, :, 8:9].to_broadcast([SUB, 3, EXPERTS]),
                                                  ALU.mult)
                    ins.then_inc(S["lgr_c"], 1)
                    dve.wait_ge(S["lgr_c"], g + 1 + CREDIT)
                    link(nc.vector.tensor_tensor(pr_s[:, :, 0, :], pr_s[:, :, 0, :],
                                                 router_bias_s[0:SUB, :].unsqueeze(1).to_broadcast([SUB, 3, EXPERTS]),
                                                 ALU.add))
                    m1 = bs_s[:, :, 7:8]
                    link(nc.vector.reduce_max(m1.rearrange("p s o -> p (s o)"), pr_s[:, :, 0, :], axis=AX.X))
                    nc.vector.tensor_tensor(pr_s[:, :, 1, :], pr_s[:, :, 0, :], m1.to_broadcast([SUB, 3, EXPERTS]),
                                            ALU.subtract).then_inc(S["probs_c"], 1)
                    dve.wait_ge(S["ex2_c"], g + 1)
                    link(nc.vector.reduce_sum(m1.rearrange("p s o -> p (s o)"), pr_s[:, :, 2, :], axis=AX.X))
                    link(nc.vector.reciprocal(m1, m1))
                    link(nc.vector.tensor_tensor(pr_s[:, :, 1, :], pr_s[:, :, 2, :], m1.to_broadcast([SUB, 3, EXPERTS]),
                                                 ALU.mult))
                    gt, eq = (cmp_s[:, k].rearrange("p s (e j) -> p s e j", j=EXPERTS) for k in range(2))
                    for s in range(3):
                        mine = pr_s[:, s, 1, :].unsqueeze(2).to_broadcast([SUB, EXPERTS, EXPERTS])
                        other = pr_s[:, s, 1, :].unsqueeze(1).to_broadcast([SUB, EXPERTS, EXPERTS])
                        nc.vector.tensor_tensor(gt[:, s], other, mine, ALU.is_gt)
                        ins = nc.vector.tensor_tensor(eq[:, s], other, mine, ALU.is_equal)
                    link(ins)
                    link(nc.vector.tensor_tensor(cmp_s[:, 1], cmp_s[:, 1],
                                                 lower_s[0:SUB, :].unsqueeze(1).to_broadcast([SUB, 3, E2]), ALU.mult))
                    link(nc.vector.tensor_tensor(cmp_s[:, 0], cmp_s[:, 0], cmp_s[:, 1], ALU.add))
                    link(nc.vector.tensor_reduce(pr_s[:, :, 3, :], gt, axis=AX.X, op=ALU.add))
                    nc.vector.tensor_scalar(hot_s[:, 0], pr_s[:, :, 3, :], 0.0, None, ALU.is_equal)
                    nc.vector.tensor_scalar(hot_s[:, 1], pr_s[:, :, 3, :], 1.0, None, ALU.is_equal)
                    link(nc.vector.tensor_scalar(hot_s[:, 2], pr_s[:, :, 3, :], 1.5, None, ALU.is_lt))
                    nc.vector.reduce_sum(tot_s[:, :], hot_s[:, 2].rearrange("p s e -> p e s"),
                                         axis=AX.X).then_inc(S["tot_c"], 1)
                    for k in range(2):
                        ins = nc.vector.tensor_tensor(pick_s[:, k], pr_s[:, :, 1, :], hot_s[:, k], ALU.mult)
                    link(ins)
                    for k in range(2):
                        ins = nc.vector.reduce_sum(wt_s[:, bass.ds(g * 6 + 3 * k, 3)], pick_s[:, k], axis=AX.X)
                    dve.wait_ge(S["tri_p"], g + 1)
                    link(nc.vector.tensor_tensor(at_s[:, 0], base_s[:, :], ps[0:SUB, 3, 0:EXPERTS], ALU.add))
                    nc.vector.tensor_tensor(base_s[:, :], base_s[:, :], ps[0:SUB, 3, EXPERTS:2 * EXPERTS], ALU.add)
                    for s in range(2):
                        link(nc.vector.tensor_tensor(at_s[:, s + 1], at_s[:, s], hot_s[:, 2, s], ALU.add))
                    for k in range(2):
                        ins = nc.vector.tensor_tensor(pick_s[:, 2 + k], at_s[:, :, :], hot_s[:, k], ALU.mult)
                    link(ins)
                    for k in range(2):
                        ins = nc.vector.reduce_sum(pos_s[:, bass.ds(g * 6 + 3 * k, 3)], pick_s[:, 2 + k], axis=AX.X)
                    link(ins)
                    dve.wait_ge(S[f"sent{par}"], i + CREDIT)
                    dve.sem_inc(S["settle_v"], 1)
                    nc.vector.tensor_copy(idx_s[:, par, :], pos_s[:, bass.ds(g * 6, 6)]).then_inc(S["idx_c"], 1)
            assert done["links"] == 2 * per_r, done["links"]
            done["before"], done["links"] = base + per_r * GROUPS, 0
            for par in range(2):
                dve.wait_ge(S[f"scat{par}"], 96 * (GROUPS // 2))
            nc.vector.memset(zero_s[:, :, :], 0.0)
            cnt, tiles, ends, delta = (til_s[:, k, :] for k in range(4))
            nc.vector.tensor_copy(tili_s[:, 1, :], base_s[:, :])
            link(nc.vector.tensor_tensor(cnt, base_s[:, :], region_s[0:SUB, :], ALU.subtract))
            link(nc.vector.tensor_scalar(cnt, cnt, float(SLOTS - 1), None, ALU.add))
            link(nc.vector.tensor_copy(tili_s[:, 0, :], cnt))
            link(nc.vector.tensor_scalar(tili_s[:, 0, :], tili_s[:, 0, :], SLOTS.bit_length() - 1, None,
                                         ALU.arith_shift_right))
            link(nc.vector.tensor_copy(tiles, tili_s[:, 0, :]))
            link(nc.vector.tensor_copy(ends, tiles))
            for e in range(1, EXPERTS):
                link(nc.vector.tensor_tensor(ends[:, e:e + 1], ends[:, e:e + 1], ends[:, e - 1:e], ALU.add))
            link(nc.vector.tensor_tensor(delta, ends, tiles, ALU.subtract))
            link(nc.vector.scalar_tensor_tensor(delta, delta, float(SLOTS), region_s[0:SUB, :], ALU.mult, ALU.subtract))
            link(nc.vector.tensor_tensor(cnt[:, 1:EXPERTS], delta[:, 1:EXPERTS], delta[:, 0:EXPERTS - 1], ALU.subtract))
            full = [1, TILES, EXPERTS]
            link(nc.vector.tensor_tensor(tcmp_s[:, 0], ends[0:1, :].unsqueeze(1).to_broadcast(full),
                                         turn_s[:, :].unsqueeze(2).to_broadcast(full), ALU.is_le))
            link(nc.vector.tensor_tensor(tcmp_s[:, 1], tcmp_s[:, 0], tiles[0:1, :].unsqueeze(1).to_broadcast(full), ALU.mult))
            nc.vector.reduce_sum(tab_s[:, 0, :], tcmp_s[:, 0], axis=AX.X)
            link(nc.vector.reduce_sum(tab_s[:, 1, :], tcmp_s[:, 1], axis=AX.X))
            nc.vector.tensor_scalar(tab_s[:, 2, :], tab_s[:, 0, :], float(EXPERTS), float(SLOTS), ALU.is_lt, ALU.mult)
            link(nc.vector.tensor_tensor(tab_s[:, 1, :], turn_s[:, :], tab_s[:, 1, :], ALU.subtract))
            link(nc.vector.tensor_tensor(tab_s[:, 1, :], tab_s[:, 1, :], tab_s[:, 2, :], ALU.mult))
            link(nc.vector.scalar_tensor_tensor(tab_s[:, 2, :], tab_s[:, 0, :], float(REGION), tab_s[:, 1, :],
                                                ALU.mult, ALU.add))
            link(nc.vector.tensor_scalar(tab_s[:, 3, :], tab_s[:, 0, :], float(EXPERTS - 1), None, ALU.min))
            link(nc.vector.tensor_copy(tabi_s[:, 0, :], tab_s[:, 2, :]))
            nc.vector.tensor_copy(tabi_s[:, 1, :], tab_s[:, 3, :]).then_inc(S["base_c"], 1)
            pos, new, other = pos_s[:, :], step_s[:, 0, :], step_s[:, 1, :]
            link(nc.vector.tensor_scalar(new, pos, delta[:, 0:1], None, ALU.add))
            for e in range(1, EXPERTS):
                link(nc.vector.tensor_scalar(other, pos, float(e * REGION), cnt[:, e:e + 1], ALU.is_ge, ALU.mult))
                link(nc.vector.tensor_tensor(new, new, other, ALU.add))
            link(nc.vector.tensor_copy(pos, new))
            dve.wait_ge(S["pad_out"], 16 * (EXPERTS + 1))
            dve.wait_ge(S["b2_in"], 16)
            dve.sem_inc(S["tab_r"], 1)

            def split_rows(t, par):
                dve.wait_ge(S["xhi_c"], t + 1)
                nc.vector.tensor_tensor(xh_s[:, par, 1, :], ps[:, par, :], xh_s[:, par, 0, :],
                                        ALU.subtract).then_inc(S["xlo_c"], 1)

            def split_hidden(t, par):
                dve.wait_ge(S["gel_c"], 4 * (t + 1) + CREDIT)
                hi, lo = (hh_s[:, par, k].rearrange("p j n -> p (j n)") for k in range(2))
                nc.vector.tensor_copy(hi, hf_s).then_inc(S["hhi_c"], 1)
                dve.wait_ge(S["hhi_c"], t + 1)
                nc.vector.tensor_tensor(lo, hf_s, hi, ALU.subtract).then_inc(S["hlo_c"], 1)

            def scaled_rows(t, par, k):
                e = dve.value_load(tabi_s[0:1, 1, bass.ds(t, 1)], min_val=0, max_val=EXPERTS - 1)
                dve.wait_ge(S["w2_p"], t + 1 + CREDIT)
                dve.wait_ge(S[f"yst{par}"], 16 * k + CREDIT)
                nc.vector.scalar_tensor_tensor(yo_s[:, par], ps[:, 6 + par, :].rearrange("p (s c) -> p s c", s=2),
                                               1.0 / WSCALE, b2_s[:, bass.ds(e * C, C)].unsqueeze(1)
                                               .to_broadcast([128, 2, C]), ALU.mult, ALU.add).then_inc(S["yo_c"], 1)

            split_rows(0, 0)
            split_rows(1, 1)
            with dve.Fori(0, TILES // 2 - 1) as i:
                for k in range(2):
                    t = i * 2 + 1 + k
                    dve.wait_ge(S["h_p"], 4 * t)
                    split_rows(t + 1, k)
                    split_hidden(t - 1, k)
                    scaled_rows(t - 1, k, i)
            for t in range(TILES - 2, TILES):
                split_hidden(t, t % 2)
                scaled_rows(t, t % 2, t // 2)

            def ask(g, par):
                dve.sem_inc(S["settle_v"], 1)
                nc.vector.tensor_copy(idx_s[:, par, :], pos_s[:, bass.ds(g * 6, 6)]).then_inc(S["idx2_c"], 1)

            def combine(g, par, come):
                dve.wait_ge(S[f"gat{par}"], 96 * come)
                dve.wait_ge(S["back_p"], g + CREDIT)
                dve.sem_inc(S["settle_v"], 1)
                w0, w1 = (wt_s[:, bass.ds(g * 6 + 3 * k, 3)].unsqueeze(2).to_broadcast([SUB, 3, C]) for k in range(2))
                nc.vector.tensor_tensor(mix_s[:, :, :], got_s[:, par, 0:3, :], w0, ALU.mult).then_inc(S["mx0_c"], 1)
                nc.vector.tensor_tensor(got_s[:, par, 3:6, :], got_s[:, par, 3:6, :], w1, ALU.mult).then_inc(S["mx0_c"], 1)
                dve.wait_ge(S["mx0_c"], 2 * g + 2)
                nc.vector.tensor_tensor(mix_s[:, :, :], mix_s[:, :, :], got_s[:, par, 3:6, :],
                                        ALU.add).then_inc(S["mix_c"], 1)
                dve.wait_ge(S["mix_c"], g + 1)

            def finish(g):
                x1 = big[:, bass.ds(g * (HALVES * TOK), HALVES * TOK)].rearrange("p (h t) -> p h t", h=HALVES)
                dve.wait_ge(S["back_p"], g + 1 + CREDIT)
                nc.vector.tensor_tensor(x1, x1, ps[:, 0:2, 0:TOK], ALU.add).then_inc(S["fin_c"], 1)

            ask(0, 0)
            ask(1, 1)
            with dve.Fori(0, GROUPS // 2 - 1) as i:
                for par in range(2):
                    combine(i * 2 + par, par, i + 1)
                    ask(i * 2 + par + 2, par)
                    finish(i * 2 + par)
            for g in range(GROUPS - 2, GROUPS):
                combine(g, g % 2, g // 2 + 1)
                finish(g)

        @block.scalar
        def _(act):
            for n, v in enumerate((se_ab[:, 0:1], sa_ab[:, :, 0:1], stats[:, 1, :])):
                act.wait_ge(S["var_c"], n + 1)
                nc.scalar.activation(v, v, ACT.Sqrt).then_inc(S["root_c"], 1)
            act.wait_ge(S["norm"], 1)
            with act.Fori(0, HW // 3) as i:
                act.wait_ge(S["tr_c"], i + CREDIT)
                nc.scalar.activation(xp_s[:, :, :], by_pixel(big)[:, bass.ds(i * 3, 3), :], ACT.Copy).then_inc(S["xp_c"], 1)
                act.wait_ge(S["tr_c"], i + 1 + CREDIT)
                act.wait_ge(S["k1_c"], i + CREDIT)
                nc.scalar.activation(xt_s[:, :, :], ps[:, 0:3, 0:C], ACT.Copy).then_inc(S["xt_c"], 1)
            act.wait_ge(S["var_c"], 4)
            nc.scalar.activation(tapbn_s[:, 1, :], tapbn_s[:, 1, :], ACT.Sqrt).then_inc(S["root_c"], 1)
            act.wait_ge(S["tab_c"], 1)
            with act.Fori(0, C // CHUNK) as i:
                for n in range(0, 9, 2):
                    act.wait_ge(S["mb_p"], i * 9 + n + 1 + CREDIT)
                    if n == 0:
                        act.wait_ge(S["cv_p"], i * 8 + CREDIT)
                    flat = ps[0:HW + 1, 0:2, :].rearrange("p b n -> p (b n)")[:, 0:9 * 2 * CHUNK]
                    nc.scalar.activation(m_s[:, :, :, n * 9:(n + 1) * 9].rearrange("p c v m -> p m v c"),
                                         flat.rearrange("p (m v c) -> p m v c", m=9, v=2), ACT.Copy).then_inc(S["mb_e0"], 1)
                for q in range(8):
                    par = q % 2
                    b0 = 6 if par == 0 else 2
                    act.wait_ge(S["cv_p"], i * 8 + q + 1 + CREDIT)
                    act.wait_ge(S[f"st_v{par}"], 48 * (i * 4 + q // 2) + CREDIT)
                    cv = ps[:, b0:b0 + 2, 0:4 * HW].rearrange("p k (c v n) -> p k c v n", c=2, v=2)
                    nc.scalar.activation(v_s[:, par].rearrange("p (k c) n -> p k c n", k=2), cv[:, :, :, 0, :],
                                         ACT.Copy).then_inc(S["v_c"], 1)
                    nc.scalar.activation(ks_s[:, par].rearrange("p (k c) n -> p k c n", k=2), cv[:, :, :, 1, :],
                                         ACT.Relu).then_inc(S["ks_c"], 1)
            act.wait_ge(S["phase_a"], 1)
            with act.Fori(0, GROUPS // 2) as i:
                for par in range(2):
                    g = i * 2 + par
                    for n in range(2):
                        act.wait_ge(S["se1_p"], g * 2 + n + 1)
                        act.wait_ge(S["lg_p"], g + CREDIT)
                        nc.scalar.activation(a_s[0:HW, 2 * n:2 * n + 2, :].rearrange("p b j -> p (b j)"), ps[0:HW, n, :],
                                             ACT.Relu, bias=se_ab[:, 1:2], scale=se_ab[:, 0:1]).then_inc(S["a_c"], 1)
                    for h in range(HALVES):
                        act.wait_ge(S["sa1_p"], g * 2 + h + 1)
                        nc.scalar.activation(a2_s[:, h, :], ps[:, 2 + h, 0:TOK], ACT.Relu, bias=sa_ab[:, h, 1:2],
                                             scale=sa_ab[:, h, 0:1]).then_inc(S["a2_c"], 1)
                    act.wait_ge(S["lgs_c"], g + 1)
                    nc.scalar.activation(lg_s[:, :, :], lg_s[:, :, :], ACT.Exp).then_inc(S["ex_c"], 1)
                    act.wait_ge(S["l2m_c"], g + 1)
                    act.wait_ge(S["x1_c"], g + CREDIT)
                    for h in range(HALVES):
                        for b in range(G):
                            j = h * G + b
                            ins = nc.scalar.activation(e_s[:, h, b, :], ps[:, 2 + h, b * HW:(b + 1) * HW], ACT.Exp,
                                                       bias=sm_s[:, 2, j:j + 1], accum_out=sm_s[:, 3, j:j + 1])
                    ins.then_inc(S["e_c"], 1)
            act.wait_ge(S["x1_c"], GROUPS + CREDIT)
            with act.Fori(0, GROUPS // 2) as i:
                for par in range(2):
                    g = i * 2 + par
                    b0 = 4 * par
                    act.wait_ge(S["rl_p"], g + CREDIT)
                    nc.scalar.activation(xs_s[:, :, :].rearrange("p h t -> p (h t)"),
                                         big[:, bass.ds(g * (HALVES * TOK), HALVES * TOK)], ACT.Copy).then_inc(S["xs_c"], 1)
                    act.wait_ge(S["var2_c"], g + 1)
                    nc.scalar.activation(bs_s[:, :, 8:9], bs_s[:, :, 8:9], ACT.Ln).then_inc(S["ln_c"], 1)
                    act.wait_ge(S["ln_c"], g + 1)
                    nc.scalar.activation(bs_s[:, :, 8:9], bs_s[:, :, 8:9], ACT.Exp, scale=-0.5).then_inc(S["rstd_c"], 1)
                    act.wait_ge(S["probs_c"], g + 1)
                    nc.scalar.activation(pr_s[:, :, 2, :], pr_s[:, :, 1, :], ACT.Exp).then_inc(S["ex2_c"], 1)
                    act.wait_ge(S["nmr_c"], g + 1)
                    act.wait_ge(S[f"sent{par}"], i + CREDIT)
                    for s in range(3):
                        ins = nc.scalar.activation(xf_s[:, par, s, :], ps[0:SUB, b0 + s // 2, (s % 2) * C:(s % 2 + 1) * C],
                                                   ACT.Identity, bias=bs_s[:, s, 9:10], scale=bs_s[:, s, 8:9])
                    ins.then_inc(S["xft_c"], 1)
            act.wait_ge(S["tab_r"], 1)

            def high_rows(t, par, first=False):
                act.wait_ge(S["tt_p"], t + 1)
                if not first:
                    act.wait_ge(S["h_p"], 4 * (t - 1))
                nc.scalar.activation(xh_s[:, par, 0, :], ps[:, par, :], ACT.Copy).then_inc(S["xhi_c"], 1)

            def gelu(t, par, first=False):
                e = act.value_load(tabi_s[0:1, 1, bass.ds(t, 1)], min_val=0, max_val=EXPERTS - 1)
                if not first:
                    act.wait_ge(S["hlo_c"], t)
                for j in range(KB):
                    act.wait_ge(S["h_p"], 4 * t + j // 2 * 2 + 2)
                    nc.scalar.activation(hf_s[:, j * SLOTS:(j + 1) * SLOTS],
                                         ps[:, 2 + 2 * par + j // 2, (j % 2) * SLOTS:(j % 2 + 1) * SLOTS], ACT.Gelu,
                                         bias=b1_s[:, bass.ds(e * KB + j, 1)], scale=1.0 / WSCALE).then_inc(S["gel_c"], 1)

            high_rows(0, 0, first=True)
            high_rows(1, 1, first=True)
            gelu(0, 0, first=True)
            with act.Fori(0, TILES // 2 - 1) as i:
                for k in range(2):
                    t = i * 2 + 1 + k
                    high_rows(t + 1, k)
                    gelu(t, 1 - k)
            gelu(TILES - 1, 1)

        @block.gpsimd
        def _(pool):
            for n in CREDITED:
                pool.sem_inc(S[n], CREDIT)
            pool.wait_ge(S["w_in"], W_IN)

            def settle():
                pool.sem_inc(S["settle_g"], 1)

            pool.sem_inc(S["sq_p"], 1)
            pool.sem_inc(S["phase_b"], 1)
            with pool.Fori(0, C // QUAD // 2) as i:
                for par in range(2):
                    q = i * 2 + par
                    pool.wait_ge(S[f"rk_in{par}"], 32 * (i + 1))
                    settle()
                    nc.gpsimd.tensor_scalar(kr_s[:, par], kr_s[:, par], alpha_s[:, 0:1], None, ALU.mult).then_inc(S["ch_g"], 1)
                    pool.wait_ge(S["ch_g"], q + 1)
                    settle()
                    nc.gpsimd.tensor_tensor(kr_s[:, par], kr_s[:, par], xr_s[:, par], ALU.add).then_inc(S["r1_c"], 1)
                    pool.wait_ge(S["r_c"], q + 1)
                    pool.wait_ge(S["cv_p"], q + 1 + CREDIT)
                    pool.sem_inc(S["sq_p"], 1)
            with pool.Fori(0, GROUPS) as g:
                pool.wait_ge(S["ar_c"], g + 1)
                pool.wait_ge(S["raw_p"], 2 * g + CREDIT)
                settle()
                nc.gpsimd.tensor_copy(arx_s[:, :, :].rearrange("p j (t n) -> p j t n", n=16),
                                      ar_s[:, :, :].unsqueeze(2).to_broadcast([128, G * 2, 8, 16])).then_inc(S["arx_c"], 1)
                pool.wait_ge(S["x1_c"], g + 1 + CREDIT)
                pool.sem_inc(S["phase_b"], 1)
            with pool.Fori(0, GROUPS // 2) as i:
                for par in range(2):
                    g = i * 2 + par
                    pool.wait_ge(S["xft_c"], g + 1 + CREDIT)
                    pool.wait_ge(S["idx_c"], g + 1)
                    settle()
                    for k in range(6):
                        nc.gpsimd.indirect_dma_start(
                            out=rows_d[:, :], out_offset=bass.IndirectOffsetOnAxis(ap=idx_s[:, par, k:k + 1], axis=0),
                            in_=xf_s[:, par, k % 3, :], in_offset=None).then_inc(S[f"scat{par}"], 16)
                for par in range(2):
                    pool.wait_ge(S[f"scat{par}"], 96 * (i + 1))
                    pool.sem_inc(S[f"sent{par}"], 1)
            for par in range(2):
                pool.wait_ge(S[f"yst{par}"], 16 * (TILES // 2) + CREDIT)
            pool.wait_ge(S["w2_p"], TILES + CREDIT)
            with pool.Fori(0, GROUPS // 2) as i:
                for par in range(2):
                    g = i * 2 + par
                    pool.wait_ge(S["idx2_c"], g + 1)
                    settle()
                    for k in range(6):
                        nc.gpsimd.indirect_dma_start(
                            out=got_s[:, par, k, :], out_offset=None, in_=y_d[:, :],
                            in_offset=bass.IndirectOffsetOnAxis(ap=idx_s[:, par, k:k + 1], axis=0))\
                          .then_inc(S[f"gat{par}"], 16)


def _shape_constants(np):
    toep = np.zeros((11, HW, HW + 1), np.float32)
    for ky in range(3):
        for kx in range(3):
            for y in range(H):
                for xx in range(W):
                    yy, xi = y + ky - 1, xx + kx - 1
                    if 0 <= yy < H and 0 <= xi < W:
                        toep[ky * 3 + kx, y * W + xx, yy * W + xi] = 1.0
    toep[9, :, HW] = -1.0
    toep[10, :, HW] = 1.0
    r = np.arange(128)
    band0 = (abs(np.arange(BAND0)[None] - r[:, None]) <= D // 2)
    band1 = (abs(np.arange(BAND1)[None] + BAND1_START - 128 - r[:, None]) <= D // 2)
    turn = (r - D // 2) % 16
    rot = np.concatenate([(turn % 4)[:, None] == np.arange(4), (turn // 4)[:, None] == np.arange(4)], 1)
    rows = np.ones((11, 2), np.float32)
    rows[:, 1] = 0.0
    rows[10] = (0.0, 1.0)
    before = (r[:, None] < r[None]).astype(np.float32)
    region = np.tile(np.arange(EXPERTS, dtype=np.float32) * REGION, (128, 1))
    tiles = np.arange(TILES, dtype=np.float32)[None]
    lower = np.tile(np.tril(np.ones((EXPERTS, EXPERTS)), -1).reshape(1, -1), (128, 1))
    f = np.float32
    return toep, np.concatenate([band0, band1], 1).astype(f), rot.astype(f), rows, lower.astype(f), before, region, tiles


def kernel(**inputs):
    import numpy as np
    import concourse.bacc as bacc
    from concourse import mybir as mb
    from concourse.bass_utils import run_bass_kernel_spmd

    i = {k.replace("L0_", ""): np.ascontiguousarray(v) for k, v in inputs.items()}
    toep, bands, rot, rows, lower, before, region, tiles = _shape_constants(np)
    f = np.float32
    taps = np.zeros((11, 2, C), f)
    taps[0:9, 0] = i["conv_se_val_w"].reshape(C, 9).T
    taps[10, 0] = i["conv_se_val_b"]
    taps[0:9, 1] = i["conv_sa_key_w"].reshape(C, 9).T
    taps[9, 1] = i["conv_sa_key_bn"][2]
    taps[10, 1] = i["conv_sa_key_bn"][1]
    tap_bn = np.ascontiguousarray(np.broadcast_to(i["conv_sa_key_bn"][[0, 3]], (11, 2, C)))
    z = np.zeros((HW, ZLEN), f)
    z[:, 127:136] = i["conv_se_key_w"][:, 0, ::-1]
    w1 = i["conv_sa_att_w1"].reshape(C, 8, 2)
    w2 = i["conv_sa_att_w2"].reshape(C // 8, 8)
    sa_w1 = np.zeros((128, HALVES, 2, 128), f)
    sa_w2 = np.zeros((128, HALVES, 128), f)
    for h in range(HALVES):
        for g in range(16):
            s = slice(g * 8, g * 8 + 8)
            for k in range(2):
                sa_w1[s, h, k, s] = w1[h * 128 + g * 8:h * 128 + g * 8 + 8, :, k].T
            sa_w2[s, h, s] = np.broadcast_to(w2[h * 16 + g][:, None], (8, 8))

    def halves(a):
        return np.ascontiguousarray(a.reshape(HALVES, 128, -1).transpose(1, 0, 2))

    se_w2 = np.concatenate([i["conv_se_att_w2"].T, i["conv_se_att_b2"][None]], 0)
    arrays = {
        "x": i["x"].reshape(BS, C * HW), "taps": taps, "tap_bn": tap_bn, "tap_rows": rows, "toeplitz_mask": toep,
        "ident": np.eye(128, dtype=f), "band_masks": bands, "rot_masks": rot, "zstrings": z,
        "key_bias": np.broadcast_to(i["conv_se_key_b"], (128, HW)),
        "se_w1": i["conv_se_att_w1"].T.reshape(2, HW, HW).transpose(1, 0, 2), "se_bn": i["conv_se_att_bn"].T,
        "se_w2": se_w2, "sa_w1": sa_w1, "sa_bn": halves(i["conv_sa_att_bn"].T), "sa_w2": sa_w2,
        "sa_b2": np.repeat(i["conv_sa_att_b2"], 8).reshape(HALVES, 128).T,
        "alpha": np.broadcast_to(i["conv_alpha"], (128, 1)),
        "router": halves(i["ffn_Wr"].T), "router_bias": np.broadcast_to(i["ffn_br"], (128, EXPERTS)),
        "lower": lower, "before": before, "region_start": region, "turn": tiles,
        "ffn_w1": i["ffn_W1"].reshape(EXPERTS, 2, 128, HID),
        "ffn_b1": i["ffn_b1"].reshape(EXPERTS * KB, 128).T,
        "ffn_w2": i["ffn_W2"].reshape(EXPERTS, 2, 2, 128, C).transpose(0, 1, 3, 2, 4).reshape(EXPERTS, 2, 128, 2 * C),
        "ffn_b2": i["ffn_b2"],
    }
    nc = bacc.Bacc("TRN2", target_bir_lowering=False, num_devices=1)
    feeds, args = {}, []
    for name, a in arrays.items():
        a = np.ascontiguousarray(a)
        feeds[f"in_{name}"] = a
        args.append(nc.dram_tensor(f"in_{name}", a.shape, mb.dt.from_np(a.dtype), kind="ExternalInput").ap())
    args.append(nc.dram_tensor("out_0", (BS, C * HW), mb.dt.float32, kind="ExternalOutput").ap())
    metaformer_kernel(nc, *args)
    r = run_bass_kernel_spmd(nc, [feeds], core_ids=[0])
    return r.results[0]["out_0"].reshape(BS, C, H, W)
```

```python
import concourse.bass as bass
from concourse import mybir
from contextlib import ExitStack

BS, C, H, W = 128, 256, 9, 9
HW = H * W
HALVES = C // 128
PIX = 3
PIX_TURNS = HW // PIX
D = 9
EXPERTS, HID = 8, 512
BN_EPS, LN_C_EPS, LN_T_EPS = 1e-5, 1e-6, 1e-5
G = 4
GROUPS = BS // G
PAIRS = GROUPS // 2
TOK = G * HW
SUBS = 3
ROWS = SUBS * 128
TURNS = BS * HW // ROWS
KB = HID // 128
QUAD = 4
QUADS = C // QUAD
DEPTH = 4
CHUNK = 32
AUX = 4624
TAP_ROWS = 64 + 11
PIECE = 512
PIECES = EXPERTS * 4
WSCALE = 64.0
SLOTS = 256
REGION = BS * HW + SLOTS
MOST = (2 * BS * HW + EXPERTS * (SLOTS - 1)) // SLOTS
TILES = MOST + MOST % 2
BAND0, BAND1 = 132, 160
ZLEN = 264
BAND1_START = 96

CREDIT = 2
CREDITED = """k1_c k1_ev tr_c xt_c xb_c v_c ks_c pt_c e_c x1_c fin_c gel_c cv_p mb_p tq_p st_v0 st_v1
              st_v2 st_v3 lg_p raw_p msk_c t_c band_p w2_p xft_c lgr_c rl_p sent0 sent1 sent2 yst0 yst1 yo_c
              back_p""".split()


def metaformer_kernel(nc, x, taps, tap_bn, tap_rows, toeplitz_mask, ident, band_masks, rot_masks, zstrings,
                      key_bias, se_w1, se_bn, se_w2, sa_w1, sa_bn, sa_w2, sa_b2, alpha, router, router_bias,
                      lower, before, region_start, turn, ffn_w, ffn_b1, ffn_b2, out):
    fp32, fp16, bf16 = mybir.dt.float32, mybir.dt.float16, mybir.dt.bfloat16
    ALU, ACT, AX = mybir.AluOpType, mybir.ActivationFunctionType, mybir.AxisListType

    ctx = ExitStack()
    with ctx:
        def sb(name, shape, dt=fp32):
            return ctx.enter_context(nc.sbuf_tensor(name, shape, dt))

        def sem(name):
            return ctx.enter_context(nc.semaphore(name))

        def dram(name, shape):
            return nc.dram_tensor(name, shape, fp32, kind="Internal").ap()

        xn_d, k1_d, v_d, ks_d = (dram(n, [BS, C * HW]) for n in ("xn_d", "k1_d", "v_d", "ks_d"))

        rows_d = dram("rows_d", [EXPERTS * REGION + SLOTS, C])
        y_d = dram("y_d", [TILES * SLOTS, C])
        u_d = dram("u_d", [HW, 128, 136])

        ident_s = sb("ident_s", [128, 128])
        band_s = sb("band_s", [128, BAND0 + BAND1])
        rot_s = sb("rot_s", [128, 8])
        alpha_s = sb("alpha_s", [128, 2])
        se_w1_s = sb("se_w1_s", [HW, 2, HW])
        se_w2_s = sb("se_w2_s", [HW + 1, D])
        se_bn_s = sb("se_bn_s", [HW, 4])
        se_ab = sb("se_ab", [HW, 3])
        sa_w1_s = sb("sa_w1_s", [128, HALVES, 2, 128])
        sa_w2_s = sb("sa_w2_s", [128, HALVES, 128])
        sa_bn_s = sb("sa_bn_s", [128, HALVES, 4])
        sa_ab = sb("sa_ab", [128, HALVES, 3])
        sa_b2_s = sb("sa_b2_s", [128, HALVES])
        router_s = sb("router_s", [128, HALVES, EXPERTS])
        router_bias_s = sb("router_bias_s", [128, EXPERTS])
        lower_s = sb("lower_s", [128, EXPERTS * EXPERTS])
        b1_s = sb("b1_s", [128, EXPERTS * KB])
        before_s = sb("before_s", [128, 128])
        ones_s = sb("ones_s", [128, 128])
        region_s = sb("region_s", [128, EXPERTS])
        turn_s = sb("turn_s", [1, TILES])
        big = sb("big", [128, C * HW])
        pool_ = sb("pool_", [128, C * HW])

        cursor = [0]

        def take(parts, *dims):
            n = 1
            for d in dims:
                n *= d
            a = pool_[0:parts, cursor[0]:cursor[0] + n]
            cursor[0] += n
            assert cursor[0] <= C * HW
            names = "abcde"[:len(dims)]
            if len(dims) > 1:
                a = a.rearrange(f"p ({' '.join(names)}) -> p {' '.join(names)}",
                                **{m: d for m, d in zip(names, dims)})
            return a

        aux = sb("aux", [128, AUX])
        aux_at = [0]

        def take_aux(parts, *dims, dt=fp32):
            n = 1
            for d in dims:
                n *= d
            words = n if dt != fp16 else n // 2
            a = aux[0:parts, aux_at[0]:aux_at[0] + words]
            aux_at[0] += words
            assert aux_at[0] <= AUX
            a = a if dt == fp32 else a.bitcast(dt)
            names = "abcde"[:len(dims)]
            if len(dims) > 1:
                a = a.rearrange(f"p ({' '.join(names)}) -> p {' '.join(names)}",
                                **{m: d for m, d in zip(names, dims)})
            return a

        stats = take_aux(128, 4, HW)
        u_s = take_aux(128, 2, PIX, 136)
        xp_s = take_aux(128, 2, PIX, C)
        xt_s = take_aux(128, 2, PIX, C)
        kb_s = take_aux(128, HW)

        ps = ctx.enter_context(nc.psum_tensor("ps", [128, 8, 512], fp32))

        cursor[0] = 0
        bn_s = take(128, HW, 2 * HALVES, 3)
        cursor[0] = 0
        mask_s = take(TAP_ROWS, HW * (HW + 1) // 2).bitcast(bf16).rearrange("p (m n) -> p m n", n=HW + 1)
        taps_s = take(11, 2, C)
        tapr_s = take(11, 2, C)
        taph_s = take(TAP_ROWS, C).bitcast(bf16).rearrange("p (v c) -> p v c", v=2)
        tapc_s = take(TAP_ROWS, CHUNK).bitcast(bf16).rearrange("p (v c) -> p v c", v=2)
        tapbn_s = take(11, 2, C)
        taprow_s = take(11, 2)
        tables_end = cursor[0]
        m_s = take(HW + 1, CHUNK, 2, HW)
        assert cursor[0] <= C * HW // 2
        aux_at[0] = 0
        xq_s = take_aux(128, 2, QUAD, HW)
        pt_s = take_aux(HW + 1, 2, QUAD, BS)
        v_s = take_aux(128, DEPTH, QUAD, HW)
        ks_s = take_aux(128, DEPTH, QUAD, HW)
        cursor[0] = 0
        kq_s = take(HW, 2, 2, G, C)
        xc_s, vc_s, kc_s, xr_s, kr_s = (take(128, 2, HALVES, G, HW) for _ in range(5))
        a_s = take(HW + 1, 2, G, C)
        lg_s = take(128, G * 4, D)
        st_s = take(128, 4, G * 4)
        ap_s = take(128, G * 4, 15)
        t1_s = take(128, G * 4, 32)
        ar_s = take(128, G * 4, 16)
        arx_s = take(128, G * 4, 128)
        a0_s = take(128, G, BAND0)
        a1_s = take(128, G, BAND1)
        a2_s = take(128, HALVES, TOK)
        e_s = take(128, 2, HALVES, G, HW)
        sm_s = take(128, 2, 4, HALVES * G)
        cursor[0] = 0
        w_s = take(128, PIECES * PIECE).bitcast(fp16).rearrange("p (s n) -> p s n", s=2)
        b2_s = take(128, EXPERTS * C)
        stage_at = cursor[0]
        rin_s = take(128, 2, 2, C)
        yo_s = take(128, 2, 2, C)
        stage_s = pool_[:, stage_at:stage_at + 3 * PIECE].rearrange("p (a n) -> p a n", a=3)
        i32, u32 = mybir.dt.int32, mybir.dt.uint32
        pos_s = sb("pos_s", [128, TURNS * 6])
        wt_s = sb("wt_s", [128, TURNS * 6])
        idx_s = sb("idx_s", [128, SUBS, 6], u32)
        base_s = sb("base_s", [128, EXPERTS])
        til_s = sb("til_s", [128, 4, EXPERTS])
        tili_s = sb("tili_s", [128, 2, EXPERTS], i32)
        tabi_s = sb("tabi_s", [1, 2, TILES], i32)
        aux_at[0] = 0
        xf_s = take_aux(128, 3, SUBS, C)
        xs_s = [take_aux(128, HALVES, ROWS) for _ in range(2)]
        xs_at = stage_at + 3 * PIECE
        xs_s.append(pool_[:, xs_at:xs_at + HALVES * ROWS].rearrange("p (h t) -> p h t", h=HALVES))
        bs_s = take_aux(128, 3, SUBS, 10)
        pr_s = take_aux(128, SUBS, 4, EXPERTS)
        cmp_s = take_aux(128, SUBS, EXPERTS, 2, EXPERTS)
        hot_s = take_aux(128, SUBS, 3, EXPERTS)
        tot_s = take_aux(128, EXPERTS)
        at_s = take_aux(128, SUBS, EXPERTS)
        pick_s = take_aux(128, 4, 3, EXPERTS)
        aux_at[0] = 3 * SUBS * C
        tab_s = take_aux(1, 4, TILES)
        tcmp_s = take_aux(1, 2, TILES, EXPERTS)
        zero_s = take_aux(128, 2, C)
        aux_at[0] = 0
        xh_s = take_aux(128, 2, 2, HALVES * SLOTS, dt=fp16)
        hf_s = take_aux(128, KB * SLOTS)
        hh_s = take_aux(128, 2, 2, KB, SLOTS, dt=fp16)
        step_s = take_aux(128, 2, TURNS * 6)
        aux_at[0] = 0
        got_s = take_aux(128, 2, 6, C)
        mix_s = take_aux(128, SUBS, C)

        names = """tapc_c settle_g settle_v settle_p var_c root_c win_out w_in x_in0 x_in1 bn_c norm xn_out
                   k1_out0 k1_outm k1_out1 u_in0 u_in1 xp_c xb_c tr_c xt_c k1_c k1_ev tab_in mask_in tab_c xq_c rk_in0
                   rk_in1 mb_p mb_e0 mb_e1 tq_p pt_c cv_p v_c ks_c r1_c st_v0 st_v1 st_v2 st_v3 ch_d ch_g kq_in0
                   kq_in1 c_in0 c_in1 v_in0 v_in1 t_c se1_p a_c lg_p lgs_c ex_c ar_c arx_c raw_p msk_c sa1_p a2_c
                   l2_p l2m_c e_c band_p x1_c phase_a wst_in0 wst_in1 wst_in2 whi_c wlo_c b2_in rm_p rw_c xs_c
                   t1_p rl_p lgr_c var2_c ln_c rstd_c nmr_c probs_c ex2_c tot_c tri_p xft_c idx_c sent0 sent1
                   sent2 scat0 scat1 scat2 ends_c base_c pad_out tab_r rin0 rin1 tt_p xhi_c xlo_c h_p gel_c hhi_c
                   hlo_c w2_p yo_c yst0 yst1 idx2_c gat0 gat1 mx0_c mix_c back_p fin_c out_s""".split()
        S = {n: sem(n) for n in names}

        def by_pixel(buf):
            return buf[:, :].rearrange("b (c p) -> b p c", p=HW)

        x1_s = big[:, :].rearrange("p (h t) -> p h t", h=HALVES)

        W_IN = 16 * 19
        block = ctx.enter_context(nc.Block())

        @block.sync
        def _(sp):
            half = C * HW // 2
            for h in range(HALVES):
                sp.dma_start(big[:, h * half:(h + 1) * half], x[:, h * half:(h + 1) * half]).then_inc(S[f"x_in{h}"], 16)
            n = 0
            for dst, src in ((ident_s[:, :], ident), (band_s[:, :], band_masks), (rot_s[:, :], rot_masks),
                             (alpha_s[:, 0:1], alpha), (se_w1_s[:, :, :], se_w1), (se_w2_s[:, :], se_w2),
                             (se_bn_s[:, :], se_bn), (sa_w1_s[:, :, :, :], sa_w1), (sa_w2_s[:, :, :], sa_w2),
                             (sa_bn_s[:, :, :], sa_bn), (sa_b2_s[:, :], sa_b2), (router_s[:, :, :], router),
                             (router_bias_s[:, :], router_bias), (lower_s[:, :], lower), (b1_s[:, :], ffn_b1),
                             (before_s[:, :], before),
                             (region_s[:, :], region_start), (turn_s[:, :], turn), (kb_s[:, :], key_bias)):
                sp.dma_start(dst, src).then_inc(S["w_in"], 16)
                n += 1
            assert 16 * n == W_IN
            window = bass.AP(zstrings.tensor, 127, [[ZLEN, HW], [-1, 128], [1, 136]])
            sp.dma_start(u_d, window).then_inc(S["win_out"], 16)
            sp.wait_ge(S["win_out"], 16)

            def load_bands(i, par):
                sp.wait_ge(S["k1_c"], i - 1 + CREDIT)
                src = u_d[bass.ds(i * PIX, PIX), :, :].rearrange("t c j -> c t j")
                sp.dma_start(u_s[:, par], src).then_inc(S[f"u_in{par}"], 16)

            with sp.Fori(0, PIX_TURNS // 2) as i:
                for par in range(2):
                    load_bands(i * 2 + par, par)
            load_bands(PIX_TURNS - 1, 0)
            sp.wait_ge(S["k1_ev"], PIX_TURNS + CREDIT)
            sp.dma_start(k1_d[:, 0:tables_end], pool_[:, 0:tables_end]).then_inc(S["k1_out0"], 16)
            sp.wait_ge(S["k1_out0"], 16)
            for dst, src in ((taps_s, taps), (tapbn_s, tap_bn), (taprow_s, tap_rows)):
                sp.dma_start(dst, src).then_inc(S["tab_in"], 16)
            sp.dma_start(mask_s.bitcast(mybir.dt.uint16), toeplitz_mask).then_inc(S["mask_in"], 16)
            sp.dma_start(k1_d[:, tables_end:half], pool_[:, tables_end:half]).then_inc(S["k1_outm"], 16)
            sp.wait_ge(S["xb_c"], PIX_TURNS + CREDIT)
            with sp.Fori(0, QUADS // DEPTH) as i:
                part = bass.ds(i * (DEPTH * QUAD * HW), DEPTH * QUAD * HW)
                sp.dma_start(xn_d[:, part], big[:, part]).then_inc(S["xn_out"], 16)
                part = bass.ds(i * (DEPTH * QUAD * HW // 2) + half, DEPTH * QUAD * HW // 2)
                sp.dma_start(k1_d[:, part], pool_[:, part]).then_inc(S["k1_out1"], 16)
                for k in range(DEPTH):
                    q = i * DEPTH + k
                    cols = bass.ds(q * (QUAD * HW), QUAD * HW)
                    for dst, src, made in ((v_d, v_s, "v_c"), (ks_d, ks_s, "ks_c")):
                        sp.wait_ge(S[made], q + 1 + CREDIT)
                        sp.dma_start(dst[:, cols].rearrange("b (c p) -> b c p", p=HW),
                                     src[:, k]).then_inc(S[f"st_v{k}"], 16)
            for k in range(DEPTH):
                sp.wait_ge(S[f"st_v{k}"], 32 * (QUADS // DEPTH) + CREDIT)
            sp.wait_ge(S["xn_out"], 16 * (QUADS // DEPTH))
            sp.wait_ge(S["k1_out1"], 16 * (QUADS // DEPTH))
            def load_pair(i, first=False):
                for par in range(2):
                    g = i * 2 + par
                    rows = bass.ds(g * G, G)
                    if not first:
                        sp.wait_ge(S["se1_p"], 2 * g - 2)
                    for k, src in enumerate((xn_d, k1_d)):
                        sp.dma_start(kq_s[:, par, k],
                                     src[rows, :].rearrange("b (i j) -> i b j", j=C)).then_inc(S[f"kq_in{par}"], 16)
                    if not first:
                        sp.wait_ge(S["t_c"], g - 1 + CREDIT)
                    for dst, src, come in ((kc_s, ks_d, "c_in"), (xc_s, xn_d, "c_in"), (kr_s, k1_d, "rk_in"),
                                           (xr_s, x, "rk_in")):
                        for h in range(HALVES):
                            sp.dma_start(dst[:, par, h],
                                         src[rows, h * 128 * HW:(h + 1) * 128 * HW]
                                         .rearrange("b (c p) -> c b p", p=HW)).then_inc(S[f"{come}{par}"], 16)

            load_pair(0, first=True)
            with sp.Fori(1, PAIRS) as i:
                load_pair(i)
            sp.wait_ge(S["x1_c"], GROUPS + CREDIT)
            sp.dma_start(b2_s, bass.AP(ffn_b2.tensor, 0, [[0, 128], [1, EXPERTS * C]])).then_inc(S["b2_in"], 16)

            def load_piece(n, slot):
                if not isinstance(n, int) or n >= 3:
                    sp.wait_ge(S["wlo_c"], n - 2)
                sp.dma_start(stage_s[:, slot:slot + 1, :],
                             ffn_w[bass.ds(n, 1), :, :].rearrange("n p c -> p n c")).then_inc(S[f"wst_in{slot}"], 16)

            for n in range(3):
                load_piece(n, n)
            with sp.Fori(1, TURNS // 3) as i:
                for k in range(3):
                    load_piece(i * 3 + k, k)
            for n in range(TURNS, PIECES):
                load_piece(n, n % 3)
            sp.wait_ge(S["ends_c"], 1)
            for e in range(EXPERTS):
                first_free = sp.value_load(tili_s[0:1, 1, e:e + 1], min_val=e * REGION,
                                           max_val=(e + 1) * REGION - SLOTS)
                sp.dma_start(rows_d[bass.ds(first_free, SLOTS), :].rearrange("(s q) c -> q s c", q=128),
                             zero_s[:, :, :]).then_inc(S["pad_out"], 16)
            sp.dma_start(rows_d[EXPERTS * REGION:, :].rearrange("(s q) c -> q s c", q=128),
                         zero_s[:, :, :]).then_inc(S["pad_out"], 16)
            sp.wait_ge(S["pad_out"], 16 * (EXPERTS + 1))
            for k in range(3):
                sp.wait_ge(S[f"scat{k}"], 96 * (TURNS // 3))
            sp.wait_ge(S["base_c"], 1)
            sp.wait_ge(S["wlo_c"], PIECES)

            def load_rows(t, par):
                row = sp.value_load(tabi_s[0:1, 0, bass.ds(t, 1)], min_val=0, max_val=EXPERTS * REGION)
                sp.dma_start(rin_s[:, par], rows_d[bass.ds(row, SLOTS), :]
                             .rearrange("(s q) c -> q s c", q=128)).then_inc(S[f"rin{par}"], 16)

            def store_rows(t, par):
                sp.dma_start(y_d[bass.ds(t * SLOTS, SLOTS), :].rearrange("(s q) c -> q s c", q=128),
                             yo_s[:, par]).then_inc(S[f"yst{par}"], 16)

            load_rows(0, 0)
            load_rows(1, 1)
            for t in range(2):
                sp.wait_ge(S["tt_p"], t + 1)
                load_rows(t + 2, t)
            with sp.Fori(1, TILES // 2 - 1) as i:
                for par in range(2):
                    t = i * 2 + par
                    sp.wait_ge(S["tt_p"], t + 1)
                    load_rows(t + 2, par)
                    sp.wait_ge(S["yo_c"], t - 1 + CREDIT)
                    store_rows(t - 2, par)
            for t in range(TILES - 4, TILES):
                sp.wait_ge(S["yo_c"], t + 1 + CREDIT)
                store_rows(t, t % 2)
            for g in range(GROUPS):
                turns = -(-(g + 1) * TOK // ROWS)
                sp.wait_ge(S["fin_c"], turns + CREDIT)
                for h in range(HALVES):
                    sp.dma_start(out[g * G:(g + 1) * G, h * 128 * HW:(h + 1) * 128 * HW]
                                 .rearrange("b (c p) -> c b p", p=HW),
                                 x1_s[:, h, g * TOK:(g + 1) * TOK]
                                 .rearrange("c (b p) -> c b p", p=HW)).then_inc(S["out_s"], 16)
            sp.wait_ge(S["out_s"], 16 * HALVES * GROUPS)

        @block.tensor
        def _(pe):
            pe.wait_ge(S["w_in"], W_IN)

            def turn_pixels(i, par):
                pe.wait_ge(S["xp_c"], i + 1)
                pe.wait_ge(S["xt_c"], i - 1 + CREDIT)
                for k in range(PIX):
                    for h in range(HALVES):
                        at = (k % 2) * C + h * 128
                        last = nc.tensor.matmul(ps[:, 2 * par + k // 2, at:at + 128], xp_s[:, par, k, h * 128:(h + 1) * 128],
                                                ident_s[:, :], start=True, stop=True)
                last.then_inc(S["tr_c"], 1)

            def convolve_pixels(i, par, come):
                pe.wait_ge(S[f"u_in{par}"], 16 * come)
                pe.wait_ge(S["xt_c"], i + 1 + CREDIT)
                pe.wait_ge(S["k1_ev"], i - 1 + CREDIT)
                for k in range(PIX):
                    b, at = 4 + 2 * par + k // 2, (k % 2) * C
                    nc.tensor.matmul(ps[:, b, at:at + 132], xt_s[:, par, k, 0:128], u_s[:, par, k, 4:136],
                                     start=True, stop=False, skip_group_check=True)
                    last = nc.tensor.matmul(ps[:, b, at + 124:at + 256], xt_s[:, par, k, 128:256],
                                            u_s[:, par, k, 0:132], start=False, stop=True, skip_group_check=True)
                last.then_inc(S["k1_c"], 1)

            turn_pixels(0, 0)
            with pe.Fori(0, PIX_TURNS // 2) as i:
                for par in range(2):
                    turn_pixels(i * 2 + par + 1, 1 - par)
                    convolve_pixels(i * 2 + par, par, i + 1)
            convolve_pixels(PIX_TURNS - 1, 0, PIX_TURNS // 2 + 1)
            pe.wait_ge(S["tab_c"], 1)
            pe.wait_ge(S["mask_in"], 16)

            def turn_quad(q, par):
                pe.wait_ge(S["xq_c"], q + 1)
                pe.wait_ge(S["pt_c"], q - 1 + CREDIT)
                for c in range(QUAD):
                    last = nc.tensor.matmul(ps[0:HW, 4 + par, c * BS:(c + 1) * BS], xq_s[:, par, c, :],
                                            ident_s[:, :], start=True, stop=True)
                last.then_inc(S["tq_p"], 1)

            per_chunk = CHUNK // QUAD
            with pe.Fori(0, C // CHUNK) as i:
                turn_quad(i * per_chunk, 0)
                pe.wait_ge(S["ks_c"], i * per_chunk + CREDIT)
                pe.wait_ge(S["tapc_c"], i + 1)
                for n in range(9):
                    if n >= 2:
                        pe.wait_ge(S[f"mb_e{n % 2}"], i * (5 - n % 2) + n // 2)
                    b0 = 2 * (n % 2)
                    flat = ps[0:HW + 1, b0:b0 + 2, :].rearrange("p b n -> p (b n)")
                    for m in range(9):
                        last = nc.tensor.matmul(flat[:, m * 2 * CHUNK:(m + 1) * 2 * CHUNK].rearrange("p (v c) -> p v c", v=2),
                                                mask_s[:, n * 9 + m, :],
                                                tapc_s[:, :, :],
                                                start=True, stop=True)
                    last.then_inc(S["mb_p"], 1)
                for k in range(per_chunk):
                    q, par = i * per_chunk + k, k % 2
                    if k + 1 < per_chunk:
                        turn_quad(q + 1, 1 - par)
                    if k == 0:
                        pe.wait_ge(S["mb_e0"], i * 5 + 5)
                        pe.wait_ge(S["mb_e1"], i * 4 + 4)
                    pe.wait_ge(S["pt_c"], q + 1 + CREDIT)
                    if k >= 2:
                        pe.wait_ge(S["ks_c"], q - 1 + CREDIT)
                    b0 = 6 if par == 0 else 2
                    for c in range(QUAD):
                        o = ps[:, b0 + c // 2, (c % 2) * 2 * HW:(c % 2 + 1) * 2 * HW]
                        last = nc.tensor.matmul(o, pt_s[:, par, c, :], m_s[:, k * QUAD + c, :, :]
                                                .rearrange("p v n -> p (v n)"), start=True, stop=True)
                    last.then_inc(S["cv_p"], 1)
            pe.wait_ge(S["phase_a"], 1)
            pe.wait_ge(S["ks_c"], QUADS + CREDIT)
            for h in range(HALVES):
                last = nc.tensor.matmul(ps[:, 6, 0:EXPERTS], ones_s[:, :], router_s[:, h, :], start=h == 0, stop=h == 1)
            last.then_inc(S["rm_p"], 1)

            def keys(g, par, i, first=False):
                pe.wait_ge(S[f"kq_in{par}"], 32 * (i + 1))
                if not first:
                    pe.wait_ge(S["a_c"], 2 * g)
                for n in range(2):
                    for k in range(2):
                        last = nc.tensor.matmul(ps[0:HW, n, :], se_w1_s[:, k, :],
                                                kq_s[:, par, k, 2 * n:2 * n + 2, :].rearrange("p b j -> p (b j)"),
                                                start=k == 0, stop=k == 1)
                    last.then_inc(S["se1_p"], 1)

            def spatial_1(g, par, i):
                pe.wait_ge(S[f"c_in{par}"], 64 * (i + 1))
                pe.wait_ge(S["e_c"], g + CREDIT)
                for h in range(HALVES):
                    nc.tensor.matmul(ps[:, 2 + h, 0:TOK], sa_w1_s[:, h, 0, :],
                                     kc_s[:, par, h, :, :].rearrange("p b n -> p (b n)"), start=True, stop=False)
                    nc.tensor.matmul(ps[:, 2 + h, 0:TOK], sa_w1_s[:, h, 1, :],
                                     xc_s[:, par, h, :, :].rearrange("p b n -> p (b n)"),
                                     start=False, stop=True).then_inc(S["sa1_p"], 1)

            def spatial_2(g):
                for h in range(HALVES):
                    pe.wait_ge(S["a2_c"], g * 2 + h + 1)
                    nc.tensor.matmul(ps[:, 2 + h, 0:TOK], sa_w2_s[:, h, :], a2_s[:, h, :],
                                     start=True, stop=True).then_inc(S["l2_p"], 1)

            def tap_logits(g, par):
                pe.wait_ge(S["a_c"], 2 * g + 2)
                pe.wait_ge(S["a2_c"], 2 * g + 1)
                for j in range(G * 2):
                    last = nc.tensor.matmul(ps[:, 2, TOK + j * D:TOK + (j + 1) * D],
                                            a_s[:, par, j // 2, (j % 2) * 128:(j % 2 + 1) * 128],
                                            se_w2_s[:, :], start=True, stop=True)
                last.then_inc(S["lg_p"], 1)

            def unmasked(g, par, i):
                pe.wait_ge(S["arx_c"], i)
                for n in range(2):
                    pe.wait_ge(S["msk_c"], 2 * g - 1 + n + CREDIT)
                    for b in range(2):
                        for h in range(HALVES):
                            last = nc.tensor.transpose(ps[:, 5 - n, b * C + h * 128:b * C + (h + 1) * 128],
                                                       arx_s[:, par * 8 + (2 * n + b) * 2 + h, :], ident_s[:, :])
                    last.then_inc(S["raw_p"], 1)

            def band(g, par, i):
                pe.wait_ge(S[f"v_in{par}"], 32 * i)
                pe.wait_ge(S["msk_c"], 2 * (g + 1) + CREDIT)
                pe.wait_ge(S["x1_c"], g + CREDIT)
                for b in range(G):
                    v0, v1 = vc_s[:, par, 0, b, :], vc_s[:, par, 1, b, :]
                    o = slice(b * HW, (b + 1) * HW)
                    nc.tensor.matmul(ps[:, 6, o], a0_s[:, b, 0:128], v0, start=True, stop=False,
                                     skip_group_check=True)
                    nc.tensor.matmul(ps[96:128, 6, o], a1_s[:, b, 0:32], v1, start=False, stop=True,
                                     skip_group_check=True)
                    nc.tensor.matmul(ps[:, 7, o], a1_s[:, b, 32:160], v1, start=True, stop=False,
                                     skip_group_check=True)
                    last = nc.tensor.matmul(ps[0:4, 7, o], a0_s[:, b, 128:132], v0, start=False, stop=True,
                                            skip_group_check=True)
                last.then_inc(S["band_p"], 1)

            def pe_turn(i, first=False, front=True, back=True, late=True):
                if front:
                    keys(2 * i, 0, i, first)
                if late:
                    band(2 * i - 3, 1, i - 1)
                if front:
                    spatial_1(2 * i, 0, i)
                    tap_logits(2 * i, 0)
                    spatial_2(2 * i)
                if back:
                    unmasked(2 * i - 2, 0, i)
                if front:
                    keys(2 * i + 1, 1, i)
                if back:
                    band(2 * i - 2, 0, i)
                if front:
                    spatial_1(2 * i + 1, 1, i)
                    tap_logits(2 * i + 1, 1)
                    spatial_2(2 * i + 1)
                if back:
                    unmasked(2 * i - 1, 1, i)

            pe_turn(0, first=True, back=False, late=False)
            pe.wait_ge(S["rw_c"], 1)
            pe_turn(1, late=False)
            with pe.Fori(2, PAIRS) as i:
                pe_turn(i)
            pe_turn(PAIRS, front=False)
            band(GROUPS - 1, 1, PAIRS)

            def token_rows(r, slot):
                pe.wait_ge(S["xs_c"], r + 1)
                if not isinstance(r, int) or r > 2:
                    pe.wait_ge(S["xft_c"], r - 2 + CREDIT)
                for s in range(SUBS):
                    for h in range(HALVES):
                        last = nc.tensor.transpose(
                            ps[:, 2 * slot + s // 2, (s % 2) * C + h * 128:(s % 2) * C + (h + 1) * 128],
                            xs_s[slot][:, h, s * 128:(s + 1) * 128], ident_s[:, :])
                last.then_inc(S["t1_p"], 1)

            def token_logits(r, slot):
                pe.wait_ge(S["lgr_c"], r + CREDIT)
                for s in range(SUBS):
                    for h in range(HALVES):
                        last = nc.tensor.matmul(ps[:, 6, s * EXPERTS:(s + 1) * EXPERTS],
                                                xs_s[slot][:, h, s * 128:(s + 1) * 128], router_s[:, h, :],
                                                start=h == 0, stop=h == 1)
                last.then_inc(S["rl_p"], 1)

            def places(r):
                pe.wait_ge(S["tot_c"], r + 1)
                nc.tensor.matmul(ps[:, 7, 0:EXPERTS], before_s[:, :], tot_s[:, :], start=True, stop=True)
                nc.tensor.matmul(ps[:, 7, EXPERTS:2 * EXPERTS], ones_s[:, :], tot_s[:, :],
                                 start=True, stop=True).then_inc(S["tri_p"], 1)

            token_rows(0, 0)
            token_rows(1, 1)
            token_logits(0, 0)
            with pe.Fori(0, TURNS // 3 - 1) as i:
                for k in range(3):
                    token_rows(i * 3 + k + 2, (k + 2) % 3)
                    token_logits(i * 3 + k + 1, (k + 1) % 3)
                    places(i * 3 + k)
            for r in range(TURNS - 3, TURNS):
                if r + 2 < TURNS:
                    token_rows(r + 2, (r + 2) % 3)
                if r + 1 < TURNS:
                    token_logits(r + 1, (r + 1) % 3)
                places(r)

            def turn_rows(t, par, come, first=False):
                pe.wait_ge(S[f"rin{par}"], 16 * come)
                if not first:
                    pe.wait_ge(S["xlo_c"], t - 1)
                for h in range(HALVES):
                    for s in range(2):
                        last = nc.tensor.transpose(ps[:, par, h * SLOTS + s * 128:h * SLOTS + (s + 1) * 128],
                                                   rin_s[:, par, s, h * 128:(h + 1) * 128], ident_s[:, :])
                last.then_inc(S["tt_p"], 1)

            def up(t, par, first=False):
                e = pe.value_load(tabi_s[0:1, 1, bass.ds(t, 1)], min_val=0, max_val=EXPERTS - 1)
                pe.wait_ge(S["xlo_c"], t + 1)
                if not first:
                    pe.wait_ge(S["gel_c"], 4 * (t - 1) + CREDIT)
                pe.sem_inc(S["settle_p"], 1)
                for j in range(KB):
                    o = ps[:, 2 + 2 * par + j // 2, (j % 2) * SLOTS:(j % 2 + 1) * SLOTS]
                    n = 0
                    for k in range(HALVES):
                        for a, b in ((0, 0), (0, 1), (1, 0)):
                            last = nc.tensor.matmul(o, w_s[:, a, bass.ds(e * (4 * PIECE) + (k * HID + j * 128), 128)],
                                                    xh_s[:, par, b, k * SLOTS:(k + 1) * SLOTS],
                                                    start=n == 0, stop=n == 5)
                            n += 1
                    last.then_inc(S["h_p"], 1)

            def down(t, par):
                e = pe.value_load(tabi_s[0:1, 1, bass.ds(t, 1)], min_val=0, max_val=EXPERTS - 1)
                pe.wait_ge(S["hlo_c"], t + 1)
                pe.wait_ge(S["yo_c"], t - 1 + CREDIT)
                for s in range(2):
                    n = 0
                    for j in range(KB):
                        for a, b in ((0, 0), (0, 1), (1, 0)):
                            last = nc.tensor.matmul(ps[:, 6 + par, s * C:(s + 1) * C],
                                                    hh_s[:, par, a, j, s * 128:(s + 1) * 128],
                                                    w_s[:, b, bass.ds(e * (4 * PIECE) + (2 * PIECE + j * C), C)],
                                                    start=n == 0, stop=n == 11)
                            n += 1
                last.then_inc(S["w2_p"], 1)

            pe.wait_ge(S["tab_r"], 1)
            pe.wait_ge(S["wlo_c"], PIECES)
            turn_rows(0, 0, 1, first=True)
            turn_rows(1, 1, 1, first=True)
            up(0, 0, first=True)
            with pe.Fori(0, TILES // 2 - 1) as i:
                for k in range(2):
                    t = i * 2 + 1 + k
                    turn_rows(t + 1, k, i + 2)
                    up(t, 1 - k)
                    down(t - 1, k)
            up(TILES - 1, 1)
            down(TILES - 2, 0)
            down(TILES - 1, 1)
            with pe.Fori(0, TURNS) as g:
                pe.wait_ge(S["mix_c"], g + 1)
                pe.wait_ge(S["fin_c"], g + CREDIT)
                for h in range(HALVES):
                    for s in range(SUBS):
                        last = nc.tensor.transpose(ps[:, h, s * 128:(s + 1) * 128], mix_s[:, s, h * 128:(h + 1) * 128],
                                                   ident_s[0:128, 0:128])
                last.then_inc(S["back_p"], 1)

        @block.vector
        def _(dve):
            done = {"before": 0, "links": 0, "roots": 0}

            def start(ins):
                done["links"] += 1
                ins.then_inc(S["ch_d"], 1)

            def settled():
                dve.wait_ge(S["ch_d"], done["before"] + done["links"])

            def link(ins):
                start(ins)
                settled()

            def inverse_root(var, eps, scale, dst):
                nc.vector.tensor_scalar(dst, var, scale, eps, ALU.mult, ALU.add).then_inc(S["var_c"], 1)
                done["roots"] += 1
                dve.wait_ge(S["root_c"], done["roots"])
                link(nc.vector.reciprocal(dst, dst))

            early, unroll = 60, 15

            def pixel_statistics(first, pixels, run, chans, part):
                with dve.Fori(0, pixels // run) as i:
                    for k in range(run):
                        at = bass.ds(i * run + (first + k), 1)
                        ins = nc.vector.bn_stats(bn_s[:, at, part:part + 2, :].rearrange("p n e s -> p (n e s)"),
                                                 by_pixel(big)[:, at, chans].rearrange("p n c -> p (n c)"))
                    ins.then_inc(S["bn_c"], 1)

            dve.wait_ge(S["x_in0"], 16)
            pixel_statistics(0, early, unroll, slice(0, 128), 0)
            dve.wait_ge(S["x_in1"], 16)
            pixel_statistics(0, early, unroll, slice(128, C), 2)
            pixel_statistics(early, HW - early, 7, slice(0, C), 0)
            dve.wait_ge(S["bn_c"], 2 * early // unroll + (HW - early) // 7)
            mean, rstd, nmr = (stats[:, k, :] for k in range(3))
            for at, parts in ((slice(0, early), 2 * HALVES), (slice(early, HW), 2)):
                means, spreads = bn_s[:, at, 0:parts, 1], bn_s[:, at, 0:parts, 2]
                n = at.stop - at.start
                link(nc.vector.reduce_sum(mean[:, at], means, axis=AX.X))
                link(nc.vector.tensor_scalar(mean[:, at], mean[:, at], 1.0 / parts, None, ALU.mult))
                link(nc.vector.tensor_tensor(means, means, mean[:, at].unsqueeze(2).to_broadcast([128, n, parts]),
                                             ALU.subtract))
                link(nc.vector.tensor_tensor(means, means, means, ALU.mult))
                link(nc.vector.scalar_tensor_tensor(spreads, spreads, float(parts) / C, means, ALU.mult, ALU.add))
                link(nc.vector.reduce_sum(rstd[:, at], spreads, axis=AX.X))
                link(nc.vector.tensor_scalar(rstd[:, at], rstd[:, at], 1.0 / parts, None, ALU.mult))
            inverse_root(rstd, LN_C_EPS, 1.0, rstd)
            nc.vector.scalar_tensor_tensor(nmr, mean, -1.0, rstd, ALU.mult, ALU.mult).then_inc(S["norm"], 1)
            dve.wait_ge(S["w_in"], W_IN)

            def xn_back(i, par):
                dve.wait_ge(S["xp_c"], i + 1)
                dve.sem_inc(S["settle_v"], 1)
                nc.vector.tensor_copy(by_pixel(big)[:, bass.ds(i * PIX, PIX), :], xp_s[:, par]).then_inc(S["xb_c"], 1)

            def k1_out(i, par):
                dve.wait_ge(S["k1_c"], i + 1 + CREDIT)
                for k in range(0, PIX, 2):
                    n = min(2, PIX - k)
                    ins = nc.vector.tensor_tensor(by_pixel(pool_)[:, bass.ds(i * PIX + k, n), :],
                                                  ps[:, 4 + 2 * par + k // 2, 0:n * C].rearrange("p (k c) -> p k c", k=n),
                                                  kb_s[:, bass.ds(i * PIX + k, n)].unsqueeze(2).to_broadcast([128, n, C]),
                                                  ALU.add)
                ins.then_inc(S["k1_ev"], 1)

            xn_back(0, 0)
            xn_back(1, 1)
            with dve.Fori(0, PIX_TURNS // 2 - 1) as i:
                for par in range(2):
                    k1_out(i * 2 + par, par)
                    xn_back(i * 2 + par + 2, par)
            k1_out(PIX_TURNS - 3, 0)
            xn_back(PIX_TURNS - 1, 0)
            k1_out(PIX_TURNS - 2, 1)
            k1_out(PIX_TURNS - 1, 0)
            for p, ab in ((se_bn_s[:, :].unsqueeze(1), se_ab[:, :].unsqueeze(1)), (sa_bn_s, sa_ab)):
                gg, bb, mm, vv = (p[:, :, k:k + 1] for k in range(4))
                inverse_root(vv, BN_EPS, 1.0, ab[:, :, 0:1])
                link(nc.vector.tensor_tensor(ab[:, :, 0:1], ab[:, :, 0:1], gg, ALU.mult))
                link(nc.vector.tensor_tensor(ab[:, :, 2:3], ab[:, :, 0:1], mm, ALU.mult))
                link(nc.vector.tensor_tensor(ab[:, :, 1:2], bb, ab[:, :, 2:3], ALU.subtract))
            link(nc.vector.tensor_scalar(alpha_s[:, 1:2], alpha_s[:, 0:1], -1.0, 1.0, ALU.mult, ALU.add))
            dve.wait_ge(S["tab_in"], 48)
            link(nc.vector.memset(taph_s, 0.0))
            inverse_root(tapbn_s[:, 1, :], BN_EPS, 1.0, tapbn_s[:, 1, :])
            link(nc.vector.tensor_tensor(tapbn_s[:, 0, :], tapbn_s[:, 0, :], tapbn_s[:, 1, :], ALU.mult))
            link(nc.vector.tensor_scalar(tapbn_s[:, 0, :], tapbn_s[:, 0, :], taprow_s[:, 0:1], taprow_s[:, 1:2],
                                         ALU.mult, ALU.add))
            link(nc.vector.tensor_tensor(taps_s[:, 1, :], taps_s[:, 1, :], tapbn_s[:, 0, :], ALU.mult))
            for k in range(3):
                part = taph_s[32 * k:32 * k + 11]
                left = taps_s if k == 0 else tapr_s
                link(nc.vector.tensor_copy(part, left))
                if k < 2:
                    link(nc.vector.tensor_tensor(tapr_s, left, part, ALU.subtract))
            dve.wait_ge(S["k1_outm"], 16)
            nc.vector.memset(pt_s[:, :, :, :], 1.0).then_inc(S["tab_c"], 1)
            with dve.Fori(0, C // CHUNK) as i:
                dve.wait_ge(S["mb_p"], i * 9 + CREDIT)
                nc.vector.tensor_copy(tapc_s[:, :, :], taph_s[:, :, bass.ds(i * CHUNK, CHUNK)]).then_inc(S["tapc_c"], 1)
                for n in range(1, 9, 2):
                    dve.wait_ge(S["mb_p"], i * 9 + n + 1 + CREDIT)
                    if n == 1:
                        dve.wait_ge(S["cv_p"], i * 8 + CREDIT)
                    flat = ps[0:HW + 1, 2:4, :].rearrange("p b n -> p (b n)")[:, 0:9 * 2 * CHUNK]
                    nc.vector.tensor_copy(m_s[:, :, :, n * 9:(n + 1) * 9].rearrange("p c v m -> p m v c"),
                                          flat.rearrange("p (m v c) -> p m v c", m=9, v=2)).then_inc(S["mb_e1"], 1)
                for k in range(CHUNK // QUAD):
                    q, par = i * (CHUNK // QUAD) + k, k % 2
                    dve.wait_ge(S["tq_p"], q + 1 + CREDIT)
                    dve.wait_ge(S["cv_p"], q - 1 + CREDIT)
                    nc.vector.tensor_copy(pt_s[0:HW, par, :, :].rearrange("p c b -> p (c b)"),
                                          ps[0:HW, 4 + par, :]).then_inc(S["pt_c"], 1)
            dve.wait_ge(S["k1_out1"], 16 * (QUADS // DEPTH))
            dve.wait_ge(S["cv_p"], QUADS + CREDIT)
            nc.vector.memset(ones_s[:, :], 1.0)
            link(nc.vector.memset(a_s[:, :, :], 1.0))
            link(nc.vector.memset(ap_s[:, :, :], 0.0))
            nc.vector.memset(t1_s[:, :, :], 0.0).then_inc(S["phase_a"], 1)
            dve.wait_ge(S["phase_a"], 1)
            dve.wait_ge(S["rm_p"], 1)
            for h in range(HALVES):
                ins = nc.vector.scalar_tensor_tensor(router_s[:, h, :], ps[:, 6, 0:EXPERTS], -1.0 / C, router_s[:, h, :],
                                                     ALU.mult, ALU.add)
            ins.then_inc(S["rw_c"], 1)

            def pixel_maximum(g, par):
                for h in range(HALVES):
                    dve.wait_ge(S["l2_p"], g * 2 + h + 1)
                    ins = nc.vector.reduce_max(sm_s[:, par, 0, h * G:(h + 1) * G],
                                               ps[:, 2 + h, 0:TOK].rearrange("p (b n) -> p b n", b=G), axis=AX.X)
                dve.wait_ge(S["lg_p"], g + 1 + CREDIT)
                ins = nc.vector.tensor_copy(lg_s[:, par * G * 2:(par + 1) * G * 2, :],
                                            ps[:, 2, TOK:TOK + G * 2 * D].rearrange("p (j d) -> p j d", d=D))
                link(ins)
                bb = sa_b2_s[:, :].unsqueeze(2).to_broadcast([128, HALVES, G])
                m3 = sm_s[:, par].rearrange("p k (h b) -> p k h b", h=HALVES)
                link(nc.vector.tensor_tensor(m3[:, 1], m3[:, 0], bb, ALU.add))
                nc.vector.tensor_tensor(m3[:, 2], bb, m3[:, 1], ALU.subtract).then_inc(S["l2m_c"], 1)

            def mask_bands(g):
                for n in range(2):
                    dve.wait_ge(S["raw_p"], g * 2 + n + 1 + CREDIT)
                    raw = ps[:, 5 - n, :].rearrange("p (b c) -> p b c", b=2)
                    nc.vector.tensor_tensor(a0_s[:, 2 * n:2 * n + 2, :], raw[:, :, 0:BAND0],
                                            band_s[:, 0:BAND0].unsqueeze(1).to_broadcast([128, 2, BAND0]), ALU.mult)
                    nc.vector.tensor_tensor(a1_s[:, 2 * n:2 * n + 2, :], raw[:, :, BAND1_START:C],
                                            band_s[:, BAND0:].unsqueeze(1).to_broadcast([128, 2, BAND1]),
                                            ALU.mult).then_inc(S["msk_c"], 1)

            def x1_rows(g):
                return x1_s[:, :, bass.ds(g * TOK, TOK)]

            def without_band(g, par):
                dve.wait_ge(S["e_c"], g + 1 + CREDIT)
                sm, e3 = sm_s[:, par], e_s[:, par].rearrange("p h b n -> p (h b) n")
                nc.vector.reciprocal(sm[:, 0, :], sm[:, 3, :])
                link(nc.vector.tensor_tensor(e3, e3, xc_s[:, par].rearrange("p h b n -> p (h b) n"), ALU.mult))
                link(nc.vector.tensor_tensor(e3, e3, sm[:, 0, :].unsqueeze(2).to_broadcast([128, HALVES * G, HW]),
                                             ALU.mult))
                link(nc.vector.tensor_tensor(e3, e3, kc_s[:, par].rearrange("p h b n -> p (h b) n"), ALU.add))
                dve.wait_ge(S["r1_c"], g + 1)
                nc.vector.scalar_tensor_tensor(x1_rows(g), e_s[:, par].rearrange("p h b n -> p h (b n)"),
                                               alpha_s[:, 1:2], kr_s[:, par].rearrange("p h b n -> p h (b n)"),
                                               ALU.mult, ALU.add).then_inc(S["t_c"], 1)

            def add_band(g):
                dve.wait_ge(S["band_p"], g + 1 + CREDIT)
                dve.wait_ge(S["t_c"], g + 1 + CREDIT)
                rows = x1_rows(g)
                nc.vector.tensor_tensor(rows, rows, ps[:, 6:8, 0:TOK], ALU.add).then_inc(S["x1_c"], 1)

            wide = [128, G * 4, D]

            def tap_maximum(i):
                link(nc.vector.reduce_max(st_s[:, 0, :], lg_s, axis=AX.X))
                nc.vector.tensor_tensor(lg_s, lg_s, st_s[:, 0, :].unsqueeze(2).to_broadcast(wide),
                                        ALU.subtract).then_inc(S["lgs_c"], 1)

            def tap_weights(i):
                dve.wait_ge(S["ex_c"], i + 1)
                link(nc.vector.reduce_sum(st_s[:, 1, :], lg_s, axis=AX.X))
                link(nc.vector.reciprocal(st_s[:, 2, :], st_s[:, 1, :]))
                link(nc.vector.tensor_scalar(st_s[:, 3, :], st_s[:, 2, :], alpha_s[:, 0:1], None, ALU.mult))
                link(nc.vector.tensor_tensor(ap_s[:, :, 3:12], lg_s, st_s[:, 3, :].unsqueeze(2).to_broadcast(wide),
                                             ALU.mult))
                for r in range(4):
                    a = ap_s[:, :, 3 - r:15 - r]
                    if r == 0:
                        link(nc.vector.tensor_scalar(t1_s[:, :, 0:12], a, rot_s[:, 0:1], None, ALU.mult))
                    else:
                        link(nc.vector.scalar_tensor_tensor(t1_s[:, :, 0:12], a, rot_s[:, r:r + 1], t1_s[:, :, 0:12],
                                                            ALU.mult, ALU.add))
                link(nc.vector.tensor_copy(t1_s[:, :, 16:28], t1_s[:, :, 0:12]))
                link(nc.vector.tensor_scalar(ar_s, t1_s[:, :, 0:16], rot_s[:, 4:5], None, ALU.mult))
                for r in range(1, 4):
                    ins = nc.vector.scalar_tensor_tensor(ar_s, t1_s[:, :, 16 - 4 * r:32 - 4 * r], rot_s[:, 4 + r:5 + r],
                                                         ar_s, ALU.mult, ALU.add)
                    if r < 3:
                        link(ins)
                    else:
                        ins.then_inc(S["ar_c"], 1)

            def dve_turn(i, front=True, back=True, late=True):
                if late:
                    add_band(2 * i - 3)
                if front:
                    pixel_maximum(2 * i, 0)
                if back:
                    mask_bands(2 * i - 2)
                if front:
                    without_band(2 * i, 0)
                if back:
                    add_band(2 * i - 2)
                if front:
                    pixel_maximum(2 * i + 1, 1)
                    tap_maximum(i)
                if back:
                    mask_bands(2 * i - 1)
                if front:
                    tap_weights(i)
                    without_band(2 * i + 1, 1)

            dve_turn(0, back=False, late=False)
            dve_turn(1, late=False)
            base, per = done["links"], 23
            with dve.Fori(2, PAIRS) as i:
                done["before"], done["links"] = (i - 2) * per + base, 0
                dve_turn(i)
            assert done["links"] == per, done["links"]
            done["before"], done["links"] = base + per * (PAIRS - 2), 0
            dve_turn(PAIRS, front=False)
            add_band(GROUPS - 1)
            link(nc.vector.tensor_copy(base_s[:, :], region_s[:, :]))

            def low_piece(n, slot):
                dve.wait_ge(S["whi_c"], n + 1)
                cols = bass.ds(n * PIECE, PIECE)
                nc.vector.scalar_tensor_tensor(w_s[:, 1, cols], stage_s[:, slot], WSCALE, w_s[:, 0, cols],
                                               ALU.mult, ALU.subtract).then_inc(S["wlo_c"], 1)

            def row_part(slot, s):
                return nc.vector.bn_stats(bs_s[:, slot, s, 0:6],
                                          ps[:, 2 * slot + s // 2, (s % 2) * C:(s % 2 + 1) * C])

            def row_total(slot):
                bs = bs_s[:, slot]
                dve.sem_inc(S["settle_v"], 1)
                for s in range(SUBS):
                    ins = nc.vector.bn_aggr(bs[:, s, 6:8], bs[:, s, 0:6])
                link(ins)
                nc.vector.tensor_scalar(bs[:, :, 8:9], bs[:, :, 7:8], LN_T_EPS, None, ALU.add).then_inc(S["var2_c"], 1)

            def row_offset(r, slot):
                bs = bs_s[:, slot]
                dve.wait_ge(S["rstd_c"], r + 1)
                nc.vector.scalar_tensor_tensor(bs[:, :, 9:10], bs[:, :, 6:7], -1.0, bs[:, :, 8:9],
                                               ALU.mult, ALU.mult).then_inc(S["nmr_c"], 1)

            def router_turn(r, i, slot, ahead=True):
                bs, after = bs_s[:, slot], (slot + 1) % 3
                if ahead:
                    dve.wait_ge(S["t1_p"], r + 2)
                dve.wait_ge(S["rl_p"], r + 1 + CREDIT)
                lgt = ps[:, 6, 0:SUBS * EXPERTS].rearrange("p (s e) -> p s e", s=SUBS)
                nc.vector.tensor_tensor(pr_s[:, :, 0, :], lgt, bs[:, :, 8:9].to_broadcast([128, SUBS, EXPERTS]),
                                        ALU.mult).then_inc(S["lgr_c"], 1)
                if ahead:
                    row_part(after, 0)
                dve.wait_ge(S["lgr_c"], r + 1 + CREDIT)
                start(nc.vector.tensor_tensor(pr_s[:, :, 0, :], pr_s[:, :, 0, :],
                                              router_bias_s[:, :].unsqueeze(1).to_broadcast([128, SUBS, EXPERTS]),
                                              ALU.add))
                if ahead:
                    row_part(after, 1)
                settled()
                m1 = bs[:, :, 7:8]
                link(nc.vector.reduce_max(m1.rearrange("p s o -> p (s o)"), pr_s[:, :, 0, :], axis=AX.X))
                nc.vector.tensor_tensor(pr_s[:, :, 1, :], pr_s[:, :, 0, :], m1.to_broadcast([128, SUBS, EXPERTS]),
                                        ALU.subtract).then_inc(S["probs_c"], 1)
                if ahead:
                    link(row_part(after, 2))
                    row_total(after)
                dve.wait_ge(S["ex2_c"], r + 1)
                link(nc.vector.reduce_sum(m1.rearrange("p s o -> p (s o)"), pr_s[:, :, 2, :], axis=AX.X))
                link(nc.vector.reciprocal(m1, m1))
                link(nc.vector.tensor_tensor(pr_s[:, :, 1, :], pr_s[:, :, 2, :], m1.to_broadcast([128, SUBS, EXPERTS]),
                                             ALU.mult))
                for s in range(SUBS):
                    mine = pr_s[:, s, 1, :].unsqueeze(2).to_broadcast([128, EXPERTS, EXPERTS])
                    other = pr_s[:, s, 1, :].unsqueeze(1).to_broadcast([128, EXPERTS, EXPERTS])
                    nc.vector.tensor_tensor(cmp_s[:, s, :, 0, :], other, mine, ALU.is_gt)
                    ins = nc.vector.tensor_tensor(cmp_s[:, s, :, 1, :], other, mine, ALU.is_equal)
                link(ins)
                link(nc.vector.tensor_tensor(cmp_s[:, :, :, 1, :], cmp_s[:, :, :, 1, :],
                                             lower_s[:, :].rearrange("p (e j) -> p e j", j=EXPERTS).unsqueeze(1)
                                             .to_broadcast([128, SUBS, EXPERTS, EXPERTS]), ALU.mult))
                link(nc.vector.tensor_reduce(pr_s[:, :, 3, :],
                                             cmp_s.rearrange("p s e k j -> p s e (k j)"), axis=AX.X, op=ALU.add))
                nc.vector.tensor_scalar(hot_s[:, 0], pr_s[:, :, 3, :], 0.0, None, ALU.is_equal)
                nc.vector.tensor_scalar(hot_s[:, 1], pr_s[:, :, 3, :], 1.0, None, ALU.is_equal)
                link(nc.vector.tensor_scalar(hot_s[:, 2], pr_s[:, :, 3, :], 1.5, None, ALU.is_lt))
                nc.vector.reduce_sum(tot_s[:, :], hot_s[:, 2].rearrange("p s e -> p e s"),
                                     axis=AX.X).then_inc(S["tot_c"], 1)
                for k in range(2):
                    ins = nc.vector.tensor_tensor(pick_s[:, k], pr_s[:, :, 1, :], hot_s[:, k], ALU.mult)
                start(ins)
                if ahead:
                    row_offset(r + 1, after)
                low_piece(r, slot)
                settled()
                dve.wait_ge(S["tri_p"], r + 1)
                start(nc.vector.tensor_tensor(at_s[:, 0], base_s[:, :], ps[:, 7, 0:EXPERTS], ALU.add))
                for s in range(2):
                    nc.vector.reduce_sum(wt_s[:, bass.ds(r * 6 + 3 * s, 3)], pick_s[:, s], axis=AX.X)
                    settled()
                    start(nc.vector.tensor_tensor(at_s[:, s + 1], at_s[:, s], hot_s[:, 2, s], ALU.add))
                start(nc.vector.tensor_tensor(base_s[:, :], base_s[:, :], ps[:, 7, EXPERTS:2 * EXPERTS], ALU.add))
                settled()
                for k in range(2):
                    ins = nc.vector.tensor_tensor(pick_s[:, 2 + k], at_s[:, :, :], hot_s[:, k], ALU.mult)
                link(ins)
                for k in range(2):
                    ins = nc.vector.reduce_sum(pos_s[:, bass.ds(r * 6 + 3 * k, 3)], pick_s[:, 2 + k], axis=AX.X)
                link(ins)
                dve.wait_ge(S[f"sent{slot}"], i + CREDIT)
                dve.sem_inc(S["settle_v"], 1)
                nc.vector.tensor_copy(idx_s[:, slot, :], pos_s[:, bass.ds(r * 6, 6)]).then_inc(S["idx_c"], 1)

            dve.wait_ge(S["t1_p"], 1)
            for s in range(SUBS):
                ins = row_part(0, s)
            link(ins)
            row_total(0)
            row_offset(0, 0)
            base = done["before"] + done["links"]
            per_r = 18
            with dve.Fori(0, TURNS // 3 - 1) as i:
                done["before"], done["links"] = i * (3 * per_r) + base, 0
                for k in range(3):
                    router_turn(i * 3 + k, i, k)
            assert done["links"] == 3 * per_r, done["links"]
            done["before"], done["links"] = base + per_r * (TURNS - 3), 0
            for r in range(TURNS - 3, TURNS):
                router_turn(r, r // 3, r % 3, ahead=r + 1 < TURNS)
            nc.vector.memset(zero_s[:, :, :], 0.0)
            nc.vector.tensor_copy(tili_s[:, 1, :], base_s[:, :]).then_inc(S["ends_c"], 1)
            for n in range(TURNS, PIECES):
                low_piece(n, n % 3)
            cnt, tiles, ends, delta = (til_s[:, k, :] for k in range(4))
            link(nc.vector.tensor_tensor(cnt, base_s[:, :], region_s[0:128, :], ALU.subtract))
            link(nc.vector.tensor_scalar(cnt, cnt, float(SLOTS - 1), None, ALU.add))
            link(nc.vector.tensor_copy(tili_s[:, 0, :], cnt))
            link(nc.vector.tensor_scalar(tili_s[:, 0, :], tili_s[:, 0, :], SLOTS.bit_length() - 1, None,
                                         ALU.arith_shift_right))
            link(nc.vector.tensor_copy(tiles, tili_s[:, 0, :]))
            link(nc.vector.tensor_copy(ends, tiles))
            for e in range(1, EXPERTS):
                link(nc.vector.tensor_tensor(ends[:, e:e + 1], ends[:, e:e + 1], ends[:, e - 1:e], ALU.add))
            link(nc.vector.tensor_tensor(delta, ends, tiles, ALU.subtract))
            link(nc.vector.scalar_tensor_tensor(delta, delta, float(SLOTS), region_s[0:128, :], ALU.mult, ALU.subtract))
            link(nc.vector.tensor_tensor(cnt[:, 1:EXPERTS], delta[:, 1:EXPERTS], delta[:, 0:EXPERTS - 1], ALU.subtract))
            full = [1, TILES, EXPERTS]
            link(nc.vector.tensor_tensor(tcmp_s[:, 0], ends[0:1, :].unsqueeze(1).to_broadcast(full),
                                         turn_s[:, :].unsqueeze(2).to_broadcast(full), ALU.is_le))
            link(nc.vector.tensor_tensor(tcmp_s[:, 1], tcmp_s[:, 0], tiles[0:1, :].unsqueeze(1).to_broadcast(full), ALU.mult))
            nc.vector.reduce_sum(tab_s[:, 0, :], tcmp_s[:, 0], axis=AX.X)
            link(nc.vector.reduce_sum(tab_s[:, 1, :], tcmp_s[:, 1], axis=AX.X))
            nc.vector.tensor_scalar(tab_s[:, 2, :], tab_s[:, 0, :], float(EXPERTS), float(SLOTS), ALU.is_lt, ALU.mult)
            link(nc.vector.tensor_tensor(tab_s[:, 1, :], turn_s[:, :], tab_s[:, 1, :], ALU.subtract))
            link(nc.vector.tensor_tensor(tab_s[:, 1, :], tab_s[:, 1, :], tab_s[:, 2, :], ALU.mult))
            link(nc.vector.scalar_tensor_tensor(tab_s[:, 2, :], tab_s[:, 0, :], float(REGION), tab_s[:, 1, :],
                                                ALU.mult, ALU.add))
            link(nc.vector.tensor_scalar(tab_s[:, 3, :], tab_s[:, 0, :], float(EXPERTS - 1), None, ALU.min))
            link(nc.vector.tensor_copy(tabi_s[:, 0, :], tab_s[:, 2, :]))
            nc.vector.tensor_copy(tabi_s[:, 1, :], tab_s[:, 3, :]).then_inc(S["base_c"], 1)
            for k in range(3):
                dve.wait_ge(S[f"scat{k}"], 96 * (TURNS // 3))
            dve.wait_ge(S["pad_out"], 16 * (EXPERTS + 1))
            dve.wait_ge(S["b2_in"], 16)
            dve.sem_inc(S["tab_r"], 1)

            def split_rows(t, par):
                dve.wait_ge(S["xhi_c"], t + 1)
                nc.vector.tensor_tensor(xh_s[:, par, 1, :], ps[:, par, :], xh_s[:, par, 0, :],
                                        ALU.subtract).then_inc(S["xlo_c"], 1)

            def split_hidden(t, par):
                dve.wait_ge(S["gel_c"], 4 * (t + 1) + CREDIT)
                hi, lo = (hh_s[:, par, k].rearrange("p j n -> p (j n)") for k in range(2))
                nc.vector.tensor_copy(hi, hf_s).then_inc(S["hhi_c"], 1)
                dve.wait_ge(S["hhi_c"], t + 1)
                nc.vector.tensor_tensor(lo, hf_s, hi, ALU.subtract).then_inc(S["hlo_c"], 1)

            def scaled_rows(t, par, k):
                e = dve.value_load(tabi_s[0:1, 1, bass.ds(t, 1)], min_val=0, max_val=EXPERTS - 1)
                dve.wait_ge(S["w2_p"], t + 1 + CREDIT)
                dve.wait_ge(S[f"yst{par}"], 16 * k + CREDIT)
                nc.vector.scalar_tensor_tensor(yo_s[:, par], ps[:, 6 + par, :].rearrange("p (s c) -> p s c", s=2),
                                               1.0 / WSCALE, b2_s[:, bass.ds(e * C, C)].unsqueeze(1)
                                               .to_broadcast([128, 2, C]), ALU.mult, ALU.add).then_inc(S["yo_c"], 1)

            split_rows(0, 0)
            split_rows(1, 1)
            pos, new, other = pos_s[:, :], step_s[:, 0, :], step_s[:, 1, :]
            link(nc.vector.tensor_scalar(new, pos, delta[:, 0:1], None, ALU.add))
            for e in range(1, EXPERTS):
                link(nc.vector.tensor_scalar(other, pos, float(e * REGION), cnt[:, e:e + 1], ALU.is_ge, ALU.mult))
                link(nc.vector.tensor_tensor(new, new, other, ALU.add))
            link(nc.vector.tensor_copy(pos, new))
            with dve.Fori(0, TILES // 2 - 1) as i:
                for k in range(2):
                    t = i * 2 + 1 + k
                    split_hidden(t - 1, k)
                    dve.wait_ge(S["h_p"], 4 * t)
                    split_rows(t + 1, k)
                    scaled_rows(t - 1, k, i)
            for t in range(TILES - 2, TILES):
                split_hidden(t, t % 2)
                scaled_rows(t, t % 2, t // 2)

            def ask(g, par):
                dve.sem_inc(S["settle_v"], 1)
                nc.vector.tensor_copy(idx_s[:, par, :], pos_s[:, bass.ds(g * 6, 6)]).then_inc(S["idx2_c"], 1)

            def combine(g, par, come):
                dve.wait_ge(S[f"gat{par}"], 96 * come)
                dve.wait_ge(S["back_p"], g + CREDIT)
                dve.sem_inc(S["settle_v"], 1)
                w0, w1 = (wt_s[:, bass.ds(g * 6 + 3 * k, 3)].unsqueeze(2).to_broadcast([128, SUBS, C]) for k in range(2))
                nc.vector.tensor_tensor(mix_s[:, :, :], got_s[:, par, 0:3, :], w0, ALU.mult).then_inc(S["mx0_c"], 1)
                nc.vector.tensor_tensor(got_s[:, par, 3:6, :], got_s[:, par, 3:6, :], w1, ALU.mult).then_inc(S["mx0_c"], 1)
                dve.wait_ge(S["mx0_c"], 2 * g + 2)
                nc.vector.tensor_tensor(mix_s[:, :, :], mix_s[:, :, :], got_s[:, par, 3:6, :],
                                        ALU.add).then_inc(S["mix_c"], 1)
                dve.wait_ge(S["mix_c"], g + 1)

            def finish(g):
                x1 = x1_s[:, :, bass.ds(g * ROWS, ROWS)]
                dve.wait_ge(S["back_p"], g + 1 + CREDIT)
                nc.vector.tensor_tensor(x1, x1, ps[:, 0:2, 0:ROWS], ALU.add).then_inc(S["fin_c"], 1)

            ask(0, 0)
            ask(1, 1)
            with dve.Fori(0, TURNS // 2 - 1) as i:
                for par in range(2):
                    combine(i * 2 + par, par, i + 1)
                    ask(i * 2 + par + 2, par)
                    finish(i * 2 + par)
            for g in range(TURNS - 3, TURNS):
                combine(g, g % 2, g // 2 + 1)
                if g == TURNS - 3:
                    ask(TURNS - 1, g % 2)
                finish(g)

        @block.scalar
        def _(act):
            act.wait_ge(S["var_c"], 1)
            nc.scalar.activation(stats[:, 1, :], stats[:, 1, :], ACT.Sqrt).then_inc(S["root_c"], 1)

            def normalise(i, par):
                act.wait_ge(S["tr_c"], i - 1 + CREDIT)
                act.wait_ge(S["xb_c"], i - 1 + CREDIT)
                for k in range(PIX):
                    at = bass.ds(i * PIX + k, 1)
                    ins = nc.scalar.activation(xp_s[:, par, k:k + 1, :], by_pixel(big)[:, at, :], ACT.Identity,
                                               bias=stats[:, 2, at], scale=stats[:, 1, at])
                ins.then_inc(S["xp_c"], 1)

            def transposed(i, par):
                act.wait_ge(S["tr_c"], i + 1 + CREDIT)
                act.wait_ge(S["k1_c"], i - 1 + CREDIT)
                nc.scalar.activation(xt_s[:, par].rearrange("p k c -> p (k c)"),
                                     ps[:, 2 * par:2 * par + 2, :].rearrange("p b n -> p (b n)")[:, 0:PIX * C],
                                     ACT.Copy).then_inc(S["xt_c"], 1)

            act.wait_ge(S["norm"], 1)
            normalise(0, 0)
            normalise(1, 1)
            with act.Fori(0, PIX_TURNS // 2 - 1) as i:
                for par in range(2):
                    transposed(i * 2 + par, par)
                    normalise(i * 2 + par + 2, par)
            transposed(PIX_TURNS - 3, 0)
            normalise(PIX_TURNS - 1, 0)
            transposed(PIX_TURNS - 2, 1)
            transposed(PIX_TURNS - 1, 0)
            for n, v in enumerate((se_ab[:, 0:1], sa_ab[:, :, 0:1])):
                act.wait_ge(S["var_c"], n + 2)
                nc.scalar.activation(v, v, ACT.Sqrt).then_inc(S["root_c"], 1)
            act.wait_ge(S["var_c"], 4)
            nc.scalar.activation(tapbn_s[:, 1, :], tapbn_s[:, 1, :], ACT.Sqrt).then_inc(S["root_c"], 1)
            act.wait_ge(S["tab_c"], 1)
            with act.Fori(0, C // CHUNK) as i:
                for n in range(0, 9, 2):
                    act.wait_ge(S["mb_p"], i * 9 + n + 1 + CREDIT)
                    if n == 0:
                        act.wait_ge(S["cv_p"], i * 8 + CREDIT)
                    flat = ps[0:HW + 1, 0:2, :].rearrange("p b n -> p (b n)")[:, 0:9 * 2 * CHUNK]
                    nc.scalar.activation(m_s[:, :, :, n * 9:(n + 1) * 9].rearrange("p c v m -> p m v c"),
                                         flat.rearrange("p (m v c) -> p m v c", m=9, v=2), ACT.Copy).then_inc(S["mb_e0"], 1)
                for k in range(CHUNK // QUAD):
                    q, par = i * (CHUNK // QUAD) + k, k % DEPTH
                    b0 = 6 if k % 2 == 0 else 2
                    act.wait_ge(S["cv_p"], q + 1 + CREDIT)
                    act.wait_ge(S[f"st_v{par}"], 32 * (i * (CHUNK // QUAD // DEPTH) + k // DEPTH) + CREDIT)
                    cv = ps[:, b0:b0 + 2, 0:4 * HW].rearrange("p k (c v n) -> p k c v n", c=2, v=2)
                    nc.scalar.activation(v_s[:, par].rearrange("p (k c) n -> p k c n", k=2), cv[:, :, :, 0, :],
                                         ACT.Copy).then_inc(S["v_c"], 1)
                    nc.scalar.activation(ks_s[:, par].rearrange("p (k c) n -> p k c n", k=2), cv[:, :, :, 1, :],
                                         ACT.Relu).then_inc(S["ks_c"], 1)
            act.wait_ge(S["phase_a"], 1)

            def residues(i):
                act.wait_ge(S["ar_c"], i + 1)
                act.wait_ge(S["raw_p"], 4 * i + CREDIT)
                nc.scalar.activation(arx_s.rearrange("p j (t n) -> p j t n", n=16),
                                     ar_s.unsqueeze(2).to_broadcast([128, G * 4, 8, 16]),
                                     ACT.Copy).then_inc(S["arx_c"], 1)

            def attentions(i, first=False):
                for par in range(2):
                    g = i * 2 + par
                    act.wait_ge(S["lg_p"], g - 1 + CREDIT)
                    for n in range(2):
                        act.wait_ge(S["se1_p"], g * 2 + n + 1)
                        nc.scalar.activation(a_s[0:HW, par, 2 * n:2 * n + 2, :].rearrange("p b j -> p (b j)"),
                                             ps[0:HW, n, :], ACT.Relu, bias=se_ab[:, 1:2],
                                             scale=se_ab[:, 0:1]).then_inc(S["a_c"], 1)
                    for h in range(HALVES):
                        act.wait_ge(S["sa1_p"], g * 2 + h + 1)
                        nc.scalar.activation(a2_s[:, h, :], ps[:, 2 + h, 0:TOK], ACT.Relu, bias=sa_ab[:, h, 1:2],
                                             scale=sa_ab[:, h, 0:1]).then_inc(S["a2_c"], 1)
                    if par == 0 and not first:
                        residues(i - 1)
                    if par == 1:
                        act.wait_ge(S["lgs_c"], i + 1)
                        nc.scalar.activation(lg_s, lg_s, ACT.Exp).then_inc(S["ex_c"], 1)
                    act.wait_ge(S["l2m_c"], g + 1)
                    act.wait_ge(S["t_c"], g - 1 + CREDIT)
                    for h in range(HALVES):
                        for b in range(G):
                            j = h * G + b
                            ins = nc.scalar.activation(e_s[:, par, h, b, :], ps[:, 2 + h, b * HW:(b + 1) * HW], ACT.Exp,
                                                       bias=sm_s[:, par, 2, j:j + 1], accum_out=sm_s[:, par, 3, j:j + 1])
                    ins.then_inc(S["e_c"], 1)

            attentions(0, first=True)
            with act.Fori(1, PAIRS) as i:
                attentions(i)
            residues(PAIRS - 1)
            act.wait_ge(S["x1_c"], GROUPS + CREDIT)

            def tokens(r, slot):
                if not isinstance(r, int) or r > 2:
                    act.wait_ge(S["rl_p"], r - 2 + CREDIT)
                nc.scalar.activation(xs_s[slot], x1_s[:, :, bass.ds(r * ROWS, ROWS)], ACT.Copy).then_inc(S["xs_c"], 1)

            def deviations(r, slot):
                v = bs_s[:, slot, :, 8:9]
                act.wait_ge(S["var2_c"], r + 1)
                nc.scalar.activation(v, v, ACT.Ln).then_inc(S["ln_c"], 1)
                act.wait_ge(S["ln_c"], r + 1)
                nc.scalar.activation(v, v, ACT.Exp, scale=-0.5).then_inc(S["rstd_c"], 1)

            def rows(r, i, slot):
                act.wait_ge(S["nmr_c"], r + 1)
                act.wait_ge(S[f"sent{slot}"], i + CREDIT)
                for s in range(SUBS):
                    ins = nc.scalar.activation(xf_s[:, slot, s, :], ps[:, 2 * slot + s // 2, (s % 2) * C:(s % 2 + 1) * C],
                                               ACT.Identity, bias=bs_s[:, slot, s, 9:10], scale=bs_s[:, slot, s, 8:9])
                ins.then_inc(S["xft_c"], 1)

            def high_piece(n, slot, come):
                act.wait_ge(S[f"wst_in{slot}"], 16 * come)
                nc.scalar.activation(w_s[:, 0, bass.ds(n * PIECE, PIECE)], stage_s[:, slot], ACT.Copy,
                                     scale=WSCALE).then_inc(S["whi_c"], 1)

            def act_turn(r, i, slot, ahead=2):
                if ahead > 1:
                    tokens(r + 2, (slot + 2) % 3)
                high_piece(r, slot, i + 1)
                act.wait_ge(S["probs_c"], r + 1)
                nc.scalar.activation(pr_s[:, :, 2, :], pr_s[:, :, 1, :], ACT.Exp).then_inc(S["ex2_c"], 1)
                if ahead:
                    deviations(r + 1, (slot + 1) % 3)
                    rows(r + 1, i + (slot + 1) // 3, (slot + 1) % 3)

            tokens(0, 0)
            tokens(1, 1)
            deviations(0, 0)
            rows(0, 0, 0)
            with act.Fori(0, TURNS // 3 - 1) as i:
                for k in range(3):
                    act_turn(i * 3 + k, i, k)
            for r in range(TURNS - 3, TURNS):
                act_turn(r, r // 3, r % 3, ahead=TURNS - 1 - r)
            for n in range(TURNS, PIECES):
                high_piece(n, n % 3, n // 3 + 1)
            act.wait_ge(S["tab_r"], 1)

            def high_rows(t, par, first=False):
                act.wait_ge(S["tt_p"], t + 1)
                if not first:
                    act.wait_ge(S["h_p"], 4 * (t - 1))
                nc.scalar.activation(xh_s[:, par, 0, :], ps[:, par, :], ACT.Copy).then_inc(S["xhi_c"], 1)

            def gelu(t, par, first=False):
                e = act.value_load(tabi_s[0:1, 1, bass.ds(t, 1)], min_val=0, max_val=EXPERTS - 1)
                if not first:
                    act.wait_ge(S["hlo_c"], t)
                for j in range(KB):
                    act.wait_ge(S["h_p"], 4 * t + j // 2 * 2 + 2)
                    nc.scalar.activation(hf_s[:, j * SLOTS:(j + 1) * SLOTS],
                                         ps[:, 2 + 2 * par + j // 2, (j % 2) * SLOTS:(j % 2 + 1) * SLOTS], ACT.Gelu,
                                         bias=b1_s[:, bass.ds(e * KB + j, 1)], scale=1.0 / WSCALE).then_inc(S["gel_c"], 1)

            high_rows(0, 0, first=True)
            high_rows(1, 1, first=True)
            gelu(0, 0, first=True)
            with act.Fori(0, TILES // 2 - 1) as i:
                for k in range(2):
                    t = i * 2 + 1 + k
                    high_rows(t + 1, k)
                    gelu(t, 1 - k)
            gelu(TILES - 1, 1)

        @block.gpsimd
        def _(pool):
            for n in CREDITED:
                pool.sem_inc(S[n], CREDIT)
            pool.wait_ge(S["w_in"], W_IN)

            def settle():
                pool.sem_inc(S["settle_g"], 1)

            pool.wait_ge(S["tab_c"], 1)
            with pool.Fori(0, QUADS // 2) as i:
                for par in range(2):
                    q = i * 2 + par
                    pool.wait_ge(S["tq_p"], q - 1 + CREDIT)
                    settle()
                    nc.gpsimd.tensor_copy(xq_s[:, par].rearrange("p c n -> p (c n)"),
                                          big[:, bass.ds(q * (QUAD * HW), QUAD * HW)]).then_inc(S["xq_c"], 1)
            pool.wait_ge(S["phase_a"], 1)
            with pool.Fori(0, PAIRS) as i:
                for par in range(2):
                    g = i * 2 + par
                    pool.wait_ge(S[f"rk_in{par}"], 64 * (i + 1))
                    settle()
                    nc.gpsimd.tensor_scalar(kr_s[:, par], kr_s[:, par], alpha_s[:, 0:1], None, ALU.mult).then_inc(S["ch_g"], 1)
                    pool.wait_ge(S["ch_g"], g + 1)
                    settle()
                    nc.gpsimd.tensor_tensor(kr_s[:, par], kr_s[:, par], xr_s[:, par], ALU.add).then_inc(S["r1_c"], 1)
                    pool.wait_ge(S["band_p"], g - 1 + CREDIT)
                    settle()
                    for h in range(HALVES):
                        nc.gpsimd.dma_start(vc_s[:, par, h], v_d[bass.ds(g * G, G), h * 128 * HW:(h + 1) * 128 * HW]
                                            .rearrange("b (c p) -> c b p", p=HW)).then_inc(S[f"v_in{par}"], 16)
            def scatter(r, i, slot, relay=True):
                pool.wait_ge(S["xft_c"], r + 1 + CREDIT)
                pool.wait_ge(S["idx_c"], r + 1)
                settle()
                for k in range(6):
                    nc.gpsimd.indirect_dma_start(
                        out=rows_d[:, :], out_offset=bass.IndirectOffsetOnAxis(ap=idx_s[:, slot, k:k + 1], axis=0),
                        in_=xf_s[:, slot, k % 3, :], in_offset=None).then_inc(S[f"scat{slot}"], 16)
                if relay:
                    before, come = (slot + 2) % 3, (i + 1 if slot else i)
                    pool.wait_ge(S[f"scat{before}"], 96 * come)
                    pool.sem_inc(S[f"sent{before}"], 1)

            for r in range(3):
                scatter(r, 0, r, relay=r > 0)
            with pool.Fori(1, TURNS // 3) as i:
                for k in range(3):
                    scatter(i * 3 + k, i, k)
            for par in range(2):
                pool.wait_ge(S[f"yst{par}"], 16 * (TILES // 2) + CREDIT)
            pool.wait_ge(S["w2_p"], TILES + CREDIT)

            def gather(r, par):
                pool.wait_ge(S["idx2_c"], r + 1)
                settle()
                for k in range(6):
                    nc.gpsimd.indirect_dma_start(
                        out=got_s[:, par, k, :], out_offset=None, in_=y_d[:, :],
                        in_offset=bass.IndirectOffsetOnAxis(ap=idx_s[:, par, k:k + 1], axis=0))\
                      .then_inc(S[f"gat{par}"], 16)

            with pool.Fori(0, TURNS // 2) as i:
                for par in range(2):
                    gather(i * 2 + par, par)
            gather(TURNS - 1, 0)


def _shape_constants(np):
    toep = np.zeros((11, HW, HW + 1), np.float32)
    for ky in range(3):
        for kx in range(3):
            for y in range(H):
                for xx in range(W):
                    yy, xi = y + ky - 1, xx + kx - 1
                    if 0 <= yy < H and 0 <= xi < W:
                        toep[ky * 3 + kx, y * W + xx, yy * W + xi] = 1.0
    toep[9, :, HW] = -1.0
    toep[10, :, HW] = 1.0
    toep3 = np.zeros((TAP_ROWS, HW, HW + 1), np.float32)
    for part in range(3):
        toep3[32 * part:32 * part + 11] = toep
    toep = (toep3.view(np.uint32) >> 16).astype(np.uint16)
    r = np.arange(128)
    band0 = (abs(np.arange(BAND0)[None] - r[:, None]) <= D // 2)
    band1 = (abs(np.arange(BAND1)[None] + BAND1_START - 128 - r[:, None]) <= D // 2)
    turn = (r - D // 2) % 16
    rot = np.concatenate([(turn % 4)[:, None] == np.arange(4), (turn // 4)[:, None] == np.arange(4)], 1)
    rows = np.ones((11, 2), np.float32)
    rows[:, 1] = 0.0
    rows[10] = (0.0, 1.0)
    before = (r[:, None] < r[None]).astype(np.float32)
    region = np.tile(np.arange(EXPERTS, dtype=np.float32) * REGION, (128, 1))
    tiles = np.arange(TILES, dtype=np.float32)[None]
    lower = np.tile(np.tril(np.ones((EXPERTS, EXPERTS)), -1).reshape(1, -1), (128, 1))
    f = np.float32
    return toep, np.concatenate([band0, band1], 1).astype(f), rot.astype(f), rows, lower.astype(f), before, region, tiles


def kernel(**inputs):
    import numpy as np
    import concourse.bacc as bacc
    from concourse import mybir as mb
    from concourse.bass_utils import run_bass_kernel_spmd

    i = {k.replace("L0_", ""): np.ascontiguousarray(v) for k, v in inputs.items()}
    toep, bands, rot, rows, lower, before, region, tiles = _shape_constants(np)
    f = np.float32
    taps = np.zeros((11, 2, C), f)
    taps[0:9, 0] = i["conv_se_val_w"].reshape(C, 9).T
    taps[10, 0] = i["conv_se_val_b"]
    taps[0:9, 1] = i["conv_sa_key_w"].reshape(C, 9).T
    taps[9, 1] = i["conv_sa_key_bn"][2]
    taps[10, 1] = i["conv_sa_key_bn"][1]
    tap_bn = np.ascontiguousarray(np.broadcast_to(i["conv_sa_key_bn"][[0, 3]], (11, 2, C)))
    z = np.zeros((HW, ZLEN), f)
    z[:, 127:136] = i["conv_se_key_w"][:, 0, ::-1]
    w1 = i["conv_sa_att_w1"].reshape(C, 8, 2)
    w2 = i["conv_sa_att_w2"].reshape(C // 8, 8)
    sa_w1 = np.zeros((128, HALVES, 2, 128), f)
    sa_w2 = np.zeros((128, HALVES, 128), f)
    for h in range(HALVES):
        for g in range(16):
            s = slice(g * 8, g * 8 + 8)
            for k in range(2):
                sa_w1[s, h, k, s] = w1[h * 128 + g * 8:h * 128 + g * 8 + 8, :, k].T
            sa_w2[s, h, s] = np.broadcast_to(w2[h * 16 + g][:, None], (8, 8))

    def halves(a):
        return np.ascontiguousarray(a.reshape(HALVES, 128, -1).transpose(1, 0, 2))

    se_w2 = np.concatenate([i["conv_se_att_w2"].T, i["conv_se_att_b2"][None]], 0)
    w1p = i["ffn_W1"].reshape(EXPERTS, 2, 128, HID)
    w2p = i["ffn_W2"].reshape(EXPERTS, 2, 2, 128, C).transpose(0, 1, 3, 2, 4).reshape(EXPERTS, 2, 128, 2 * C)
    arrays = {
        "x": i["x"].reshape(BS, C * HW), "taps": taps, "tap_bn": tap_bn, "tap_rows": rows, "toeplitz_mask": toep,
        "ident": np.eye(128, dtype=f), "band_masks": bands, "rot_masks": rot, "zstrings": z,
        "key_bias": np.broadcast_to(i["conv_se_key_b"], (128, HW)),
        "se_w1": i["conv_se_att_w1"].T.reshape(2, HW, HW).transpose(1, 0, 2), "se_bn": i["conv_se_att_bn"].T,
        "se_w2": se_w2, "sa_w1": sa_w1, "sa_bn": halves(i["conv_sa_att_bn"].T), "sa_w2": sa_w2,
        "sa_b2": np.repeat(i["conv_sa_att_b2"], 8).reshape(HALVES, 128).T,
        "alpha": np.broadcast_to(i["conv_alpha"], (128, 1)),
        "router": halves(i["ffn_Wr"].T), "router_bias": np.broadcast_to(i["ffn_br"], (128, EXPERTS)),
        "lower": lower, "before": before, "region_start": region, "turn": tiles,
        "ffn_w": np.concatenate([w1p, w2p], 1).reshape(PIECES, 128, PIECE),
        "ffn_b1": i["ffn_b1"].reshape(EXPERTS * KB, 128).T,
        "ffn_b2": i["ffn_b2"],
    }
    nc = bacc.Bacc("TRN2", target_bir_lowering=False, num_devices=1)
    feeds, args = {}, []
    for name, a in arrays.items():
        a = np.ascontiguousarray(a)
        feeds[f"in_{name}"] = a
        args.append(nc.dram_tensor(f"in_{name}", a.shape, mb.dt.from_np(a.dtype), kind="ExternalInput").ap())
    args.append(nc.dram_tensor("out_0", (BS, C * HW), mb.dt.float32, kind="ExternalOutput").ap())
    metaformer_kernel(nc, *args)
    r = run_bass_kernel_spmd(nc, [feeds], core_ids=[0])
    return r.results[0]["out_0"].reshape(BS, C, H, W)
```
